# Optimizing a Trainium2 kernel written in Bass

```python
import numpy as np
import jax
import jax.numpy as jnp

def _softmax(x, axis=-1):
    return jax.nn.softmax(x, axis=axis)

def _gelu(x):
    return jax.nn.gelu(x, approximate=True)

def _silu(x):
    return jax.nn.silu(x)

def _sigmoid(x):
    return jax.nn.sigmoid(x)

def _layernorm(x, axis=-1, eps=1e-05):
    m = jnp.mean(x, axis=axis, keepdims=True)
    v = jnp.var(x, axis=axis, keepdims=True)
    return (x - m) / jnp.sqrt(v + eps)

def _scatter_add(tgt, idx, src, axis=0):
    return tgt.at[idx].add(src)

def _segment_sum(src, seg, n):
    return jax.ops.segment_sum(src, seg, n)
kernel_name = 'mk_adaln_d1_jaxref_r4_f17831'

def setup_inputs(seed: int=0):
    np.random.seed(seed)
    _w = jnp.asarray

    def _L0_attn_setup():
        import jax, jax.numpy as jnp
        import numpy as np
        B, S, HIDDEN = (2, 512, 1024)
        TP = 2
        PART = HIDDEN // TP
        NUM_HEADS = 16 // TP
        HEAD_DIM = PART // NUM_HEADS
        MASKED_BIAS = -10000.0
        key = jax.random.key(seed)
        k_x, k_wq, k_bq, k_wo, k_bo = jax.random.split(key, 5)
        x = jax.random.normal(k_x, (B, S, HIDDEN), dtype=jnp.float32)
        w_qkv = jax.random.normal(k_wq, (3 * PART, HIDDEN), dtype=jnp.float32) * 0.02
        b_qkv = jax.random.normal(k_bq, (3 * PART,), dtype=jnp.float32) * 0.02
        w_o = jax.random.normal(k_wo, (HIDDEN, PART), dtype=jnp.float32) * 0.02
        b_o = jax.random.normal(k_bo, (HIDDEN,), dtype=jnp.float32) * 0.02
        return {'x': x, 'w_qkv': w_qkv, 'b_qkv': b_qkv, 'w_o': w_o, 'b_o': b_o}
    _L0_attn_in = _L0_attn_setup()

    def _L0_ffn_setup():
        import jax, jax.numpy as jnp
        import numpy as np
        D_MODEL = 1024
        D_FF = 2752
        key = jax.random.key(seed)
        k1, k2, k3, k4 = jax.random.split(key, 4)
        x = jax.random.normal(k1, (2, 512, D_MODEL), dtype=jnp.float32)
        W_gate = jax.random.normal(k2, (D_FF, D_MODEL), dtype=jnp.float32) * D_MODEL ** (-0.5)
        W_up = jax.random.normal(k3, (D_FF, D_MODEL), dtype=jnp.float32) * D_MODEL ** (-0.5)
        W_down = jax.random.normal(k4, (D_MODEL, D_FF), dtype=jnp.float32) * D_FF ** (-0.5)
        return {'x': x, 'W_gate': W_gate, 'W_up': W_up, 'W_down': W_down}
    _L0_ffn_in = _L0_ffn_setup()
    _L0_c = _w((lambda *s: np.random.randn(*s).astype(np.float32) * 0.05)(4, 1024))
    _L0_wmod = _w((lambda *s: np.random.randn(*s).astype(np.float32) * 0.05)(1024, 6 * 1024) * 1024 ** (-0.5))
    _d = {'L0_attn_x': _L0_attn_in['x'], 'L0_attn_w_qkv': _L0_attn_in['w_qkv'], 'L0_attn_b_qkv': _L0_attn_in['b_qkv'], 'L0_attn_w_o': _L0_attn_in['w_o'], 'L0_attn_b_o': _L0_attn_in['b_o'], 'L0_ffn_W_gate': _L0_ffn_in['W_gate'], 'L0_ffn_W_up': _L0_ffn_in['W_up'], 'L0_ffn_W_down': _L0_ffn_in['W_down'], 'L0_c': _L0_c, 'L0_wmod': _L0_wmod}
    _x0 = _d['L0_attn_x']
    _d['L0_attn_x'] = jax.random.normal(jax.random.fold_in(jax.random.key(seed), 1), (4, 512, 1024), dtype=_x0.dtype)
    del _x0
    return _d

def reference(L0_attn_x, L0_attn_w_qkv, L0_attn_b_qkv, L0_attn_w_o, L0_attn_b_o, L0_ffn_W_gate, L0_ffn_W_up, L0_ffn_W_down, L0_c, L0_wmod):

    def _L0_attn_ref(x, w_qkv, b_qkv, w_o, b_o):
        import jax, jax.numpy as jnp
        import numpy as np
        B, S, HIDDEN = (2, 512, 1024)
        TP = 2
        PART = HIDDEN // TP
        NUM_HEADS = 16 // TP
        HEAD_DIM = PART // NUM_HEADS
        MASKED_BIAS = -10000.0
        b, s, _ = x.shape
        qkv = x @ w_qkv.T + b_qkv
        q, k, v = jnp.split(qkv, 3, axis=-1)

        def to_heads(a):
            return a.reshape(b, s, NUM_HEADS, HEAD_DIM).transpose(0, 2, 1, 3)
        q, k, v = (to_heads(q), to_heads(k), to_heads(v))
        scores = jnp.einsum('bhfc,bhtc->bhft', k, q)
        causal = jnp.triu(jnp.ones((s, s), dtype=bool))
        scores = jnp.where(causal[None, None], scores, MASKED_BIAS)
        attn = jax.nn.softmax(scores, axis=-2)
        vals = jnp.einsum('bhft,bhfc->bhtc', attn, v)
        vals = vals.transpose(0, 2, 1, 3).reshape(b, s, PART)
        out = vals @ w_o.T + b_o
        return out

    def _L0_ffn_ref(x, W_gate, W_up, W_down):
        import jax, jax.numpy as jnp
        import numpy as np
        D_MODEL = 1024
        D_FF = 2752
        out_shape = x.shape[:-1] + (W_down.shape[0],)
        xf = x.reshape(-1, x.shape[-1])
        up = jnp.einsum('td,fd->tf', xf, W_up)
        gate = jax.nn.silu(jnp.einsum('td,fd->tf', xf, W_gate))
        h = gate * up
        y = jnp.einsum('tf,df->td', h, W_down)
        return y.reshape(out_shape)
    x = L0_attn_x
    mod = (_silu(L0_c) @ L0_wmod).reshape(L0_c.shape[0], 6, 1, -1)
    sa, ca, ga, sb, cb, gb = (mod[:, 0], mod[:, 1], mod[:, 2], mod[:, 3], mod[:, 4], mod[:, 5])
    ga = (2 * (ga >= 0) - 1) * jnp.maximum(jnp.abs(ga), 0.25)
    gb = (2 * (gb >= 0) - 1) * jnp.maximum(jnp.abs(gb), 0.25)
    h = _layernorm(x, axis=-1) * (1 + ca) + sa
    x = x + ga * _L0_attn_ref(h, L0_attn_w_qkv, L0_attn_b_qkv, L0_attn_w_o, L0_attn_b_o)
    h = _layernorm(x, axis=-1) * (1 + cb) + sb
    x = x + gb * _L0_ffn_ref(h, L0_ffn_W_gate, L0_ffn_W_up, L0_ffn_W_down)
    return x

_drawn_inputs = setup_inputs


def setup_inputs(seed=0):
    import zlib

    import numpy as np

    out = dict(_drawn_inputs(seed))
    spreads = {}
    factors = {'L0_attn_b_qkv': 8.0, 'L0_attn_b_o': 8.0}
    for name, (base, spread) in spreads.items():
        noise = np.random.default_rng([zlib.crc32(name.encode()), seed]).standard_normal(out[name].shape)
        drawn = base * np.exp(spread * noise) if base else spread * noise
        out[name] = jnp.asarray(drawn.astype(out[name].dtype))
    for name, factor in factors.items():
        out[name] = (out[name] * factor).astype(out[name].dtype)
    return out
```

```python
from contextlib import ExitStack

import concourse.bass as bass
from concourse import mybir

F32 = mybir.dt.float32
F32R = mybir.dt.float32r
I32 = mybir.dt.int32
U32 = mybir.dt.uint32
ALU = mybir.AluOpType
ACT = mybir.ActivationFunctionType
AX = mybir.AxisListType

P = 128
B, S, D = 4, 512, 1024
PART = 512
HEADS, HD = 8, 64
PAIRS = HEADS // 2
F = 2752
FT = -(-F // P)
DK = D // P
TT = S // P
NEG = -10000.0
EPS = 1e-5
W = 1024
RAW, SPLIT = 4, 2
MLP_RAW = 2
MOD_CHUNKS = 6 * D // 512
GATES = {4: (0, 0), 5: (0, 1), 10: (1, 0), 11: (1, 1)}

PRO = ([("mod", n) for n in range(4)] + [("t1", 0)] + [("q", 0), ("mod", 4), ("k", 0), ("mod", 5), ("v", 0), ("mod", 6)]
       + [("q", 1)] + [("mod", n) for n in range(7, MOD_CHUNKS)])
PRO_SLOTS = []
for kind, n in PRO:
    if kind == "mod":
        PRO_SLOTS += [("mod", 4 * n + q) for q in range(4)]
    elif kind != "t1":
        PRO_SLOTS.append((kind, n))
BODY_SLOTS = [("k", 1), ("v", 1), ("q", 2), ("k", 2), ("v", 2), ("q", 3), ("k", 3), ("v", 3),
              ("q", 0), ("k", 0), ("v", 0), ("o", 0), ("o", 1), ("o", 2), ("o", 3), ("q", 1)]
LAST_SLOTS = BODY_SLOTS[:8] + BODY_SLOTS[11:15]
FILLS = {0: [0], 1: [1, 2], 2: [3], 3: [4, 5], 4: [6], 5: [7], 7: [8], 8: [9], 9: [10]}
BASE_BODY = len(PRO_SLOTS)
BASE_LAST = BASE_BODY + (B - 1) * len(BODY_SLOTS)
BASE_MLP = BASE_LAST + len(LAST_SLOTS)
MLP_SLOTS = 3 * FT
assert BASE_BODY % 4 == 0 and BASE_MLP % 4 == 0 and MLP_SLOTS % MLP_RAW == 0

STRIP = {3: 0, 2: 512, 0: 896, 1: 1024}
STRIPS = 1280
TP_UNITS = [(0, 512), (512, 1024), (1024, 1280)]
TP_BANK = [3, 4, 3]


def step_uses(s, has_next):
    out = []
    if 2 <= s <= 9:
        out.append((5, ("pv", s - 2)))
    if 1 <= s <= 8:
        out += [(3, ("tp", s - 1, 0)), (4, ("tp", s - 1, 1))]
    for j in FILLS.get(s, []):
        if j < 8 or has_next:
            kind, p = BODY_SLOTS[j]
            out.append(({"q": 6, "k": 7, "v": 6}[kind], (kind, p)))
    if s == 6 and has_next:
        out += [(6 + kh, ("t1", tt, kh)) for tt in range(TT) for kh in range(2)]
    if 1 <= s <= 8:
        out.append((3, ("tp", s - 1, 2)))
    if s in (2, 4, 6):
        out.append((7, ("vt", s // 2)))
    if s in (3, 5, 7):
        out.append((5, ("vs", s // 2)))
    if s in (4, 6, 8):
        out.append((7, ("vals", s // 2 - 2)))
    return out


def stage_uses(has_next):
    out = [u for s in range(10) for u in step_uses(s, has_next)]
    out.append((7, ("vals", 3)))
    for j in range(4):
        out += [(3, ("o", j, 0)), (4, ("o", j, 1))]
        if has_next and j == 0:
            out.append((7, ("vt", 0)))
        if has_next and j == 1:
            out.append((5, ("vs", 0)))
    if has_next:
        out.append((6, ("q", 1)))
    out += [(3 + kh, ("t2", tt, kh)) for tt in range(TT) for kh in range(2)]
    return out


def prologue_uses():
    out = []
    for kind, n in PRO:
        if kind == "mod":
            out.append((3 + n % 2, ("mod", n)))
            if n in (1, 2, 3, 7, 8, 9, 10):
                out.append((5, ("mt", n - 1)))
            if n == 3:
                out.append((5, ("mt", 3)))
            if n == 6:
                out.append((7, ("vt", 0)))
            if n == 7:
                out.append((7, ("vs", 0)))
        elif kind == "t1":
            out += [(6 + kh, ("t1", tt, kh)) for tt in range(TT) for kh in range(2)]
        else:
            out.append(({"q": 6, "k": 7, "v": 6}[kind], (kind, n)))
    return out


def number(uses):
    seen, at = {}, {}
    for bank, label in uses:
        at[label] = (bank, seen.get(bank, 0))
        seen[bank] = seen.get(bank, 0) + 1
    return at, seen


PRO_AT, PRO_N = number(prologue_uses())
BODY_AT, BODY_N = number(stage_uses(True))
LAST_AT, LAST_N = number(stage_uses(False))


class Stage:

    def __init__(self, b, has_next):
        self.b, self.next = b, has_next
        self.at = BODY_AT if has_next else LAST_AT
        self.slots = BODY_SLOTS if has_next else LAST_SLOTS
        self.base = BASE_BODY + len(BODY_SLOTS) * b
        self.x_t1 = 4 + 8 * b
        self.x_t2 = self.x_t1 + (4 if has_next else 0)

    def use(self, *label):
        bank, n = self.at[label]
        return bank, PRO_N.get(bank, 0) + BODY_N.get(bank, 0) * self.b + n

    def pair(self, p, ahead=0):
        return PAIRS * self.b + PAIRS * ahead + p


class Prologue:
    b, next, x_t1 = 0, True, 0

    def use(self, *label):
        return PRO_AT[label]

    def pair(self, p, ahead=0):
        return p


def mlp_block(nc, x, c_t, w_mod, w_pairs, b_pairs, w_out, b_out, w_mlp, out):
    ctx = ExitStack()
    with ctx:
        attention_only = ExitStack()

        def sb(name, shape, dt=F32, where=ctx):
            return where.enter_context(nc.sbuf_tensor(name, shape, dt))

        def att(name, shape, dt=F32):
            return sb(name, shape, dt, attention_only)

        def sem(name):
            return ctx.enter_context(nc.semaphore(name))

        gate_rows = nc.dram_tensor("gate_rows", (2, B, D), F32, kind="Internal").ap()
        x1_dram = nc.dram_tensor("x1_dram", (B, P, TT, D), F32, kind="Internal").ap()
        h2_dram = nc.dram_tensor("h2_dram", (B, 2, P, DK, S), F32R, kind="Internal").ap()

        raw = sb("raw", [P, RAW, W])
        w_h = sb("w_h", [P, SPLIT, W], F32R)
        w_l = sb("w_l", [P, SPLIT, W], F32R)
        ht_h = sb("ht_h", [P, DK, S], F32R)
        ht_l = sb("ht_l", [P, DK, S], F32R)

        q_st = att("q_st", [P, 2, 2, S], F32R)
        k_h = att("k_h", [P, 2, 2, S], F32R)
        k_l = att("k_l", [P, 2, 2, S], F32R)
        v_h = att("v_h", [P, 2, TT, P], F32R)
        v_l = att("v_l", [P, 2, TT, P], F32R)
        v_col = att("v_col", [P, S])
        v_tail = att("v_tail", [P, 2, TT, P])
        probs = att("probs", [P, 2, STRIPS])
        pt_h = att("pt_h", [P, STRIPS], F32R)
        pt_l = att("pt_l", [P, STRIPS], F32R)
        vals = att("vals", [P, 2, TT, P])
        vt_h = att("vt_h", [P, PAIRS, S], F32R)
        vt_l = att("vt_l", [P, PAIRS, S], F32R)
        x_next = att("x_next", [P, TT, D])
        x_cur = att("x_cur", [P, TT, D])
        xn = att("xn", [P, 2, D])
        h_tmp = att("h_tmp", [P, 2, S])
        ga_row = att("ga_row", [P, D])
        bo_row = att("bo_row", [P, D])
        o_tmp = att("o_tmp", [P, 2, 256])
        mod_t = att("mod_t", [P, MOD_CHUNKS * 4, B])
        mod_a = att("mod_a", [P, 2 * DK])
        mod_b = att("mod_b", [P, 2 * DK])
        bias = att("bias", [P, 3 * PAIRS])
        c_sb = att("c_sb", [P, DK, B])
        c_act = att("c_act", [P, DK, B])
        ident = att("ident", [P, P])
        ones = att("ones", [P, P], F32R)
        masked = att("masked", [P, P])
        neg_fill = att("neg_fill", [P, P])
        neg_col = att("neg_col", [P, 1])
        n_tail = att("n_tail", [P, TT])
        neg_m = att("neg_m", [P, 4, TT])
        tail_e = att("tail_e", [P, 4, TT])
        sums = att("sums", [P, 4, TT])
        den = att("den", [P, 4, TT])
        r_den = att("r_den", [P, 4, TT])
        tail_w = att("tail_w", [P, TT, HD])
        pv_sum = att("pv_sum", [P, TT, HD])
        stats = att("stats", [P, TT, 2, 6])
        mv = att("mv", [P, TT, 2])
        ve = att("ve", [P, TT])
        rs = att("rs", [P, 2, TT])
        rt = att("rt", [P, TT])
        c_st = pt_h[:, 0:DK * P].rearrange("p (k m) -> p k m", k=DK)
        mod_lo = probs[0:B, 0, 0:1024].rearrange("p (n c) -> p n c", n=2)
        mod_row = probs[0:B, 1, 0:1024].rearrange("p (n c) -> p n c", n=2)
        gate_row = x_cur[0:B, 0, :].rearrange("p (n c) -> p n c", n=2)
        gate_row2 = x_cur[0:B, 1, :].rearrange("p (n c) -> p n c", n=2)
        gate_sgn = x_cur[0:B, 2, 0:512]
        gate_abs = x_cur[0:B, 2, 512:1024]

        attention_only.close()
        act = sb("act", [P, FT, S])
        a_h = sb("a_h", [P, 2, S], F32R)
        a_l = sb("a_l", [P, 2, S], F32R)
        silu = sb("silu", [P, 2, S])
        gb_row = sb("gb_row", [P, D])
        x1_sb = sb("x1_sb", [P, TT, D])
        y_sb = sb("y_sb", [P, 2, S])

        ps = ctx.enter_context(nc.psum_tensor("ps", [P, 8, 512], F32))
        scores = ps[:, 0:3, :].rearrange("p b c -> p (b c)")

        w_loaded = [sem(f"w_loaded{i}") for i in range(RAW)]
        w_loaded_mlp = [sem(f"w_loaded_mlp{i}") for i in range(MLP_RAW)]
        w_hi, w_lo, w_used = sem("w_hi"), sem("w_lo"), sem("w_used")
        small_loaded = sem("small_loaded")
        c_loaded = sem("c_loaded")
        c_silu, c_ready = sem("c_silu"), sem("c_ready")
        consts = sem("consts")
        pool_consts = sem("pool_consts")
        bank_full = {k: sem(f"bank_full{k}") for k in range(3, 8)}
        bank_free = {k: sem(f"bank_free{k}") for k in range(3, 8)}
        scores_full, scores_free = sem("scores_full"), sem("scores_free")
        mod_lo_ready, mod_row_ready, mod_picked = sem("mod_lo_ready"), sem("mod_row_ready"), sem("mod_picked")
        gate_ready, gate_stored = sem("gate_ready"), sem("gate_stored")
        x0_loaded, x_loaded, xc_loaded, ga_loaded = sem("x0_loaded"), sem("x_loaded"), sem("xc_loaded"), sem("ga_loaded")
        xn_ready, xn_used = sem("xn_ready"), sem("xn_used")
        t_tmp, t_hi, t_lo = sem("t_tmp"), sem("t_hi"), sem("t_lo")
        q_hi, k_hi, v_hi = sem("q_hi"), sem("k_hi"), sem("v_hi")
        q_ready, k_ready, v_ready = sem("q_ready"), sem("k_ready"), sem("v_ready")
        v_col_ready, tail_ready = sem("v_col_ready"), sem("tail_ready")
        negm_ready, exp_done = sem("negm_ready"), sem("exp_done")
        pt_hi, pt_ready = sem("pt_hi"), sem("pt_ready")
        vals_ready, vals_hi, valsT_ready = sem("vals_ready"), sem("vals_hi"), sem("valsT_ready")
        x1_ready, x1_stored = sem("x1_ready"), sem("x1_stored")
        h2_stored = [sem(f"h2_stored{i}") for i in range(4)]
        stage_clear = sem("stage_clear")
        ht_loaded, ht_free = sem("ht_loaded"), sem("ht_free")
        gate_full, up_full, silu_ready, act_ready = sem("gate_full"), sem("up_full"), sem("silu_ready"), sem("act_ready")
        a_hi, a_lo = sem("a_hi"), sem("a_lo")
        down_full, down_free = sem("down_full"), sem("down_free")
        mlp_loaded = sem("mlp_loaded")
        y_ready, y_added, out_stored = sem("y_ready"), sem("y_added"), sem("out_stored")
        att_done = sem("att_done")
        waited = {e: sem(f"waited_{e}") for e in ("pool", "dve", "pe")}

        def hold(engine, name):
            engine.sem_inc(waited[name], 1)

        block = ctx.enter_context(nc.Block())

        @block.sync
        def _(sp):
            def load(n, static_n, src):
                if not isinstance(n, int) or n >= RAW:
                    sp.wait_ge(w_lo, n - RAW + 1)
                sp.dma_start(raw[:, static_n % RAW, :], src).then_inc(w_loaded[static_n % RAW], 16)

            def source(kind, i):
                return {"mod": w_mod, "o": w_out}[kind][i] if kind in ("mod", "o") else w_pairs[3 * i + "qkv".index(kind)]

            sp.dma_start(c_sb[:], c_t).then_inc(c_loaded, 16)
            for n, (kind, i) in enumerate(PRO_SLOTS):
                load(n, n, source(kind, i))
                if n == 3:
                    sp.dma_start(x_next[:], x[0].rearrange("(t p) d -> p t d", p=P)).then_inc(x0_loaded, 16)
                    sp.dma_start(bias[:], b_pairs).then_inc(small_loaded, 16)
                    sp.dma_start(bo_row[:], b_out.partition_broadcast(P)).then_inc(small_loaded, 16)
            with sp.Fori(0, B - 1) as b:
                for j, (kind, i) in enumerate(BODY_SLOTS):
                    load(BASE_BODY + 16 * b + j, BASE_BODY + j, source(kind, i))
            for j, (kind, i) in enumerate(LAST_SLOTS):
                load(BASE_LAST + j, BASE_LAST + j, source(kind, i))

            with sp.Fori(0, B) as blk:
                with sp.Fori(0, MLP_SLOTS // 2) as i:
                    for r in range(2):
                        n = BASE_MLP + MLP_SLOTS * blk + 2 * i + r
                        sp.wait_ge(w_lo, n - 1)
                        sp.dma_start(raw[:, r, :], w_mlp[i * 2 + r]).then_inc(w_loaded_mlp[r], 16)

        @block.gpsimd
        def _(pool):
            pool.sem_inc(stage_clear, 1)
            nc.gpsimd.memset(ident[:], 0.0).then_inc(pool_consts, 1)
            nc.gpsimd.memset(masked[:], 0.0).then_inc(pool_consts, 1)
            pool.wait_ge(pool_consts, 2)
            nc.gpsimd.affine_select(out=ident[:], in_=ident[:], compare_op=ALU.not_equal, fill=1.0, base=0,
                                    pattern=[[-1, P]], channel_multiplier=1).then_inc(consts, 1)
            nc.gpsimd.affine_select(out=masked[:], in_=masked[:], compare_op=ALU.is_ge, fill=1.0, base=0,
                                    pattern=[[-1, P]], channel_multiplier=1).then_inc(consts, 1)

            def t_unit_lo(u_count, dst, tmp, hi):
                pool.wait_ge(t_hi, u_count + 1)
                nc.gpsimd.tensor_tensor(dst, tmp, hi.bitcast(F32), ALU.subtract).then_inc(t_lo, 1)

            def t1_units(x0):
                for tt in range(TT):
                    for kh in range(2):
                        sl = (slice(None), slice(4 * kh, 4 * kh + 4), slice(P * tt, P * tt + P))
                        tmp = h_tmp[:, kh, :].rearrange("p (k t) -> p k t", k=4)
                        t_unit_lo(2 * (x0 + tt) + kh, ht_l[sl], tmp, ht_h[sl])

            t1_units(0)
            for i, n in enumerate(sorted(GATES)):
                which, half = GATES[n]
                pool.wait_ge(gate_ready, i + 1)
                src = (gate_row if which == 0 else gate_row2)[:, half, :]
                pool.dma_start(gate_rows[which][:, 512 * half:512 * half + 512], src).then_inc(gate_stored, 16)
            pool.wait_ge(gate_stored, 64)

            def attention(st):
                b = st.b
                pool.wait_ge(xn_ready, 8 * b + 4)
                hold(pool, "pool")
                pool.dma_start(x_cur[:], x[b].rearrange("(t p) d -> p t d", p=P)).then_inc(xc_loaded, 16)
                pool.dma_start(ga_row[:], gate_rows[0][b].partition_broadcast(P)).then_inc(ga_loaded, 16)
                if st.next:
                    pool.dma_start(x_next[:], x[b + 1].rearrange("(t p) d -> p t d", p=P)).then_inc(x_loaded, 16)
                    t1_units(st.x_t1)
                pool.wait_ge(x1_ready, b + 1)
                hold(pool, "pool")
                pool.dma_start(x1_dram[b], x_cur[:]).then_inc(x1_stored, 16)
                for tt in range(TT):
                    for kh in range(2):
                        u = 2 * tt + kh
                        count = 2 * (st.x_t2 + tt) + kh
                        t_unit_lo(count, vt_l[:, u % 4, :], h_tmp[:, kh, :], vt_h[:, u % 4, :])
                        pool.wait_ge(t_lo, count + 1)
                        hold(pool, "pool")
                        for hl, stage in ((0, vt_h), (1, vt_l)):
                            pool.dma_start(h2_dram[b][hl][:, 4 * kh:4 * kh + 4, P * tt:P * tt + P],
                                           stage[:, u % 4, :].rearrange("p (k t) -> p k t", k=4)
                                           ).then_inc(h2_stored[u % 4], 16)
                for s in range(4):
                    pool.wait_ge(h2_stored[s], 64 * b + 64)
                pool.wait_ge(x1_stored, 16 * b + 16)
                hold(pool, "pool")
                nc.gpsimd.drain().then_inc(stage_clear, 1)

            with pool.Fori(0, B - 1) as b:
                attention(Stage(b, True))
            attention(Stage(B - 1, False))

            pool.wait_ge(att_done, 3)

            def mlp_loads(blk):
                pool.dma_start(x1_sb[:], x1_dram[blk]).then_inc(mlp_loaded, 16)
                pool.dma_start(gb_row[:], gate_rows[1][blk].partition_broadcast(P)).then_inc(mlp_loaded, 16)

            def weight_lo(n, r):
                pool.wait_ge(w_hi, n + 1)
                nc.gpsimd.tensor_tensor(w_l[:, r, :], raw[:, r, :], w_h[:, r, :].bitcast(F32),
                                        ALU.subtract).then_inc(w_lo, 1)

            with pool.Fori(0, B) as blk:
                n0 = BASE_MLP + MLP_SLOTS * blk
                mlp_loads(blk)
                pool.dma_start(ht_h[:], h2_dram[blk][0]).then_inc(ht_loaded, 16)
                pool.dma_start(ht_l[:], h2_dram[blk][1]).then_inc(ht_loaded, 16)
                with pool.Fori(0, MLP_SLOTS // 2) as i:
                    for r in range(2):
                        weight_lo(n0 + 2 * i + r, r)
                for u in range(2 * TT):
                    tt, dh = divmod(u, 2)
                    xs = x1_sb[:, tt, 512 * dh:512 * dh + 512]
                    if u == 0:
                        pool.wait_ge(mlp_loaded, 32 * blk + 32)
                    pool.wait_ge(y_ready, 8 * blk + u + 1)
                    nc.gpsimd.tensor_tensor(xs, xs, y_sb[:, u % 2, :], ALU.add).then_inc(y_added, 1)
                    pool.wait_ge(y_added, 8 * blk + u + 1)
                    hold(pool, "pool")
                    pool.dma_start(out[blk][P * tt:P * tt + P, 512 * dh:512 * dh + 512], xs).then_inc(out_stored, 16)
                pool.wait_ge(out_stored, 128 * blk + 128)

        @block.scalar
        def _(act_e):
            A = nc.scalar.activation

            def weight_hi(n, static_n):
                act_e.wait_ge(w_loaded[static_n % RAW], 16 * (n // RAW + 1) if isinstance(n, int)
                              else (16 * (static_n // RAW + 1) + (n - static_n) * (16 // RAW)))
                if not isinstance(n, int) or n >= SPLIT:
                    act_e.wait_ge(w_used, n - SPLIT + 1)
                A(w_h[:, static_n % SPLIT, :], raw[:, static_n % RAW, :], ACT.Copy).then_inc(w_hi, 1)

            def full(st, *label):
                bank, n = st.use(*label)
                act_e.wait_ge(bank_full[bank], n + 1)
                return bank

            def t_units(st, name, x0, mod, picked):
                act_e.wait_ge(mod_picked, picked)
                for tt in range(TT):
                    for kh in range(2):
                        bank = full(st, name, tt, kh)
                        count = 2 * (x0 + tt) + kh
                        if not isinstance(count, int) or count >= 2:
                            act_e.wait_ge(t_lo, count - 1)
                        for k in range(4):
                            last = A(h_tmp[:, kh, P * k:P * k + P], ps[:, bank, P * k:P * k + P], ACT.Identity,
                                     bias=mod[:, 4 * kh + k:4 * kh + k + 1],
                                     scale=mod[:, DK + 4 * kh + k:DK + 4 * kh + k + 1])
                            if k < 3:
                                continue
                            last.then_inc(t_tmp, 1)
                        act_e.wait_ge(t_tmp, count + 1)
                        act_e.sem_inc(bank_free[bank], 1)

            def q_evac(st, p):
                bank = full(st, "q", p)
                col = bias[:, 3 * p:3 * p + 1]
                A(q_st[0:64, p % 2, 0, :], ps[0:64, bank, :], ACT.Identity, bias=col[0:64])
                A(q_st[64:128, p % 2, 1, :], ps[64:128, bank, :], ACT.Identity, bias=col[64:128]).then_inc(q_hi, 1)

            def k_evac(st, p):
                bank = full(st, "k", p)
                col = bias[:, 3 * p + 1:3 * p + 2]
                for hd in range(2):
                    rows = slice(64 * hd, 64 * hd + 64)
                    for half in (0, 64):
                        last = A(k_h[half:half + 64, p % 2, hd, :], ps[rows, bank, :], ACT.Identity, bias=col[rows])
                last.then_inc(k_hi, 1)

            def v_evac(st, p):
                bank = full(st, "v", p)
                A(v_col[:], ps[:, bank, :], ACT.Identity, bias=bias[:, 3 * p + 2:3 * p + 3]).then_inc(v_col_ready, 1)

            def vt_evac(st, p):
                bank = full(st, "vt", p)
                A(v_h[:, p % 2].rearrange("p t c -> p (t c)"), ps[:, bank, :], ACT.Copy).then_inc(v_hi, 1)

            def vs_evac(st, p):
                bank = full(st, "vs", p)
                A(v_tail[:, p % 2, 0:3, :].rearrange("p t c -> p (t c)"), ps[:, bank, 0:384], ACT.Copy
                  ).then_inc(tail_ready, 1)

            def vals_evac(st, p):
                bank = full(st, "vals", p)
                A(vt_h[:, p, :], ps[:, bank, :], ACT.Copy).then_inc(vals_hi, 1)

            def tp_evac(st, h, u):
                bank = full(st, "tp", h, u)
                lo, hi = TP_UNITS[u]
                A(pt_h[:, lo:hi], ps[:, bank, 0:hi - lo], ACT.Copy).then_inc(pt_hi, 1)

            def softmax(st, h):
                g = 8 * st.b + h
                act_e.wait_ge(negm_ready, g + 1)
                par = h % 4
                for i in (3, 2, 0, 1):
                    o, n = STRIP[i], P * (i + 1)
                    last = A(probs[:, h % 2, o:o + n], scores[:, o:o + n], ACT.Exp, bias=neg_m[:, par, i:i + 1],
                             accum_out=sums[:, par, i:i + 1])
                last.then_inc(scores_free, 1)
                A(tail_e[:, par, :], neg_m[:, par, :], ACT.Exp, bias=neg_col[:]).then_inc(exp_done, 1)

            EVAC = {"q": q_evac, "k": k_evac, "v": v_evac}

            act_e.sem_inc(scores_free, 1)
            act_e.sem_inc(silu_ready, 2)
            act_e.wait_ge(c_loaded, 16)
            A(c_act[:], c_sb[:], ACT.Silu).then_inc(c_silu, 1)
            act_e.wait_ge(small_loaded, 32)
            pro = Prologue()

            def pro_evac(kind, n):
                if kind == "mod":
                    bank = full(pro, "mod", n)
                    if n >= 2:
                        act_e.wait_ge(mod_row_ready, n - 1)
                    A(mod_lo[:, n % 2, :], ps[32:32 + B, bank, :], ACT.Copy).then_inc(mod_lo_ready, 1)
                    if n == 6:
                        vt_evac(pro, 0)
                    if n == 7:
                        vs_evac(pro, 0)
                elif kind == "t1":
                    t_units(pro, "t1", 0, mod_a, 1)
                else:
                    EVAC[kind](pro, n)

            n = 0
            for idx, (kind, i) in enumerate(PRO):
                for _ in range({"mod": 4, "t1": 0}.get(kind, 1)):
                    weight_hi(n, n)
                    n += 1
                if idx:
                    pro_evac(*PRO[idx - 1])
            pro_evac(*PRO[-1])
            weight_hi(BASE_BODY, BASE_BODY)
            act_e.wait_ge(gate_stored, 64)
            act_e.wait_ge(mod_picked, 1)

            def next_slots(st, js):
                for j in js:
                    if j < len(st.slots):
                        weight_hi(st.base + j, BASE_BODY + j)

            def attention(st):
                for s in range(10):
                    if 1 <= s <= 8:
                        tp_evac(st, s - 1, 0)
                        tp_evac(st, s - 1, 1)
                    if s < 8:
                        softmax(st, s)
                    fills = [j for j in FILLS.get(s, []) if j < 8 or st.next]
                    ahead = [j for j in FILLS.get(s + 1, []) if j < 8 or st.next]
                    if s == 6:
                        ahead = [8]
                    if s == 9:
                        ahead = [11 if st.next else 8]
                    if s == 6 and not st.next:
                        ahead = []
                    for j in ahead:
                        weight_hi(st.base + j, BASE_BODY + j)
                    for j in fills:
                        kind, p = BODY_SLOTS[j]
                        EVAC[kind](st, p)
                    if s == 6 and st.next:
                        t_units(st, "t1", st.x_t1, mod_a, 2 * st.b + 2)
                    if 1 <= s <= 8:
                        tp_evac(st, s - 1, 2)
                    if s in (2, 4, 6):
                        vt_evac(st, s // 2)
                    if s in (3, 5, 7):
                        vs_evac(st, s // 2)
                    if s in (4, 6, 8):
                        if s == 4:
                            act_e.wait_ge(stage_clear, st.b + 1)
                        vals_evac(st, s // 2 - 2)
                vals_evac(st, 3)
                o0 = 11 if st.next else 8
                for j in range(4):
                    if st.next or j < 3:
                        weight_hi(st.base + o0 + j + 1, BASE_BODY + o0 + j + 1)
                    if j == 0 and st.next:
                        vt_evac(st, 0)
                    if j == 1 and st.next:
                        vs_evac(st, 0)
                if st.next:
                    q_evac(st, 1)
                    weight_hi(st.base + 16, BASE_BODY + 16)
                t_units(st, "t2", st.x_t2, mod_b, 2 * st.b + 3 if st.next else 2 * st.b + 2)

            with act_e.Fori(0, B - 1) as b:
                attention(Stage(b, True))
            attention(Stage(B - 1, False))
            act_e.sem_inc(att_done, 1)

            act_e.wait_ge(att_done, 3)

            def mlp_hi(n, r, blk, i):
                act_e.wait_ge(w_loaded_mlp[r], 16 * (MLP_SLOTS // 2 * blk + i + 1))
                act_e.wait_ge(w_used, n - SPLIT + 1)
                A(w_h[:, r, :], raw[:, r, :], ACT.Copy).then_inc(w_hi, 1)

            with act_e.Fori(0, B) as blk:
                n0 = BASE_MLP + MLP_SLOTS * blk
                with act_e.Fori(0, FT // 2) as i:
                    for s in range(2):
                        for r in range(2):
                            mlp_hi(n0 + 4 * i + 2 * s + r, r, blk, 2 * i + s)
                        act_e.wait_ge(gate_full, FT * blk + 2 * i + s + 1)
                        act_e.wait_ge(act_ready, FT * blk + 2 * i + s + 1)
                        A(silu[:, s, :], ps[:, 2 * s, :], ACT.Silu).then_inc(silu_ready, 1)
                with act_e.Fori(0, FT // 2) as i:
                    for r in range(2):
                        mlp_hi(n0 + 2 * FT + 2 * i + r, r, blk, FT + i)
                        act_e.wait_ge(act_ready, FT * blk + 2 * i + r + 3)
                        A(a_h[:, r, :], act[:, bass.ds(2 * i + r, 1), :].rearrange("p a t -> p (a t)"), ACT.Copy
                          ).then_inc(a_hi, 1)

        @block.vector
        def _(dve):
            V = nc.vector

            def weight_lo(n, static_n):
                dve.wait_ge(w_hi, n + 1)
                V.tensor_tensor(w_l[:, static_n % SPLIT, :], raw[:, static_n % RAW, :],
                                w_h[:, static_n % SPLIT, :].bitcast(F32), ALU.subtract).then_inc(w_lo, 1)

            def q_lo(st, p, ahead=0):
                bank, _ = st.use("q", p)
                dve.wait_ge(q_hi, st.pair(p, ahead) + 1)
                for hd in range(2):
                    rows, other = slice(64 * hd, 64 * hd + 64), slice(64 - 64 * hd, 128 - 64 * hd)
                    last = V.scalar_tensor_tensor(out=q_st[other, p % 2, hd, :], in0=ps[rows, bank, :],
                                                  scalar=bias[rows, 3 * p:3 * p + 1],
                                                  in1=q_st[rows, p % 2, hd, :].bitcast(F32),
                                                  op0=ALU.add, op1=ALU.subtract)
                last.then_inc(q_ready, 1)
                dve.wait_ge(q_ready, st.pair(p, ahead) + 1)
                dve.sem_inc(bank_free[bank], 1)

            def k_lo(st, p, ahead=0):
                bank, _ = st.use("k", p)
                dve.wait_ge(k_hi, st.pair(p, ahead) + 1)
                for hd in range(2):
                    rows = slice(64 * hd, 64 * hd + 64)
                    for half in (0, 64):
                        last = V.scalar_tensor_tensor(out=k_l[half:half + 64, p % 2, hd, :], in0=ps[rows, bank, :],
                                                      scalar=bias[rows, 3 * p + 1:3 * p + 2],
                                                      in1=k_h[rows, p % 2, hd, :].bitcast(F32),
                                                      op0=ALU.add, op1=ALU.subtract)
                last.then_inc(k_ready, 1)
                dve.wait_ge(k_ready, st.pair(p, ahead) + 1)
                dve.sem_inc(bank_free[bank], 1)

            def v_lo(st, p, ahead=0):
                bank, _ = st.use("v", p)
                dve.wait_ge(v_col_ready, st.pair(p, ahead) + 1)
                dve.sem_inc(bank_free[bank], 1)

            def vt_lo(st, p, ahead=0):
                bank, _ = st.use("vt", p)
                dve.wait_ge(v_hi, st.pair(p, ahead) + 1)
                V.tensor_tensor(v_l[:, p % 2].rearrange("p t c -> p (t c)"), ps[:, bank, :],
                                v_h[:, p % 2].rearrange("p t c -> p (t c)").bitcast(F32), ALU.subtract).then_inc(v_ready, 1)
                dve.wait_ge(v_ready, st.pair(p, ahead) + 1)
                dve.sem_inc(bank_free[bank], 1)

            def vs_free(st, p, ahead=0):
                bank, _ = st.use("vs", p)
                dve.wait_ge(tail_ready, st.pair(p, ahead) + 1)
                dve.sem_inc(bank_free[bank], 1)

            def vals_lo(st, p):
                bank, _ = st.use("vals", p)
                dve.wait_ge(vals_hi, st.pair(p) + 1)
                V.tensor_tensor(vt_l[:, p, :], ps[:, bank, :], vt_h[:, p, :].bitcast(F32), ALU.subtract
                                ).then_inc(valsT_ready, 1)
                dve.wait_ge(valsT_ready, st.pair(p) + 1)
                dve.sem_inc(bank_free[bank], 1)

            def tp_lo(st, h, u):
                bank, _ = st.use("tp", h, u)
                lo, hi = TP_UNITS[u]
                count = 3 * (8 * st.b + h) + u
                dve.wait_ge(pt_hi, count + 1)
                V.tensor_tensor(pt_l[:, lo:hi], ps[:, bank, 0:hi - lo], pt_h[:, lo:hi].bitcast(F32), ALU.subtract
                                ).then_inc(pt_ready, 1)
                dve.wait_ge(pt_ready, count + 1)
                dve.sem_inc(bank_free[bank], 1)

            def row_max(st, h):
                par, g = h % 4, 8 * st.b + h
                dve.wait_ge(scores_full, g + 1)
                hold(dve, "dve")
                for i in range(TT):
                    o = STRIP[i] + P * i
                    V.copy_predicated(scores[:, o:o + P], masked[:].bitcast(U32), neg_fill[:])
                V.drain()
                for i in range(TT):
                    o, n = STRIP[i], P * (i + 1)
                    V.tensor_reduce(neg_m[:, par, i:i + 1], scores[:, o:o + n], AX.X, ALU.max, negate=True)
                V.drain()
                V.tensor_scalar(neg_m[:, par, 0:3], neg_m[:, par, 0:3], -NEG, None, ALU.min).then_inc(negm_ready, 1)

            def denominators(st, h):
                par, g = h % 4, 8 * st.b + h
                dve.wait_ge(exp_done, g + 1)
                V.tensor_tensor(den[:, par, :], tail_e[:, par, :], n_tail[:], ALU.mult)
                V.drain()
                V.tensor_tensor(den[:, par, :], den[:, par, :], sums[:, par, :], ALU.add)
                V.drain()
                V.reciprocal(r_den[:, par, :], den[:, par, :])

            def pv_evac(st, h):
                par, g = h % 4, 8 * st.b + h
                p, hd = divmod(h, 2)
                bank, n = st.use("pv", h)
                cols = slice(HD * hd, HD * hd + HD)
                dve.wait_ge(tail_ready, st.pair(p) + 1)
                V.tensor_tensor(tail_w[:], v_tail[:, p % 2, :, cols],
                                tail_e[:, par, :].unsqueeze(2).to_broadcast([P, TT, HD]), ALU.mult)
                V.drain()
                dve.wait_ge(bank_full[bank], n + 1)
                V.tensor_tensor(pv_sum[:], ps[:, bank, 0:TT * HD].rearrange("p (t c) -> p t c", t=TT), tail_w[:], ALU.add)
                V.drain()
                V.tensor_tensor(vals[:, p % 2, :, cols], pv_sum[:],
                                r_den[:, par, :].unsqueeze(2).to_broadcast([P, TT, HD]), ALU.mult).then_inc(vals_ready, 1)
                dve.sem_inc(bank_free[bank], 1)

            def layer_stats(xt):
                for tt in range(TT):
                    for half in range(2):
                        V.bn_stats(stats[:, tt, half, :], xt[:, tt, 512 * half:512 * half + 512])
                V.drain()
                for tt in range(TT):
                    V.bn_aggr(mv[:, tt, :], stats[:, tt, :, :])
                V.drain()
                V.tensor_scalar(ve[:], mv[:, :, 1], EPS, None, ALU.add)
                V.drain()
                V.tensor_scalar(rs[:, 0, :].bitcast(I32), ve[:].bitcast(I32), -0.5, 1597463007.0, ALU.mult, ALU.add)
                V.drain()
                for it in range(3):
                    y, y2 = rs[:, it % 2, :], rs[:, (it + 1) % 2, :]
                    V.tensor_tensor(rt[:], y, y, ALU.mult)
                    V.drain()
                    V.scalar_tensor_tensor(out=rt[:], in0=rt[:], scalar=-0.5, in1=ve[:], op0=ALU.mult, op1=ALU.mult)
                    V.drain()
                    V.scalar_tensor_tensor(out=y2, in0=rt[:], scalar=1.5, in1=y, op0=ALU.add, op1=ALU.mult)
                    V.drain()

            def normalise(xt, tt, count):
                if not isinstance(count, int) or count >= 2:
                    dve.wait_ge(xn_used, count - 1)
                V.tensor_scalar(xn[:, tt % 2, :], xt[:, tt, :], mv[:, tt, 0:1], rs[:, 1, tt:tt + 1],
                                ALU.subtract, ALU.mult).then_inc(xn_ready, 1)

            def pick(dst, first, b):
                src = mod_t[:, first:first + 2 * DK, b:b + 1] if isinstance(b, int) else \
                    mod_t[:, first:first + 2 * DK, bass.ds(b, 1)]
                V.tensor_copy(dst[:].unsqueeze(2), src).then_inc(mod_picked, 1)

            def t_units(xt, x0, staged, b):
                for tt in range(TT):
                    if tt >= 2:
                        normalise(xt, tt, x0 + tt)
                    for kh in range(2):
                        u, count = 2 * tt + kh, 2 * (x0 + tt) + kh
                        dve.wait_ge(t_tmp, count + 1)
                        if staged:
                            if u >= 4:
                                dve.wait_ge(h2_stored[u % 4], 64 * b + 32)
                            dst, src = vt_h[:, u % 4, :], h_tmp[:, kh, :]
                        else:
                            dst = ht_h[:, 4 * kh:4 * kh + 4, P * tt:P * tt + P]
                            src = h_tmp[:, kh, :].rearrange("p (k t) -> p k t", k=4)
                        V.tensor_copy(dst, src).then_inc(t_hi, 1)

            LO = {"q": q_lo, "k": k_lo, "v": v_lo}

            dve.sem_inc(act_ready, 2)
            V.memset(ones[:].bitcast(F32), 1.0)
            V.memset(neg_fill[:], NEG)
            V.memset(neg_col[:], NEG)
            V.memset(v_tail[:, :, 3, :], 0.0)
            for i in range(TT):
                V.memset(n_tail[:, i:i + 1], float(P * (TT - 1 - i)))
            V.memset(c_st.bitcast(F32), 0.0)
            V.drain().then_inc(consts, 1)
            dve.wait_ge(c_silu, 1)
            V.tensor_copy(c_st[:, :, 0:B], c_act[:])
            V.drain()
            V.tensor_tensor(c_st[:, :, 32:32 + B], c_act[:], c_st[:, :, 0:B].bitcast(F32), ALU.subtract).then_inc(c_ready, 1)
            dve.wait_ge(small_loaded, 32)
            pro = Prologue()

            def mod_row_evac(n):
                bank, _ = pro.use("mod", n)
                dve.wait_ge(mod_lo_ready, n + 1)
                V.tensor_tensor(mod_row[:, n % 2, :], ps[0:B, bank, :], mod_lo[:, n % 2, :], ALU.add).then_inc(mod_row_ready, 1)
                dve.wait_ge(mod_row_ready, n + 1)
                dve.sem_inc(bank_free[bank], 1)
                if n in GATES:
                    which, half = GATES[n]
                    row = mod_row[:, n % 2, :]
                    V.tensor_scalar(gate_sgn, row, 0.0, 2.0, ALU.is_ge, ALU.mult)
                    V.tensor_scalar(gate_abs, row, -1.0, None, ALU.mult)
                    V.drain()
                    V.tensor_tensor(gate_abs, gate_abs, row, ALU.max)
                    V.drain()
                    V.tensor_scalar(gate_abs, gate_abs, 0.25, None, ALU.max)
                    V.drain()
                    V.scalar_tensor_tensor(out=(gate_row if which == 0 else gate_row2)[:, half, :], in0=gate_sgn,
                                           scalar=-1.0, in1=gate_abs, op0=ALU.add, op1=ALU.mult).then_inc(gate_ready, 1)
                    V.drain()

            def mod_t_evac(n):
                bank, used = pro.use("mt", n)
                dve.wait_ge(bank_full[bank], used + 1)
                V.tensor_scalar(mod_t[:, 4 * n:4 * n + 4, :], ps[:, bank, 0:4 * B].rearrange("p (t b) -> p t b", t=4),
                                1.0 if n // 2 in (1, 4) else 0.0, None, ALU.add)
                V.drain().then_inc(bank_free[bank], 1)

            def pro_evac(kind, n):
                if kind == "mod":
                    mod_row_evac(n)
                    if n in (1, 2, 3, 7, 8, 9, 10):
                        mod_t_evac(n - 1)
                    if n == 3:
                        mod_t_evac(3)
                        pick(mod_a, 0, 0)
                    if n == 6:
                        vt_lo(pro, 0)
                    if n == 7:
                        vs_free(pro, 0)
                elif kind == "t1":
                    dve.wait_ge(x0_loaded, 16)
                    layer_stats(x_next)
                    normalise(x_next, 0, 0)
                    normalise(x_next, 1, 1)
                    t_units(x_next, 0, False, 0)
                else:
                    LO[kind](pro, n)

            n = 0
            for idx, (kind, i) in enumerate(PRO):
                for _ in range({"mod": 4, "t1": 0}.get(kind, 1)):
                    weight_lo(n, n)
                    n += 1
                if idx:
                    pro_evac(*PRO[idx - 1])
            pro_evac(*PRO[-1])
            weight_lo(BASE_BODY, BASE_BODY)

            def attention(st):
                b = st.b
                for s in range(10):
                    if s < 8:
                        row_max(st, s)
                    if 2 <= s <= 9:
                        pv_evac(st, s - 2)
                    if 1 <= s <= 8:
                        tp_lo(st, s - 1, 0)
                        tp_lo(st, s - 1, 1)
                    fills = [j for j in FILLS.get(s, []) if j < 8 or st.next]
                    ahead = [j for j in FILLS.get(s + 1, []) if j < 8 or st.next]
                    if s == 6:
                        ahead = [8] if st.next else []
                    if s == 9:
                        ahead = [11 if st.next else 8]
                    for j in ahead:
                        weight_lo(st.base + j, BASE_BODY + j)
                    for j in fills:
                        kind, p = BODY_SLOTS[j]
                        LO[kind](st, p, 1 if j >= 8 else 0)
                    if s == 5 and st.next:
                        dve.wait_ge(x_loaded, 16 * b + 16)
                        layer_stats(x_next)
                        normalise(x_next, 0, st.x_t1)
                        normalise(x_next, 1, st.x_t1 + 1)
                        pick(mod_a, 0, b + 1)
                    if s == 6 and st.next:
                        t_units(x_next, st.x_t1, False, b)
                    if 1 <= s <= 8:
                        tp_lo(st, s - 1, 2)
                    if s in (2, 4, 6):
                        vt_lo(st, s // 2)
                    if s in (3, 5, 7):
                        vs_free(st, s // 2)
                    if s in (4, 6, 8):
                        vals_lo(st, s // 2 - 2)
                    if s < 8:
                        denominators(st, s)
                vals_lo(st, 3)
                o0 = 11 if st.next else 8
                dve.wait_ge(xc_loaded, 16 * b + 16)
                dve.wait_ge(ga_loaded, 16 * b + 16)
                for j in range(4):
                    if st.next or j < 3:
                        weight_lo(st.base + o0 + j + 1, BASE_BODY + o0 + j + 1)
                    cols = slice(256 * j, 256 * j + 256)
                    for half in range(2):
                        bank, used = st.use("o", j, half)
                        dve.wait_ge(bank_full[bank], used + 1)
                        for t in range(2):
                            V.tensor_tensor(o_tmp[:, t, :], ps[:, bank, 256 * t:256 * t + 256], bo_row[:, cols], ALU.add)
                        V.drain().then_inc(bank_free[bank], 1)
                        for t in range(2):
                            V.tensor_tensor(o_tmp[:, t, :], o_tmp[:, t, :], ga_row[:, cols], ALU.mult)
                        V.drain()
                        V.tensor_tensor(x_cur[:, 2 * half:2 * half + 2, cols], x_cur[:, 2 * half:2 * half + 2, cols],
                                        o_tmp[:], ALU.add)
                        V.drain()
                    if j == 0 and st.next:
                        vt_lo(st, 0, 1)
                    if j == 1 and st.next:
                        vs_free(st, 0, 1)
                V.drain().then_inc(x1_ready, 1)
                layer_stats(x_cur)
                normalise(x_cur, 0, st.x_t2)
                normalise(x_cur, 1, st.x_t2 + 1)
                pick(mod_b, 6 * DK // 2, b)
                if st.next:
                    q_lo(st, 1, 1)
                    weight_lo(st.base + 16, BASE_BODY + 16)
                t_units(x_cur, st.x_t2, True, b)

            with dve.Fori(0, B - 1) as b:
                attention(Stage(b, True))
            attention(Stage(B - 1, False))
            V.drain().then_inc(att_done, 1)

            dve.wait_ge(att_done, 3)
            with dve.Fori(0, B) as blk:
                with dve.Fori(0, FT // 2) as i:
                    for s in range(2):
                        tile = FT * blk + 2 * i + s
                        dve.wait_ge(silu_ready, tile + 3)
                        dve.wait_ge(up_full, tile + 1)
                        V.tensor_tensor(act[:, bass.ds(2 * i + s, 1), :].rearrange("p a t -> p (a t)"),
                                        ps[:, 2 * s + 1, :], silu[:, s, :], ALU.mult).then_inc(act_ready, 1)
                with dve.Fori(0, FT // 2) as i:
                    for r in range(2):
                        k = FT * blk + 2 * i + r
                        dve.wait_ge(a_hi, k + 1)
                        V.tensor_tensor(a_l[:, r, :], act[:, bass.ds(2 * i + r, 1), :].rearrange("p a t -> p (a t)"),
                                        a_h[:, r, :].bitcast(F32), ALU.subtract).then_inc(a_lo, 1)
                dve.wait_ge(mlp_loaded, 32 * blk + 32)
                for u in range(2 * TT):
                    tt, dh = divmod(u, 2)
                    dve.wait_ge(down_full, 8 * blk + u + 1)
                    if u >= 2:
                        dve.wait_ge(y_added, 8 * blk + u - 1)
                    V.tensor_tensor(y_sb[:, u % 2, :], ps[:, u, :], gb_row[:, 512 * dh:512 * dh + 512], ALU.mult
                                    ).then_inc(y_ready, 1)
                    dve.wait_ge(y_ready, 8 * blk + u + 1)
                    dve.sem_inc(down_free, 1)

        @block.tensor
        def _(pe):
            mm = nc.tensor.matmul

            def claim(st, *label):
                bank, n = st.use(*label)
                if not isinstance(n, int) or n > 0:
                    pe.wait_ge(bank_free[bank], n)
                return bank

            def three(out, a_h_, a_l_, b_h_, b_l_, first, last):
                mm(out, a_h_, b_h_, start=first, stop=False)
                mm(out, a_h_, b_l_, start=False, stop=False)
                return mm(out, a_l_, b_h_, start=False, stop=last)

            def slot(n, static_n):
                pe.wait_ge(w_lo, n + 1)
                r = static_n % SPLIT
                return w_h[:, r, :], w_l[:, r, :]

            def project(st, kind, p, n, static_n):
                bank = claim(st, kind, p)
                wh, wl = slot(n, static_n)
                for k in range(DK):
                    c = slice(P * k, P * k + P)
                    last = three(ps[:, bank, :], wh[:, c], wl[:, c], ht_h[:, k, :], ht_l[:, k, :], k == 0, k == DK - 1)
                last.then_inc(bank_full[bank], 1)
                pe.wait_ge(bank_full[bank], st.use(kind, p)[1] + 1)
                pe.sem_inc(w_used, 1)

            def modulation(n, n0):
                bank = claim(pro, "mod", n)
                for q in range(4):
                    wh, wl = slot(n0 + q, n0 + q)
                    for kk in range(2):
                        k = 2 * q + kk
                        c = slice(512 * kk, 512 * kk + 512)
                        mm(ps[:, bank, :], c_st[:, k, :], wh[:, c], start=(k == 0), stop=False)
                        last = mm(ps[:, bank, :], c_st[:, k, :], wl[:, c], start=False, stop=(k == DK - 1))
                    last.then_inc(w_used, 1)
                pe.wait_ge(w_used, n0 + 4)
                pe.sem_inc(bank_full[bank], 1)

            def mod_transpose(n):
                bank = claim(pro, "mt", n)
                pe.wait_ge(mod_row_ready, n + 1)
                for t in range(4):
                    last = nc.tensor.transpose(ps[:, bank, B * t:B * t + B], mod_row[:, n % 2, P * t:P * t + P],
                                               ident[0:B, 0:B])
                last.then_inc(bank_full[bank], 1)

            def t_units(st, name, x0):
                for tt in range(TT):
                    pe.wait_ge(xn_ready, x0 + tt + 1)
                    for kh in range(2):
                        bank = claim(st, name, tt, kh)
                        for k in range(4):
                            c = P * (4 * kh + k)
                            last = nc.tensor.transpose(ps[:, bank, P * k:P * k + P], xn[:, tt % 2, c:c + P], ident[:])
                        last.then_inc(bank_full[bank], 1)
                    pe.wait_ge(bank_full[bank], st.use(name, tt, 1)[1] + 1)
                    pe.sem_inc(xn_used, 1)

            def v_transpose(st, p, ahead=0):
                bank = claim(st, "vt", p)
                pe.wait_ge(v_col_ready, st.pair(p, ahead) + 1)
                for t in range(TT):
                    last = nc.tensor.transpose(ps[:, bank, P * t:P * t + P], v_col[:, P * t:P * t + P], ident[:])
                last.then_inc(bank_full[bank], 1)

            def v_tails(st, p, ahead=0):
                bank = claim(st, "vs", p)
                pe.wait_ge(v_ready, st.pair(p, ahead) + 1)
                for i in range(3):
                    for j in range(i + 1, TT):
                        for part in (v_h, v_l):
                            last = mm(ps[:, bank, P * i:P * i + P], ones[:], part[:, p % 2, j, :],
                                      start=(j == i + 1 and part is v_h), stop=(j == TT - 1 and part is v_l))
                last.then_inc(bank_full[bank], 1)

            def head_scores(st, h):
                p, hd = divmod(h, 2)
                g = 8 * st.b + h
                pe.wait_ge(q_ready, st.pair(p) + 1)
                pe.wait_ge(k_ready, st.pair(p) + 1)
                if not isinstance(g, int) or g > 0:
                    pe.wait_ge(scores_free, g + 1)
                for i in (3, 2, 0, 1):
                    o, n = STRIP[i], P * (i + 1)
                    mm(scores[:, o:o + n], q_st[:, p % 2, hd, P * i:P * i + P], k_h[:, p % 2, hd, 0:n], start=True, stop=False)
                    last = mm(scores[:, o:o + n], q_st[:, p % 2, hd, P * i:P * i + P], k_l[:, p % 2, hd, 0:n],
                              start=False, stop=True)
                last.then_inc(scores_full, 1)

            def prob_transpose(st, h, u):
                bank = claim(st, "tp", h, u)
                pe.wait_ge(exp_done, 8 * st.b + h + 1)
                lo, hi = TP_UNITS[u]
                for o in range(lo, hi, P):
                    last = nc.tensor.transpose(ps[:, bank, o - lo:o - lo + P], probs[:, h % 2, o:o + P], ident[:])
                last.then_inc(bank_full[bank], 1)

            def head_values(st, h):
                p, hd = divmod(h, 2)
                bank = claim(st, "pv", h)
                pe.wait_ge(pt_ready, 3 * (8 * st.b + h) + 3)
                pe.wait_ge(v_ready, st.pair(p) + 1)
                c = slice(HD * hd, HD * hd + HD)
                for i in range(TT):
                    for j in range(i + 1):
                        o = STRIP[i] + P * j
                        last = three(ps[:, bank, HD * i:HD * i + HD], pt_h[:, o:o + P], pt_l[:, o:o + P],
                                     v_h[:, p % 2, j, c], v_l[:, p % 2, j, c], j == 0, j == i)
                last.then_inc(bank_full[bank], 1)

            def vals_transpose(st, p):
                bank = claim(st, "vals", p)
                pe.wait_ge(vals_ready, 8 * st.b + 2 * p + 2)
                for t in range(TT):
                    last = nc.tensor.transpose(ps[:, bank, P * t:P * t + P], vals[:, p % 2, t, :], ident[:])
                last.then_inc(bank_full[bank], 1)

            def out_projection(st, j, n, static_n):
                wh, wl = slot(n, static_n)
                if j == 0:
                    pe.wait_ge(valsT_ready, st.pair(3) + 1)
                for half in range(2):
                    bank = claim(st, "o", j, half)
                    for t in range(2):
                        tt = 2 * half + t
                        for p in range(PAIRS):
                            c = slice(256 * p, 256 * p + 256)
                            last = three(ps[:, bank, 256 * t:256 * t + 256], vt_h[:, p, P * tt:P * tt + P],
                                         vt_l[:, p, P * tt:P * tt + P], wh[:, c], wl[:, c], p == 0, p == PAIRS - 1)
                    last.then_inc(bank_full[bank], 1)
                pe.wait_ge(bank_full[bank], st.use("o", j, 1)[1] + 1)
                pe.sem_inc(w_used, 1)

            pe.wait_ge(c_ready, 1)
            pe.wait_ge(consts, 3)
            pro = Prologue()
            n = 0
            for kind, i in PRO:
                if kind == "mod":
                    modulation(i, n)
                    n += 4
                    if i in (1, 2, 3, 7, 8, 9, 10):
                        mod_transpose(i - 1)
                    if i == 3:
                        mod_transpose(3)
                    if i == 6:
                        v_transpose(pro, 0)
                    if i == 7:
                        v_tails(pro, 0)
                elif kind == "t1":
                    t_units(pro, "t1", 0)
                    pe.wait_ge(t_lo, 8)
                else:
                    project(pro, kind, i, n, n)
                    n += 1

            def attention(st):
                for s in range(10):
                    if s < 8:
                        head_scores(st, s)
                    if 2 <= s <= 9:
                        head_values(st, s - 2)
                    if 1 <= s <= 8:
                        prob_transpose(st, s - 1, 0)
                        prob_transpose(st, s - 1, 1)
                    for j in FILLS.get(s, []):
                        if j < 8 or st.next:
                            kind, p = BODY_SLOTS[j]
                            if j == 8:
                                pe.wait_ge(t_lo, 2 * (st.x_t1 + 4))
                            project(st, kind, p, st.base + j, BASE_BODY + j)
                    if s == 6 and st.next:
                        t_units(st, "t1", st.x_t1)
                    if 1 <= s <= 8:
                        prob_transpose(st, s - 1, 2)
                    if s in (2, 4, 6):
                        v_transpose(st, s // 2)
                    if s in (3, 5, 7):
                        v_tails(st, s // 2)
                    if s in (4, 6, 8):
                        vals_transpose(st, s // 2 - 2)
                vals_transpose(st, 3)
                o0 = 11 if st.next else 8
                for j in range(4):
                    out_projection(st, j, st.base + o0 + j, BASE_BODY + o0 + j)
                    if j == 0 and st.next:
                        v_transpose(st, 0, 1)
                    if j == 1 and st.next:
                        v_tails(st, 0, 1)
                if st.next:
                    project(st, "q", 1, st.base + 15, BASE_BODY + 15)
                t_units(st, "t2", st.x_t2)

            with pe.Fori(0, B - 1) as b:
                attention(Stage(b, True))
            attention(Stage(B - 1, False))
            for bank in (3, 4, 5, 6, 7):
                total = PRO_N.get(bank, 0) + (B - 1) * BODY_N.get(bank, 0) + LAST_N.get(bank, 0)
                pe.wait_ge(bank_free[bank], total)
            pe.wait_ge(scores_free, HEADS * B + 1)
            pe.sem_inc(att_done, 1)

            def mlp_slot(n, r):
                pe.wait_ge(w_lo, n + 1)
                return w_h[:, r, :], w_l[:, r, :]

            def down_chunk(n, r, k_count, first, last_chunk, blk):
                wh, wl = mlp_slot(n, r)
                pe.wait_ge(a_lo, k_count + 1)
                for tt in range(TT):
                    c = slice(P * tt, P * tt + P)
                    banks = (ps[:, 2 * tt, :], ps[:, 2 * tt + 1, :])
                    d = (slice(0, 512), slice(512, 1024))
                    for dh in range(2):
                        mm(banks[dh], a_h[:, r, c], wh[:, d[dh]], start=first, stop=False)
                        mm(banks[dh], a_h[:, r, c], wl[:, d[dh]], start=False, stop=False)
                    for dh in range(2):
                        last = mm(banks[dh], a_l[:, r, c], wh[:, d[dh]], start=False, stop=last_chunk)
                        if last_chunk:
                            last.then_inc(down_full, 1)
                if last_chunk:
                    pe.wait_ge(down_full, 8 * blk + 8)
                    pe.sem_inc(w_used, 1)
                else:
                    last.then_inc(w_used, 1)

            with pe.Fori(0, B) as blk:
                n0 = BASE_MLP + MLP_SLOTS * blk
                pe.wait_ge(ht_loaded, 32 * blk + 32)
                hold(pe, "pe")
                with pe.Fori(0, FT // 2) as i:
                    for s in range(2):
                        tile = FT * blk + 2 * i + s
                        for r, (filled, bank) in enumerate(((gate_full, 2 * s), (up_full, 2 * s + 1))):
                            wh, wl = mlp_slot(n0 + 4 * i + 2 * s + r, r)
                            pe.wait_ge(silu_ready if r == 0 else act_ready, tile + 1)
                            for k in range(DK):
                                c = slice(P * k, P * k + P)
                                last = three(ps[:, bank, :], wh[:, c], wl[:, c], ht_h[:, k, :], ht_l[:, k, :],
                                             k == 0, k == DK - 1)
                            last.then_inc(filled, 1)
                            pe.wait_ge(filled, tile + 1)
                            pe.sem_inc(w_used, 1)
                pe.wait_ge(act_ready, FT * blk + FT + 2)
                nd = n0 + 2 * FT
                down_chunk(nd, 0, FT * blk, True, False, blk)
                down_chunk(nd + 1, 1, FT * blk + 1, False, False, blk)
                with pe.Fori(1, FT // 2 - 1) as i:
                    for r in range(2):
                        down_chunk(nd + 2 * i + r, r, FT * blk + 2 * i + r, False, False, blk)
                down_chunk(nd + FT - 2, 0, FT * blk + FT - 2, False, False, blk)
                down_chunk(nd + FT - 1, 1, FT * blk + FT - 1, False, True, blk)
                pe.wait_ge(down_free, 8 * blk + 8)


def kernel(**inputs):
    import numpy as np
    import concourse.bacc as bacc
    from concourse.bass_utils import run_bass_kernel_spmd as run

    g = {k: np.asarray(v) for k, v in inputs.items()}
    pad = FT * P - F
    gate, up = (np.pad(g[n], ((0, pad), (0, 0))).reshape(FT, P, DK, P).transpose(0, 3, 2, 1)
                for n in ("L0_ffn_W_gate", "L0_ffn_W_up"))
    gate_up = np.stack([gate, up], axis=1).reshape(2 * FT, P, W)
    down = np.pad(g["L0_ffn_W_down"], ((0, 0), (0, pad))).T.reshape(FT, P, D)
    arrays = {
        "x_in": g["L0_attn_x"],
        "c_in": g["L0_c"].T.reshape(DK, P, B).transpose(1, 0, 2),
        "w_mod": g["L0_wmod"].reshape(4, 2, P, MOD_CHUNKS, 512).transpose(3, 0, 2, 1, 4).reshape(4 * MOD_CHUNKS, P, W),
        "w_pairs": g["L0_attn_w_qkv"].reshape(3, PAIRS, P, DK, P).transpose(1, 0, 4, 3, 2).reshape(3 * PAIRS, P, W),
        "b_pairs": g["L0_attn_b_qkv"].reshape(3, PAIRS, P).transpose(2, 1, 0).reshape(P, 3 * PAIRS),
        "w_o": g["L0_attn_w_o"].reshape(4, 256, PAIRS, P).transpose(0, 3, 2, 1).reshape(4, P, W),
        "b_o": g["L0_attn_b_o"],
        "w_mlp": np.concatenate([gate_up, down], axis=0),
    }
    arrays = {k: np.ascontiguousarray(v) for k, v in arrays.items()}
    nc = bacc.Bacc("TRN2", target_bir_lowering=False, num_devices=1)
    args = [nc.dram_tensor(k, a.shape, F32, kind="ExternalInput").ap() for k, a in arrays.items()]
    y = nc.dram_tensor("y_out", (B, S, D), F32, kind="ExternalOutput").ap()
    mlp_block(nc, *args, y)
    r = run(nc, [arrays], core_ids=[0])
    return r.results[0]["y_out"]
```

```python
from contextlib import ExitStack

import concourse.bass as bass
from concourse import mybir

F32 = mybir.dt.float32
F32R = mybir.dt.float32r
I32 = mybir.dt.int32
U32 = mybir.dt.uint32
ALU = mybir.AluOpType
ACT = mybir.ActivationFunctionType
AX = mybir.AxisListType

P = 128
B, S, D = 4, 512, 1024
PART = 512
HEADS, HD = 8, 64
PAIRS = HEADS // 2
F = 2752
FT = -(-F // P)
DK = D // P
TT = S // P
NEG = -10000.0
EPS = 1e-5
W = 1024
RAW, SPLIT = 4, 2
GATE_SLOTS = 4
MOD_CHUNKS = 6 * D // 512
GATES = {4: (0, 0), 5: (0, 1), 10: (1, 0), 11: (1, 1)}

PRO = ([("mod", n) for n in range(4)] + [("t1", 0)] + [("q", 0), ("mod", 4), ("k", 0), ("mod", 5), ("v", 0), ("mod", 6)]
       + [("q", 1)] + [("mod", n) for n in range(7, MOD_CHUNKS)])
PRO_SLOTS = []
for kind, n in PRO:
    if kind == "mod":
        PRO_SLOTS += [("mod", 4 * n + q) for q in range(4)]
    elif kind != "t1":
        PRO_SLOTS.append((kind, n))
BODY_SLOTS = [("k", 1), ("v", 1), ("q", 2), ("k", 2), ("v", 2), ("q", 3), ("k", 3), ("v", 3),
              ("q", 0), ("k", 0), ("v", 0), ("o", 0), ("o", 1), ("o", 2), ("o", 3), ("q", 1)]
LAST_SLOTS = BODY_SLOTS[:8] + BODY_SLOTS[11:15]
FILLS = {0: [0], 1: [1, 2], 2: [3], 3: [4, 5], 4: [6], 5: [7], 7: [8], 8: [9], 9: [10]}
BASE_BODY = len(PRO_SLOTS)
BASE_LAST = BASE_BODY + (B - 1) * len(BODY_SLOTS)
BASE_MLP = BASE_LAST + len(LAST_SLOTS)
MLP_SLOTS = 3 * FT
assert BASE_BODY % RAW == 0 and BASE_MLP % RAW == 0 and GATE_SLOTS == RAW and FT % 2 == 0

STRIP = {3: 0, 2: 512, 0: 896, 1: 1024}
STRIPS = 1280
TP_UNITS = [(0, 512), (512, 1024), (1024, 1280)]
TP_BANK = [3, 4, 3]


FILL_BANK = {("k", 1): 7, ("v", 1): 6, ("q", 2): 7, ("k", 2): 6, ("v", 2): 7, ("q", 3): 6, ("k", 3): 7, ("v", 3): 6,
             ("q", 0): 7, ("k", 0): 6, ("v", 0): 7, ("q", 1): 6}
VT_BANK = {1: 7, 2: 6, 3: 6}


def body_fills(s, has_next):
    return [j for j in FILLS.get(s, []) if j < 8 or has_next]


def next_fills(s, has_next):
    if s == 9:
        return [11 if has_next else 8]
    return body_fills(7 if s == 6 else s + 1, has_next) if s != 5 else []


def step_uses(s, has_next):
    out = []
    fills = [(FILL_BANK[BODY_SLOTS[j]], BODY_SLOTS[j]) for j in body_fills(s, has_next)]
    out += fills[:-1]
    if 2 <= s <= 9:
        out.append((5, ("pv", s - 2)))
    if 1 <= s <= 8:
        out += [(3, ("tp", s - 1, 0)), (4, ("tp", s - 1, 1))]
    out += fills[-1:]
    if s == 6 and has_next:
        out += [(6 + kh, ("t1", tt, kh)) for tt in range(TT) for kh in range(2)]
    if 1 <= s <= 8:
        out.append((3, ("tp", s - 1, 2)))
    if s in (2, 4, 6):
        out.append((VT_BANK[s // 2], ("vt", s // 2)))
    if s in (3, 5, 7):
        out.append((5, ("vs", s // 2)))
    if s in (4, 6, 8):
        out.append((5, ("vals", s // 2 - 2)))
    return out


def stage_uses(has_next):
    out = [u for s in range(10) for u in step_uses(s, has_next)]
    out.append((5, ("vals", 3)))
    for j in range(4):
        out += [(3, ("o", j, 0)), (4, ("o", j, 1))]
        if has_next and j == 0:
            out.append((6, ("vt", 0)))
        if has_next and j == 1:
            out.append((5, ("vs", 0)))
    if has_next:
        out.append((6, ("q", 1)))
    t2_bank = 3 if has_next else 6
    out += [(t2_bank + kh, ("t2", tt, kh)) for tt in range(TT) for kh in range(2)]
    return out


def prologue_uses():
    out = []
    for kind, n in PRO:
        if kind == "mod":
            out.append((3 + n % 2, ("mod", n)))
            if n in (1, 2, 3, 7, 8, 9, 10):
                out.append((5, ("mt", n - 1)))
            if n == 3:
                out.append((5, ("mt", 3)))
            if n == 6:
                out.append((6, ("vt", 0)))
            if n == 7:
                out.append((7, ("vs", 0)))
        elif kind == "t1":
            out += [(6 + kh, ("t1", tt, kh)) for tt in range(TT) for kh in range(2)]
        else:
            out.append((FILL_BANK[kind, n], (kind, n)))
    return out


def filled_by(label):
    if label[0] in ("q", "k", "v", "mod") or (label[0] == "o" and label[2] == 1):
        return "w_used"
    return "xn_used" if label[0] in ("t1", "t2") and label[2] == 1 else "bank_full"


def number(uses):
    seen, full, at = {}, {}, {}
    for bank, label in uses:
        at[label] = (bank, seen.get(bank, 0), full.get(bank, 0))
        seen[bank] = seen.get(bank, 0) + 1
        full[bank] = full.get(bank, 0) + (filled_by(label) == "bank_full")
    return at, seen, full


PRO_AT, PRO_N, PRO_FULL = number(prologue_uses())
BODY_AT, BODY_N, BODY_FULL = number(stage_uses(True))
LAST_AT, LAST_N, LAST_FULL = number(stage_uses(False))


class Stage:

    def __init__(self, b, has_next):
        self.b, self.next = b, has_next
        self.at = BODY_AT if has_next else LAST_AT
        self.slots = BODY_SLOTS if has_next else LAST_SLOTS
        self.base = BASE_BODY + len(BODY_SLOTS) * b
        self.x_t1 = 4 + 8 * b
        self.x_t2 = self.x_t1 + (4 if has_next else 0)

    def use(self, *label):
        bank, n, _ = self.at[label]
        return bank, PRO_N.get(bank, 0) + BODY_N.get(bank, 0) * self.b + n

    def made(self, *label):
        bank, n = self.use(*label)
        return bank, n + 1

    def pair(self, p, ahead=0):
        return PAIRS * self.b + PAIRS * ahead + p

    def before(self, bank):
        return PRO_N.get(bank, 0) + BODY_N.get(bank, 0) * self.b

    def filled(self, *label):
        bank, _, n = self.at[label]
        how = filled_by(label)
        if how == "w_used":
            slot = ("o", label[1]) if label[0] == "o" else label
            return how, self.base + self.slots.index(slot) + 1
        if how == "xn_used":
            return how, (self.x_t1 if label[0] == "t1" else self.x_t2) + label[1] + 1
        return bank, PRO_FULL.get(bank, 0) + BODY_FULL.get(bank, 0) * self.b + n + 1


class Prologue:
    b, next, x_t1 = 0, True, 0

    def use(self, *label):
        return PRO_AT[label][:2]

    def made(self, *label):
        bank, n, _ = PRO_AT[label]
        return bank, n + 1

    def pair(self, p, ahead=0):
        return p

    def filled(self, *label):
        bank, _, n = PRO_AT[label]
        how = filled_by(label)
        if how == "w_used":
            slot = ("mod", 4 * label[1] + 3) if label[0] == "mod" else label
            return how, PRO_SLOTS.index(slot) + 1
        return (how, label[1] + 1) if how == "xn_used" else (bank, n + 1)


def mlp_block(nc, x, c_t, w_mod, w_pairs, b_pairs, w_out, b_out, w_mlp, out):
    ctx = ExitStack()
    with ctx:
        attention_only = ExitStack()

        def sb(name, shape, dt=F32, where=ctx):
            return where.enter_context(nc.sbuf_tensor(name, shape, dt))

        def att(name, shape, dt=F32):
            return sb(name, shape, dt, attention_only)

        def sem(name):
            return ctx.enter_context(nc.semaphore(name))

        gate_rows = nc.dram_tensor("gate_rows", (2, B, D), F32, kind="Internal").ap()
        x1_dram = nc.dram_tensor("x1_dram", (B, P, TT, D), F32, kind="Internal").ap()
        h2_dram = nc.dram_tensor("h2_dram", (B, 2, P, DK, S), F32R, kind="Internal").ap()

        raw = sb("raw", [P, RAW, W])
        w_h = sb("w_h", [P, SPLIT, W], F32R)
        w_l = sb("w_l", [P, SPLIT, W], F32R)
        ht_h = sb("ht_h", [P, DK, S], F32R)
        ht_l = sb("ht_l", [P, DK, S], F32R)

        q_st = att("q_st", [P, 2, 2, S], F32R)
        k_h = att("k_h", [P, 2, 2, S], F32R)
        k_l = att("k_l", [P, 2, 2, S], F32R)
        v_h = att("v_h", [P, 2, TT, P], F32R)
        v_l = att("v_l", [P, 2, TT, P], F32R)
        v_tail = att("v_tail", [P, 2, TT, P])
        probs = att("probs", [P, 2, STRIPS])
        pt_h = att("pt_h", [P, STRIPS], F32R)
        pt_l = att("pt_l", [P, STRIPS], F32R)
        vals = att("vals", [P, 2, TT, P])
        v_col = att("v_col", [P, S])
        vt_h = att("vt_h", [P, PAIRS, S], F32R)
        vt_l = att("vt_l", [P, PAIRS, S], F32R)
        x_next = att("x_next", [P, TT, D])
        x_cur = att("x_cur", [P, TT, D])
        xn = att("xn", [P, 2, D])
        h_tmp = att("h_tmp", [P, 2, S])
        ga_row = att("ga_row", [P, D])
        bo_row = att("bo_row", [P, D])
        o_tmp = att("o_tmp", [P, 2, 256])
        mod_t = att("mod_t", [P, MOD_CHUNKS * 4, B])
        mod_a = att("mod_a", [P, 2 * DK])
        mod_b = att("mod_b", [P, 2 * DK])
        bias = att("bias", [P, 3 * PAIRS])
        c_sb = att("c_sb", [P, DK, B])
        c_act = att("c_act", [P, DK, B])
        ident = att("ident", [P, P])
        ones = att("ones", [P, P], F32R)
        masked = att("masked", [P, P])
        neg_fill = att("neg_fill", [P, P])
        neg_col = att("neg_col", [P, 1])
        n_tail = att("n_tail", [P, TT])
        neg_m = att("neg_m", [P, 4, TT])
        tail_e = att("tail_e", [P, 4, TT])
        sums = att("sums", [P, 4, TT])
        den = att("den", [P, 4, TT])
        r_den = att("r_den", [P, 4, TT])
        tail_w = att("tail_w", [P, TT, HD])
        pv_sum = att("pv_sum", [P, TT, HD])
        stats = att("stats", [P, TT, 2, 6])
        mv = att("mv", [P, TT, 2])
        ve = att("ve", [P, TT])
        rs = att("rs", [P, 2, TT])
        rt = att("rt", [P, TT])
        c_st = pt_h[:, 0:DK * P].rearrange("p (k m) -> p k m", k=DK)
        mod_lo = probs[0:B, 0, 0:1024].rearrange("p (n c) -> p n c", n=2)
        mod_row = probs[0:B, 1, 0:1024].rearrange("p (n c) -> p n c", n=2)
        gate_row = x_cur[0:B, 0, :].rearrange("p (n c) -> p n c", n=2)
        gate_row2 = x_cur[0:B, 1, :].rearrange("p (n c) -> p n c", n=2)
        gate_sgn = x_cur[0:B, 2, 0:512]
        gate_abs = x_cur[0:B, 2, 512:1024]

        attention_only.close()
        gu_h = sb("gu_h", [P, GATE_SLOTS, W], F32R)
        gu_l = sb("gu_l", [P, GATE_SLOTS, W], F32R)
        silu = sb("silu", [P, 2, S])
        act = sb("act", [P, FT, S])
        raw_down = sb("raw_down", [P, 2, W])
        a_h = sb("a_h", [P, 2, S], F32R)
        a_l = sb("a_l", [P, 2, S], F32R)
        gb_row = sb("gb_row", [P, D])
        x1_sb = sb("x1_sb", [P, TT, D])
        y_sb = sb("y_sb", [P, 2, S])

        ps = ctx.enter_context(nc.psum_tensor("ps", [P, 8, 512], F32))
        scores = ps[:, 0:3, :].rearrange("p b c -> p (b c)")

        w_loaded = [sem(f"w_loaded{i}") for i in range(RAW)]
        down_loaded = [sem(f"down_loaded{i}") for i in range(2)]
        w_hi, w_lo, w_used = sem("w_hi"), sem("w_lo"), sem("w_used")
        small_loaded = sem("small_loaded")
        c_loaded = sem("c_loaded")
        c_silu, c_ready = sem("c_silu"), sem("c_ready")
        consts = sem("consts")
        pool_consts = sem("pool_consts")
        bank_full = {k: sem(f"bank_full{k}") for k in range(3, 8)}
        bank_free = {k: sem(f"bank_free{k}") for k in range(3, 8)}
        scores_full, scores_free = sem("scores_full"), sem("scores_free")
        mod_lo_ready, mod_picked = sem("mod_lo_ready"), sem("mod_picked")
        gate_ready, gate_stored = sem("gate_ready"), sem("gate_stored")
        x0_loaded, x_loaded, xc_loaded, ga_loaded = sem("x0_loaded"), sem("x_loaded"), sem("xc_loaded"), sem("ga_loaded")
        xn_ready, xn_used = sem("xn_ready"), sem("xn_used")
        t_hi, t_lo = sem("t_hi"), sem("t_lo")
        q_hi, k_hi, v_hi = sem("q_hi"), sem("k_hi"), sem("v_hi")
        negm_ready, exp_done = sem("negm_ready"), sem("exp_done")
        pt_hi, vals_ready, vals_hi = sem("pt_hi"), sem("vals_ready"), sem("vals_hi")
        x1_ready, x1_stored = sem("x1_ready"), sem("x1_stored")
        h2_stored = [sem(f"h2_stored{i}") for i in range(4)]
        stage_clear = sem("stage_clear")
        ht_loaded, ht_free = sem("ht_loaded"), sem("ht_free")
        silu_ready, act_ready = sem("silu_ready"), sem("act_ready")
        a_hi, a_lo = sem("a_hi"), sem("a_lo")
        down_full = sem("down_full")
        mlp_loaded = sem("mlp_loaded")
        y_ready, y_added, out_stored = sem("y_ready"), sem("y_added"), sem("out_stored")
        att_done = sem("att_done")
        waited = {e: sem(f"waited_{e}") for e in ("pool", "dve", "pe")}

        def hold(engine, name):
            engine.sem_inc(waited[name], 1)

        def filled(engine, st, *label):
            how, value = st.filled(*label)
            engine.wait_ge({"w_used": w_used, "xn_used": xn_used}[how] if isinstance(how, str) else bank_full[how], value)
            return st.use(*label)[0]

        def made(engine, st, *label):
            bank, count = st.made(*label)
            engine.wait_ge(bank_free[bank], count)

        block = ctx.enter_context(nc.Block())

        @block.sync
        def _(sp):
            def load(n, static_n, src):
                if not isinstance(n, int) or n >= RAW:
                    sp.wait_ge(w_lo, n - RAW + 1)
                sp.dma_start(raw[:, static_n % RAW, :], src).then_inc(w_loaded[static_n % RAW], 16)

            def source(kind, i):
                return {"mod": w_mod, "o": w_out}[kind][i] if kind in ("mod", "o") else w_pairs[3 * i + "qkv".index(kind)]

            sp.dma_start(c_sb[:], c_t).then_inc(c_loaded, 16)
            for n, (kind, i) in enumerate(PRO_SLOTS):
                load(n, n, source(kind, i))
                if n == 3:
                    sp.dma_start(x_next[:], x[0].rearrange("(t p) d -> p t d", p=P)).then_inc(x0_loaded, 16)
                    sp.dma_start(bias[:], b_pairs).then_inc(small_loaded, 16)
                    sp.dma_start(bo_row[:], b_out.partition_broadcast(P)).then_inc(small_loaded, 16)
            with sp.Fori(0, B - 1) as b:
                for j, (kind, i) in enumerate(BODY_SLOTS):
                    load(BASE_BODY + 16 * b + j, BASE_BODY + j, source(kind, i))
            for j, (kind, i) in enumerate(LAST_SLOTS):
                load(BASE_LAST + j, BASE_LAST + j, source(kind, i))

            with sp.Fori(0, B) as blk:
                n0 = BASE_MLP + MLP_SLOTS * blk
                with sp.Fori(0, FT // 2) as i:
                    for r in range(GATE_SLOTS):
                        sp.wait_ge(w_lo, n0 + 4 * i + r - RAW + 1)
                        sp.dma_start(raw[:, r, :], w_mlp[i * 4 + r]).then_inc(w_loaded[r], 16)
                with sp.Fori(0, FT // 2) as i:
                    for r in range(2):
                        sp.wait_ge(w_lo, n0 + 2 * FT + 2 * i + r - 1)
                        sp.dma_start(raw_down[:, r, :], w_mlp[i * 2 + r + 2 * FT]).then_inc(down_loaded[r], 16)

        @block.gpsimd
        def _(pool):
            pool.sem_inc(stage_clear, 1)
            nc.gpsimd.memset(ident[:], 0.0).then_inc(pool_consts, 1)
            nc.gpsimd.memset(masked[:], 0.0).then_inc(pool_consts, 1)
            pool.wait_ge(pool_consts, 2)
            nc.gpsimd.affine_select(out=ident[:], in_=ident[:], compare_op=ALU.not_equal, fill=1.0, base=0,
                                    pattern=[[-1, P]], channel_multiplier=1).then_inc(consts, 1)
            nc.gpsimd.affine_select(out=masked[:], in_=masked[:], compare_op=ALU.is_ge, fill=1.0, base=0,
                                    pattern=[[-1, P]], channel_multiplier=1).then_inc(consts, 1)

            def t_unit_lo(u_count, dst, tmp, hi):
                pool.wait_ge(t_hi, u_count + 1)
                nc.gpsimd.tensor_tensor(dst, tmp, hi.bitcast(F32), ALU.subtract).then_inc(t_lo, 1)

            def t1_units(x0):
                for tt in range(TT):
                    for kh in range(2):
                        sl = (slice(None), slice(4 * kh, 4 * kh + 4), slice(P * tt, P * tt + P))
                        tmp = h_tmp[:, kh, :].rearrange("p (k t) -> p k t", k=4)
                        t_unit_lo(2 * (x0 + tt) + kh, ht_l[sl], tmp, ht_h[sl])

            t1_units(0)
            for i, n in enumerate(sorted(GATES)):
                which, half = GATES[n]
                pool.wait_ge(gate_ready, i + 1)
                src = (gate_row if which == 0 else gate_row2)[:, half, :]
                pool.dma_start(gate_rows[which][:, 512 * half:512 * half + 512], src).then_inc(gate_stored, 16)
            pool.wait_ge(gate_stored, 64)

            def attention(st):
                b = st.b
                pool.wait_ge(xn_ready, 8 * b + 4)
                hold(pool, "pool")
                pool.dma_start(x_cur[:], x[b].rearrange("(t p) d -> p t d", p=P)).then_inc(xc_loaded, 16)
                pool.dma_start(ga_row[:], gate_rows[0][b].partition_broadcast(P)).then_inc(ga_loaded, 16)
                if st.next:
                    pool.dma_start(x_next[:], x[b + 1].rearrange("(t p) d -> p t d", p=P)).then_inc(x_loaded, 16)
                    t1_units(st.x_t1)
                else:
                    pool.wait_ge(w_used, BASE_LAST + 8)
                    load_h2(0)
                pool.wait_ge(x1_ready, b + 1)
                hold(pool, "pool")
                pool.dma_start(x1_dram[b], x_cur[:]).then_inc(x1_stored, 16)
                for tt in range(TT):
                    for kh in range(2):
                        u = 2 * tt + kh
                        count = 2 * (st.x_t2 + tt) + kh
                        t_unit_lo(count, vt_l[:, u % 4, :], h_tmp[:, kh, :], vt_h[:, u % 4, :])
                        pool.wait_ge(t_lo, count + 1)
                        hold(pool, "pool")
                        for hl, stage in ((0, vt_h), (1, vt_l)):
                            pool.dma_start(h2_dram[b][hl][:, 4 * kh:4 * kh + 4, P * tt:P * tt + P],
                                           stage[:, u % 4, :].rearrange("p (k t) -> p k t", k=4)
                                           ).then_inc(h2_stored[u % 4], 16)
                for s in range(4):
                    pool.wait_ge(h2_stored[s], 64 * b + 64)
                pool.wait_ge(x1_stored, 16 * b + 16)
                hold(pool, "pool")
                nc.gpsimd.drain().then_inc(stage_clear, 1)

            def load_h2(blk):
                pool.dma_start(ht_h[:], h2_dram[blk][0]).then_inc(ht_loaded, 16)
                pool.dma_start(ht_l[:], h2_dram[blk][1]).then_inc(ht_loaded, 16)

            with pool.Fori(0, B - 1) as b:
                attention(Stage(b, True))
            attention(Stage(B - 1, False))

            pool.sem_inc(att_done, 1)
            pool.wait_ge(att_done, 4)

            def mlp(blk, more):
                n0 = BASE_MLP + MLP_SLOTS * blk
                pool.dma_start(x1_sb[:], x1_dram[blk]).then_inc(mlp_loaded, 16)
                pool.dma_start(gb_row[:], gate_rows[1][blk].partition_broadcast(P)).then_inc(mlp_loaded, 16)
                if more:
                    pool.wait_ge(w_used, n0 + 2 * FT)
                    hold(pool, "pool")
                    load_h2(blk + 1)
                for u in range(2 * TT):
                    tt, dh = divmod(u, 2)
                    xs = x1_sb[:, tt, 512 * dh:512 * dh + 512]
                    if u == 0:
                        pool.wait_ge(mlp_loaded, 32 * blk + 32)
                    pool.wait_ge(y_ready, 8 * blk + u + 1)
                    nc.gpsimd.tensor_tensor(xs, xs, y_sb[:, u % 2, :], ALU.add).then_inc(y_added, 1)
                    pool.wait_ge(y_added, 8 * blk + u + 1)
                    hold(pool, "pool")
                    pool.dma_start(out[blk][P * tt:P * tt + P, 512 * dh:512 * dh + 512], xs).then_inc(out_stored, 16)
                pool.wait_ge(out_stored, 128 * blk + 128)
                hold(pool, "pool")

            with pool.Fori(0, B - 1) as blk:
                mlp(blk, True)
            mlp(B - 1, False)

        @block.scalar
        def _(act_e):
            A, COPY = nc.scalar.activation, nc.scalar.copy

            def weight_hi(n, static_n):
                act_e.wait_ge(w_loaded[static_n % RAW], 16 * (n // RAW + 1) if isinstance(n, int)
                              else (16 * (static_n // RAW + 1) + (n - static_n) * (16 // RAW)))
                if not isinstance(n, int) or n >= SPLIT:
                    act_e.wait_ge(w_used, n - SPLIT + 1)
                COPY(w_h[:, static_n % SPLIT, :], raw[:, static_n % RAW, :]).then_inc(w_hi, 1)

            def t_units(st, name, x0, mod, picked):
                act_e.wait_ge(mod_picked, picked)
                for tt in range(TT):
                    for kh in range(2):
                        bank = filled(act_e, st, name, tt, kh)
                        count = 2 * (x0 + tt) + kh
                        if not isinstance(count, int) or count >= 2:
                            act_e.wait_ge(t_lo, count - 1)
                        for k in range(4):
                            last = A(h_tmp[:, kh, P * k:P * k + P], ps[:, bank, P * k:P * k + P], ACT.Identity,
                                     bias=mod[:, 4 * kh + k:4 * kh + k + 1],
                                     scale=mod[:, DK + 4 * kh + k:DK + 4 * kh + k + 1])
                        last.then_inc(bank_free[bank], 1)

            def q_evac(st, p):
                bank = filled(act_e, st, "q", p)
                col = bias[:, 3 * p:3 * p + 1]
                A(q_st[0:64, p % 2, 0, :], ps[0:64, bank, :], ACT.Identity, bias=col[0:64])
                A(q_st[64:128, p % 2, 1, :], ps[64:128, bank, :], ACT.Identity, bias=col[64:128]).then_inc(q_hi, 1)

            def k_evac(st, p):
                bank = filled(act_e, st, "k", p)
                col = bias[:, 3 * p + 1:3 * p + 2]
                for hd in range(2):
                    rows = slice(64 * hd, 64 * hd + 64)
                    for half in (0, 64):
                        last = A(k_h[half:half + 64, p % 2, hd, :], ps[rows, bank, :], ACT.Identity, bias=col[rows])
                last.then_inc(k_hi, 1)

            def v_evac(st, p):
                bank = filled(act_e, st, "v", p)
                A(v_col[:], ps[:, bank, :], ACT.Identity, bias=bias[:, 3 * p + 2:3 * p + 3]).then_inc(bank_free[bank], 1)

            def vt_evac(st, p):
                bank = filled(act_e, st, "vt", p)
                COPY(v_h[:, p % 2].rearrange("p t c -> p (t c)"), ps[:, bank, :]).then_inc(v_hi, 1)

            def vs_evac(st, p):
                bank = filled(act_e, st, "vs", p)
                COPY(v_tail[:, p % 2, 0:3, :].rearrange("p t c -> p (t c)"), ps[:, bank, 0:384]
                     ).then_inc(bank_free[bank], 1)

            def vals_evac(st, p):
                bank = filled(act_e, st, "vals", p)
                COPY(vt_h[:, p, :], ps[:, bank, :]).then_inc(vals_hi, 1)

            def tp_evac(st, h, u):
                bank = filled(act_e, st, "tp", h, u)
                lo, hi = TP_UNITS[u]
                COPY(pt_h[:, lo:hi], ps[:, bank, 0:hi - lo]).then_inc(pt_hi, 1)

            def softmax(st, h):
                g = 8 * st.b + h
                act_e.wait_ge(negm_ready, g + 1)
                par = h % 4
                for i in (3, 2, 0, 1):
                    o, n = STRIP[i], P * (i + 1)
                    last = A(probs[:, h % 2, o:o + n], scores[:, o:o + n], ACT.Exp, bias=neg_m[:, par, i:i + 1],
                             accum_out=sums[:, par, i:i + 1])
                last.then_inc(scores_free, 1)
                A(tail_e[:, par, :], neg_m[:, par, :], ACT.Exp, bias=neg_col[:]).then_inc(exp_done, 1)

            EVAC = {"q": q_evac, "k": k_evac, "v": v_evac}

            act_e.sem_inc(scores_free, 1)
            act_e.wait_ge(c_loaded, 16)
            A(c_act[:], c_sb[:], ACT.Silu).then_inc(c_silu, 1)
            act_e.wait_ge(small_loaded, 32)
            pro = Prologue()

            def pro_evac(kind, n):
                if kind == "mod":
                    bank = filled(act_e, pro, "mod", n)
                    if n >= 2:
                        made(act_e, pro, "mod", n - 2)
                    COPY(mod_lo[:, n % 2, :], ps[32:32 + B, bank, :]).then_inc(mod_lo_ready, 1)
                    if n == 6:
                        vt_evac(pro, 0)
                    if n == 7:
                        vs_evac(pro, 0)
                elif kind == "t1":
                    t_units(pro, "t1", 0, mod_a, 1)
                else:
                    EVAC[kind](pro, n)

            n = 0
            for idx, (kind, i) in enumerate(PRO):
                for _ in range({"mod": 4, "t1": 0}.get(kind, 1)):
                    weight_hi(n, n)
                    n += 1
                if idx:
                    pro_evac(*PRO[idx - 1])
            pro_evac(*PRO[-1])
            weight_hi(BASE_BODY, BASE_BODY)
            act_e.wait_ge(gate_stored, 64)
            act_e.wait_ge(mod_picked, 1)

            def gate_hi(n, r, blk, i):
                act_e.wait_ge(w_loaded[r], 16 * (BASE_MLP // RAW + FT // 2 * blk + i + 1))
                COPY(gu_h[:, r, :], raw[:, r, :]).then_inc(w_hi, 1)

            def gate_hi_first(blk, used):
                act_e.wait_ge(w_used, used)
                for r in range(GATE_SLOTS):
                    gate_hi(BASE_MLP + MLP_SLOTS * blk + r, r, blk, 0)

            def attention(st):
                for s in range(10):
                    fills = body_fills(s, st.next)
                    ahead = next_fills(s, st.next)
                    if 1 <= s <= 8:
                        tp_evac(st, s - 1, 0)
                        tp_evac(st, s - 1, 1)
                    if s < 8:
                        softmax(st, s)
                    for j in fills[:-1]:
                        EVAC[BODY_SLOTS[j][0]](st, BODY_SLOTS[j][1])
                    for j in ahead:
                        weight_hi(st.base + j, BASE_BODY + j)
                    for j in fills[-1:]:
                        EVAC[BODY_SLOTS[j][0]](st, BODY_SLOTS[j][1])
                    if s == 6 and st.next:
                        t_units(st, "t1", st.x_t1, mod_a, 2 * st.b + 2)
                    if 1 <= s <= 8:
                        tp_evac(st, s - 1, 2)
                    if s in (2, 4, 6):
                        vt_evac(st, s // 2)
                    if s in (3, 5, 7):
                        vs_evac(st, s // 2)
                    if s in (4, 6, 8):
                        if s == 4:
                            act_e.wait_ge(stage_clear, st.b + 1)
                        vals_evac(st, s // 2 - 2)
                vals_evac(st, 3)
                o0 = 11 if st.next else 8
                for j in range(4):
                    if st.next or j < 3:
                        weight_hi(st.base + o0 + j + 1, BASE_BODY + o0 + j + 1)
                    else:
                        gate_hi_first(0, BASE_MLP - RAW + 1)
                    if j == 0 and st.next:
                        vt_evac(st, 0)
                    if j == 1 and st.next:
                        vs_evac(st, 0)
                if st.next:
                    q_evac(st, 1)
                    weight_hi(st.base + 16, BASE_BODY + 16)
                t_units(st, "t2", st.x_t2, mod_b, 2 * st.b + 3 if st.next else 2 * st.b + 2)

            with act_e.Fori(0, B - 1) as b:
                attention(Stage(b, True))
            attention(Stage(B - 1, False))
            act_e.sem_inc(att_done, 1)

            def silu_tile(i, s, blk, first=False):
                n0 = BASE_MLP + MLP_SLOTS * blk
                act_e.wait_ge(w_used, n0 + 4 * i + 2 * s + 1)
                if not first:
                    act_e.wait_ge(act_ready, FT * blk + 2 * i + s - 1)
                A(silu[:, s, :], ps[:, 2 * s, :], ACT.Silu).then_inc(silu_ready, 1)

            def down_hi(i, r, blk):
                n = BASE_MLP + MLP_SLOTS * blk + 2 * FT + 2 * i + r
                act_e.wait_ge(down_loaded[r], 16 * (FT // 2 * blk + i + 1))
                act_e.wait_ge(w_used, n - 1)
                COPY(w_h[:, r, :], raw_down[:, r, :]).then_inc(w_hi, 1)

            def act_hi(i, r, blk):
                act_e.wait_ge(act_ready, FT * blk + 2 * i + r + 1)
                COPY(a_h[:, r, :], act[:, bass.ds(2 * i + r, 1), :].rearrange("p a t -> p (a t)")).then_inc(a_hi, 1)

            def mlp(blk, more):
                n0 = BASE_MLP + MLP_SLOTS * blk

                def gate_pair(i, first=False):
                    for s in range(2):
                        silu_tile(i, s, blk, first)
                        for r in (2 * s, 2 * s + 1):
                            act_e.wait_ge(w_used, n0 + 4 * i + r + 1)
                            gate_hi(n0 + 4 * i + 4 + r, r, blk, i + 1)

                gate_pair(0, True)
                with act_e.Fori(1, FT // 2 - 1) as i:
                    gate_pair(i)
                for s in range(2):
                    silu_tile(FT // 2 - 1, s, blk)
                    down_hi(0, s, blk)
                for r in range(2):
                    act_e.wait_ge(att_done, 4)
                    act_hi(0, r, blk)
                with act_e.Fori(1, FT // 2) as i:
                    for r in range(2):
                        down_hi(i, r, blk)
                        act_hi(i, r, blk)
                if more:
                    gate_hi_first(blk + 1, n0 + 2 * FT)

            with act_e.Fori(0, B - 1) as blk:
                mlp(blk, True)
            mlp(B - 1, False)

        @block.vector
        def _(dve):
            V = nc.vector

            def weight_lo(n, static_n):
                dve.wait_ge(w_hi, n + 1)
                V.tensor_tensor(w_l[:, static_n % SPLIT, :], raw[:, static_n % RAW, :],
                                w_h[:, static_n % SPLIT, :].bitcast(F32), ALU.subtract).then_inc(w_lo, 1)

            def q_lo(st, p, ahead=0):
                bank, _ = st.use("q", p)
                dve.wait_ge(q_hi, st.pair(p, ahead) + 1)
                for hd in range(2):
                    rows, other = slice(64 * hd, 64 * hd + 64), slice(64 - 64 * hd, 128 - 64 * hd)
                    last = V.scalar_tensor_tensor(out=q_st[other, p % 2, hd, :], in0=ps[rows, bank, :],
                                                  scalar=bias[rows, 3 * p:3 * p + 1],
                                                  in1=q_st[rows, p % 2, hd, :].bitcast(F32),
                                                  op0=ALU.add, op1=ALU.subtract)
                last.then_inc(bank_free[bank], 1)

            def k_lo(st, p, ahead=0):
                bank, _ = st.use("k", p)
                dve.wait_ge(k_hi, st.pair(p, ahead) + 1)
                for hd in range(2):
                    rows = slice(64 * hd, 64 * hd + 64)
                    for half in (0, 64):
                        last = V.scalar_tensor_tensor(out=k_l[half:half + 64, p % 2, hd, :], in0=ps[rows, bank, :],
                                                      scalar=bias[rows, 3 * p + 1:3 * p + 2],
                                                      in1=k_h[rows, p % 2, hd, :].bitcast(F32),
                                                      op0=ALU.add, op1=ALU.subtract)
                last.then_inc(bank_free[bank], 1)

            def vt_lo(st, p, ahead=0):
                bank, _ = st.use("vt", p)
                dve.wait_ge(v_hi, st.pair(p, ahead) + 1)
                V.tensor_tensor(v_l[:, p % 2].rearrange("p t c -> p (t c)"), ps[:, bank, :],
                                v_h[:, p % 2].rearrange("p t c -> p (t c)").bitcast(F32), ALU.subtract
                                ).then_inc(bank_free[bank], 1)

            def vals_lo(st, p):
                bank, _ = st.use("vals", p)
                dve.wait_ge(vals_hi, st.pair(p) + 1)
                V.tensor_tensor(vt_l[:, p, :], ps[:, bank, :], vt_h[:, p, :].bitcast(F32), ALU.subtract
                                ).then_inc(bank_free[bank], 1)

            def tp_lo(st, h, u):
                bank, _ = st.use("tp", h, u)
                lo, hi = TP_UNITS[u]
                dve.wait_ge(pt_hi, 3 * (8 * st.b + h) + u + 1)
                V.tensor_tensor(pt_l[:, lo:hi], ps[:, bank, 0:hi - lo], pt_h[:, lo:hi].bitcast(F32), ALU.subtract
                                ).then_inc(bank_free[bank], 1)

            def row_max(st, h):
                par, g = h % 4, 8 * st.b + h
                dve.wait_ge(scores_full, g + 1)
                hold(dve, "dve")
                for i in range(TT):
                    o = STRIP[i] + P * i
                    V.copy_predicated(scores[:, o:o + P], masked[:].bitcast(U32), neg_fill[:])
                V.drain()
                for i in range(TT):
                    o, n = STRIP[i], P * (i + 1)
                    V.tensor_reduce(neg_m[:, par, i:i + 1], scores[:, o:o + n], AX.X, ALU.max, negate=True)
                V.drain()
                V.tensor_scalar(neg_m[:, par, 0:3], neg_m[:, par, 0:3], -NEG, None, ALU.min).then_inc(negm_ready, 1)

            def denominators(st, h):
                par, g = h % 4, 8 * st.b + h
                dve.wait_ge(exp_done, g + 1)
                V.tensor_tensor(den[:, par, :], tail_e[:, par, :], n_tail[:], ALU.mult)
                V.drain()
                V.tensor_tensor(den[:, par, :], den[:, par, :], sums[:, par, :], ALU.add)
                V.drain()
                V.reciprocal(r_den[:, par, :], den[:, par, :])

            def pv_evac(st, h):
                par, g = h % 4, 8 * st.b + h
                p, hd = divmod(h, 2)
                cols = slice(HD * hd, HD * hd + HD)
                if p:
                    made(dve, st, "vs", p)
                elif h == 0:
                    for k in (5, 7):
                        dve.wait_ge(bank_free[k], st.before(k))
                V.tensor_tensor(tail_w[:], v_tail[:, p % 2, :, cols],
                                tail_e[:, par, :].unsqueeze(2).to_broadcast([P, TT, HD]), ALU.mult)
                V.drain()
                bank = filled(dve, st, "pv", h)
                V.tensor_tensor(pv_sum[:], ps[:, bank, 0:TT * HD].rearrange("p (t c) -> p t c", t=TT), tail_w[:], ALU.add
                                ).then_inc(bank_free[bank], 1)
                V.drain()
                V.tensor_tensor(vals[:, p % 2, :, cols], pv_sum[:],
                                r_den[:, par, :].unsqueeze(2).to_broadcast([P, TT, HD]), ALU.mult).then_inc(vals_ready, 1)

            def layer_stats(xt):
                for tt in range(TT):
                    for half in range(2):
                        V.bn_stats(stats[:, tt, half, :], xt[:, tt, 512 * half:512 * half + 512])
                V.drain()
                for tt in range(TT):
                    V.bn_aggr(mv[:, tt, :], stats[:, tt, :, :])
                V.drain()
                V.tensor_scalar(ve[:], mv[:, :, 1], EPS, None, ALU.add)
                V.drain()
                V.tensor_scalar(rs[:, 0, :].bitcast(I32), ve[:].bitcast(I32), -0.5, 1597463007.0, ALU.mult, ALU.add)
                V.drain()
                for it in range(3):
                    y, y2 = rs[:, it % 2, :], rs[:, (it + 1) % 2, :]
                    V.tensor_tensor(rt[:], y, y, ALU.mult)
                    V.drain()
                    V.scalar_tensor_tensor(out=rt[:], in0=rt[:], scalar=-0.5, in1=ve[:], op0=ALU.mult, op1=ALU.mult)
                    V.drain()
                    V.scalar_tensor_tensor(out=y2, in0=rt[:], scalar=1.5, in1=y, op0=ALU.add, op1=ALU.mult)
                    V.drain()

            def normalise(xt, tt, count):
                if not isinstance(count, int) or count >= 2:
                    dve.wait_ge(xn_used, count - 1)
                V.tensor_scalar(xn[:, tt % 2, :], xt[:, tt, :], mv[:, tt, 0:1], rs[:, 1, tt:tt + 1],
                                ALU.subtract, ALU.mult).then_inc(xn_ready, 1)

            def pick(dst, first, b):
                src = mod_t[:, first:first + 2 * DK, b:b + 1] if isinstance(b, int) else \
                    mod_t[:, first:first + 2 * DK, bass.ds(b, 1)]
                V.tensor_copy(dst[:].unsqueeze(2), src).then_inc(mod_picked, 1)

            def t_units(st, name, xt, x0):
                staged, b = name == "t2", st.b
                for tt in range(TT):
                    if 2 <= tt + 1 < TT:
                        normalise(xt, tt + 1, x0 + tt + 1)
                    for kh in range(2):
                        u = 2 * tt + kh
                        made(dve, st, name, tt, kh)
                        if staged:
                            if u >= 4:
                                dve.wait_ge(h2_stored[u % 4], 64 * b + 32)
                            dst, src = vt_h[:, u % 4, :], h_tmp[:, kh, :]
                        else:
                            dst = ht_h[:, 4 * kh:4 * kh + 4, P * tt:P * tt + P]
                            src = h_tmp[:, kh, :].rearrange("p (k t) -> p k t", k=4)
                        V.tensor_copy(dst, src).then_inc(t_hi, 1)

            LO = {"q": q_lo, "k": k_lo}

            V.memset(ones[:].bitcast(F32), 1.0)
            V.memset(neg_fill[:], NEG)
            V.memset(neg_col[:], NEG)
            V.memset(v_tail[:, :, 3, :], 0.0)
            for i in range(TT):
                V.memset(n_tail[:, i:i + 1], float(P * (TT - 1 - i)))
            V.memset(c_st.bitcast(F32), 0.0)
            V.drain().then_inc(consts, 1)
            dve.wait_ge(c_silu, 1)
            V.tensor_copy(c_st[:, :, 0:B], c_act[:])
            V.drain()
            V.tensor_tensor(c_st[:, :, 32:32 + B], c_act[:], c_st[:, :, 0:B].bitcast(F32), ALU.subtract).then_inc(c_ready, 1)
            dve.wait_ge(small_loaded, 32)
            pro = Prologue()

            def mod_row_evac(n):
                bank, _ = pro.use("mod", n)
                dve.wait_ge(mod_lo_ready, n + 1)
                V.tensor_tensor(mod_row[:, n % 2, :], ps[0:B, bank, :], mod_lo[:, n % 2, :], ALU.add
                                ).then_inc(bank_free[bank], 1)
                if n in GATES:
                    V.drain()
                    which, half = GATES[n]
                    row = mod_row[:, n % 2, :]
                    V.tensor_scalar(gate_sgn, row, 0.0, 2.0, ALU.is_ge, ALU.mult)
                    V.tensor_scalar(gate_abs, row, -1.0, None, ALU.mult)
                    V.drain()
                    V.tensor_tensor(gate_abs, gate_abs, row, ALU.max)
                    V.drain()
                    V.tensor_scalar(gate_abs, gate_abs, 0.25, None, ALU.max)
                    V.drain()
                    V.scalar_tensor_tensor(out=(gate_row if which == 0 else gate_row2)[:, half, :], in0=gate_sgn,
                                           scalar=-1.0, in1=gate_abs, op0=ALU.add, op1=ALU.mult).then_inc(gate_ready, 1)
                    V.drain()

            def mod_t_evac(n):
                bank = filled(dve, pro, "mt", n)
                V.tensor_scalar(mod_t[:, 4 * n:4 * n + 4, :], ps[:, bank, 0:4 * B].rearrange("p (t b) -> p t b", t=4),
                                1.0 if n // 2 in (1, 4) else 0.0, None, ALU.add).then_inc(bank_free[bank], 1)

            def pro_evac(kind, n):
                if kind == "mod":
                    mod_row_evac(n)
                    if n in (1, 2, 3, 7, 8, 9, 10):
                        mod_t_evac(n - 1)
                    if n == 3:
                        mod_t_evac(3)
                        V.drain()
                        pick(mod_a, 0, 0)
                    if n == 6:
                        vt_lo(pro, 0)
                elif kind == "t1":
                    dve.wait_ge(x0_loaded, 16)
                    layer_stats(x_next)
                    normalise(x_next, 0, 0)
                    normalise(x_next, 1, 1)
                    t_units(pro, "t1", x_next, 0)
                elif kind in LO:
                    LO[kind](pro, n)

            n = 0
            for idx, (kind, i) in enumerate(PRO):
                for _ in range({"mod": 4, "t1": 0}.get(kind, 1)):
                    weight_lo(n, n)
                    n += 1
                if idx:
                    pro_evac(*PRO[idx - 1])
            pro_evac(*PRO[-1])
            weight_lo(BASE_BODY, BASE_BODY)

            def gate_lo(n, r):
                dve.wait_ge(w_hi, n + 1)
                V.tensor_tensor(gu_l[:, r, :], raw[:, r, :], gu_h[:, r, :].bitcast(F32), ALU.subtract).then_inc(w_lo, 1)

            def attention(st):
                b = st.b
                for s in range(10):
                    fills = body_fills(s, st.next)
                    if s < 8:
                        row_max(st, s)
                    if 1 <= s <= 8:
                        tp_lo(st, s - 1, 0)
                        tp_lo(st, s - 1, 1)
                    if 2 <= s <= 9:
                        pv_evac(st, s - 2)
                    for j in fills[:-1]:
                        if BODY_SLOTS[j][0] in LO:
                            LO[BODY_SLOTS[j][0]](st, BODY_SLOTS[j][1])
                    for j in next_fills(s, st.next):
                        weight_lo(st.base + j, BASE_BODY + j)
                    for j in fills[-1:]:
                        kind, p = BODY_SLOTS[j]
                        if kind in LO:
                            LO[kind](st, p, 1 if j >= 8 else 0)
                    if s == 5 and st.next:
                        dve.wait_ge(x_loaded, 16 * b + 16)
                        layer_stats(x_next)
                        normalise(x_next, 0, st.x_t1)
                        normalise(x_next, 1, st.x_t1 + 1)
                        pick(mod_a, 0, b + 1)
                    if s == 6 and st.next:
                        t_units(st, "t1", x_next, st.x_t1)
                    if 1 <= s <= 8:
                        tp_lo(st, s - 1, 2)
                    if s in (2, 4, 6):
                        vt_lo(st, s // 2)
                    if s in (4, 6, 8):
                        vals_lo(st, s // 2 - 2)
                    if s < 8:
                        denominators(st, s)
                vals_lo(st, 3)
                o0 = 11 if st.next else 8
                dve.wait_ge(xc_loaded, 16 * b + 16)
                dve.wait_ge(ga_loaded, 16 * b + 16)
                for j in range(4):
                    if st.next or j < 3:
                        weight_lo(st.base + o0 + j + 1, BASE_BODY + o0 + j + 1)
                    else:
                        gate_lo(BASE_MLP, 0)
                    cols = slice(256 * j, 256 * j + 256)
                    for half in range(2):
                        bank = filled(dve, st, "o", j, half)
                        for t in range(2):
                            last = V.tensor_tensor(o_tmp[:, t, :], ps[:, bank, 256 * t:256 * t + 256], bo_row[:, cols], ALU.add)
                        last.then_inc(bank_free[bank], 1)
                        V.drain()
                        for t in range(2):
                            V.tensor_tensor(o_tmp[:, t, :], o_tmp[:, t, :], ga_row[:, cols], ALU.mult)
                        V.drain()
                        V.tensor_tensor(x_cur[:, 2 * half:2 * half + 2, cols], x_cur[:, 2 * half:2 * half + 2, cols],
                                        o_tmp[:], ALU.add)
                        V.drain()
                    if j == 0 and st.next:
                        vt_lo(st, 0, 1)
                V.drain().then_inc(x1_ready, 1)
                if not st.next:
                    gate_lo(BASE_MLP + 1, 1)
                layer_stats(x_cur)
                normalise(x_cur, 0, st.x_t2)
                normalise(x_cur, 1, st.x_t2 + 1)
                pick(mod_b, 6 * DK // 2, b)
                if st.next:
                    q_lo(st, 1, 1)
                    weight_lo(st.base + 16, BASE_BODY + 16)
                else:
                    gate_lo(BASE_MLP + 2, 2)
                    gate_lo(BASE_MLP + 3, 3)
                t_units(st, "t2", x_cur, st.x_t2)

            with dve.Fori(0, B - 1) as b:
                attention(Stage(b, True))
            attention(Stage(B - 1, False))
            V.drain().then_inc(att_done, 1)

            def act_tile(i, s, blk):
                n0 = BASE_MLP + MLP_SLOTS * blk
                dve.wait_ge(silu_ready, FT * blk + 2 * i + s + 1)
                dve.wait_ge(w_used, n0 + 4 * i + 2 * s + 2)
                tile = act[:, 2 * i + s, :] if isinstance(i, int) else \
                    act[:, bass.ds(2 * i + s, 1), :].rearrange("p a t -> p (a t)")
                V.tensor_tensor(tile, ps[:, 2 * s + 1, :], silu[:, s, :], ALU.mult).then_inc(act_ready, 1)

            def down_lo(i, r, blk):
                dve.wait_ge(w_hi, BASE_MLP + MLP_SLOTS * blk + 2 * FT + 2 * i + r + 1)
                V.tensor_tensor(w_l[:, r, :], raw_down[:, r, :], w_h[:, r, :].bitcast(F32), ALU.subtract).then_inc(w_lo, 1)

            def act_lo(i, r, blk):
                dve.wait_ge(a_hi, FT * blk + 2 * i + r + 1)
                tile = act[:, 2 * i + r, :] if isinstance(i, int) else \
                    act[:, bass.ds(2 * i + r, 1), :].rearrange("p a t -> p (a t)")
                V.tensor_tensor(a_l[:, r, :], tile, a_h[:, r, :].bitcast(F32), ALU.subtract).then_inc(a_lo, 1)

            def mlp(blk, more):
                n0 = BASE_MLP + MLP_SLOTS * blk

                def gate_pair(i):
                    for s in range(2):
                        gate_lo(n0 + 4 * i + 4 + 2 * s, 2 * s)
                        act_tile(i, s, blk)
                        gate_lo(n0 + 4 * i + 5 + 2 * s, 2 * s + 1)

                gate_pair(0)
                dve.wait_ge(att_done, 4)
                with dve.Fori(1, FT // 2 - 1) as i:
                    gate_pair(i)
                for s in range(2):
                    down_lo(0, s, blk)
                    act_tile(FT // 2 - 1, s, blk)
                for r in range(2):
                    act_lo(0, r, blk)
                with dve.Fori(1, FT // 2) as i:
                    for r in range(2):
                        down_lo(i, r, blk)
                        act_lo(i, r, blk)
                if more:
                    for r in range(GATE_SLOTS):
                        gate_lo(n0 + MLP_SLOTS + r, r)
                dve.wait_ge(mlp_loaded, 32 * blk + 32)
                for u in range(2 * TT):
                    tt, dh = divmod(u, 2)
                    if u < 7:
                        dve.wait_ge(down_full, 7 * blk + u + 1)
                    else:
                        dve.wait_ge(w_used, n0 + MLP_SLOTS)
                    if u >= 2:
                        dve.wait_ge(y_added, 8 * blk + u - 1)
                    V.tensor_tensor(y_sb[:, u % 2, :], ps[:, u, :], gb_row[:, 512 * dh:512 * dh + 512], ALU.mult
                                    ).then_inc(y_ready, 1)

            with dve.Fori(0, B - 1) as blk:
                mlp(blk, True)
            mlp(B - 1, False)

        @block.tensor
        def _(pe):
            mm = nc.tensor.matmul

            def claim(st, *label):
                bank, n = st.use(*label)
                if not isinstance(n, int) or n > 0:
                    pe.wait_ge(bank_free[bank], n)
                return bank

            def three(out, a_h_, a_l_, b_h_, b_l_, first, last):
                mm(out, a_h_, b_h_, start=first, stop=False)
                mm(out, a_h_, b_l_, start=False, stop=False)
                return mm(out, a_l_, b_h_, start=False, stop=last)

            def slot(n, static_n):
                pe.wait_ge(w_lo, n + 1)
                r = static_n % SPLIT
                return w_h[:, r, :], w_l[:, r, :]

            def project(st, kind, p, n, static_n):
                bank = claim(st, kind, p)
                wh, wl = slot(n, static_n)
                for k in range(DK):
                    c = slice(P * k, P * k + P)
                    last = three(ps[:, bank, :], wh[:, c], wl[:, c], ht_h[:, k, :], ht_l[:, k, :], k == 0, k == DK - 1)
                last.then_inc(w_used, 1)

            def modulation(n, n0):
                bank = claim(pro, "mod", n)
                for q in range(4):
                    wh, wl = slot(n0 + q, n0 + q)
                    for kk in range(2):
                        k = 2 * q + kk
                        c = slice(512 * kk, 512 * kk + 512)
                        mm(ps[:, bank, :], c_st[:, k, :], wh[:, c], start=(k == 0), stop=False)
                        last = mm(ps[:, bank, :], c_st[:, k, :], wl[:, c], start=False, stop=(k == DK - 1))
                    last.then_inc(w_used, 1)

            def mod_transpose(n):
                bank = claim(pro, "mt", n)
                made(pe, pro, "mod", n)
                for t in range(4):
                    last = nc.tensor.transpose(ps[:, bank, B * t:B * t + B], mod_row[:, n % 2, P * t:P * t + P],
                                               ident[0:B, 0:B])
                last.then_inc(bank_full[bank], 1)

            def t_units(st, name, x0, between=()):
                for tt in range(TT):
                    if tt - 1 in between:
                        between[tt - 1]()
                    pe.wait_ge(xn_ready, x0 + tt + 1)
                    for kh in range(2):
                        bank = claim(st, name, tt, kh)
                        for k in range(4):
                            c = P * (4 * kh + k)
                            last = nc.tensor.transpose(ps[:, bank, P * k:P * k + P], xn[:, tt % 2, c:c + P], ident[:])
                        last.then_inc(xn_used if kh else bank_full[bank], 1)

            def v_transpose(st, p, ahead=0):
                bank = claim(st, "vt", p)
                made(pe, st, "v", p)
                for t in range(TT):
                    last = nc.tensor.transpose(ps[:, bank, P * t:P * t + P], v_col[:, P * t:P * t + P], ident[:])
                last.then_inc(bank_full[bank], 1)

            def v_tails(st, p, ahead=0):
                bank = claim(st, "vs", p)
                made(pe, st, "vt", p)
                for i in range(3):
                    for j in range(i + 1, TT):
                        for part in (v_h, v_l):
                            last = mm(ps[:, bank, P * i:P * i + P], ones[:], part[:, p % 2, j, :],
                                      start=(j == i + 1 and part is v_h), stop=(j == TT - 1 and part is v_l))
                last.then_inc(bank_full[bank], 1)

            def head_scores(st, h):
                p, hd = divmod(h, 2)
                g = 8 * st.b + h
                if h == 0:
                    for k in (6, 7):
                        pe.wait_ge(bank_free[k], st.before(k))
                if hd == 0 and p >= 2:
                    made(pe, st, "q", p)
                if hd == 0 and p >= 1:
                    made(pe, st, "k", p)
                if not isinstance(g, int) or g > 0:
                    pe.wait_ge(scores_free, g + 1)
                for i in (3, 2, 0, 1):
                    o, n = STRIP[i], P * (i + 1)
                    mm(scores[:, o:o + n], q_st[:, p % 2, hd, P * i:P * i + P], k_h[:, p % 2, hd, 0:n], start=True, stop=False)
                    last = mm(scores[:, o:o + n], q_st[:, p % 2, hd, P * i:P * i + P], k_l[:, p % 2, hd, 0:n],
                              start=False, stop=True)
                last.then_inc(scores_full, 1)

            def prob_transpose(st, h, u):
                bank = claim(st, "tp", h, u)
                pe.wait_ge(exp_done, 8 * st.b + h + 1)
                lo, hi = TP_UNITS[u]
                for o in range(lo, hi, P):
                    last = nc.tensor.transpose(ps[:, bank, o - lo:o - lo + P], probs[:, h % 2, o:o + P], ident[:])
                last.then_inc(bank_full[bank], 1)

            def head_values(st, h):
                p, hd = divmod(h, 2)
                bank = claim(st, "pv", h)
                made(pe, st, "tp", h, 1)
                made(pe, st, "tp", h, 2)
                if hd == 0 and p:
                    made(pe, st, "vt", p)
                c = slice(HD * hd, HD * hd + HD)
                for i in range(TT):
                    for j in range(i + 1):
                        o = STRIP[i] + P * j
                        last = three(ps[:, bank, HD * i:HD * i + HD], pt_h[:, o:o + P], pt_l[:, o:o + P],
                                     v_h[:, p % 2, j, c], v_l[:, p % 2, j, c], j == 0, j == i)
                last.then_inc(bank_full[bank], 1)

            def vals_transpose(st, p):
                bank = claim(st, "vals", p)
                pe.wait_ge(vals_ready, 8 * st.b + 2 * p + 2)
                for t in range(TT):
                    last = nc.tensor.transpose(ps[:, bank, P * t:P * t + P], vals[:, p % 2, t, :], ident[:])
                last.then_inc(bank_full[bank], 1)

            def out_projection(st, j, n, static_n):
                wh, wl = slot(n, static_n)
                if j == 0:
                    made(pe, st, "vals", 3)
                for half in range(2):
                    bank = claim(st, "o", j, half)
                    for t in range(2):
                        tt = 2 * half + t
                        for p in range(PAIRS):
                            c = slice(256 * p, 256 * p + 256)
                            last = three(ps[:, bank, 256 * t:256 * t + 256], vt_h[:, p, P * tt:P * tt + P],
                                         vt_l[:, p, P * tt:P * tt + P], wh[:, c], wl[:, c], p == 0, p == PAIRS - 1)
                    last.then_inc(w_used if half else bank_full[bank], 1)

            pe.wait_ge(c_ready, 1)
            pe.wait_ge(consts, 3)
            pro = Prologue()
            n = 0
            for kind, i in PRO:
                if kind == "mod":
                    modulation(i, n)
                    n += 4
                    if i in (1, 2, 3, 7, 8, 9, 10):
                        mod_transpose(i - 1)
                    if i == 3:
                        mod_transpose(3)
                    if i == 6:
                        v_transpose(pro, 0)
                    if i == 7:
                        v_tails(pro, 0)
                elif kind == "t1":
                    t_units(pro, "t1", 0)
                    pe.wait_ge(t_lo, 8)
                else:
                    project(pro, kind, i, n, n)
                    n += 1

            def fill(st, j):
                kind, p = BODY_SLOTS[j]
                if j == 8:
                    pe.wait_ge(t_lo, 2 * (st.x_t1 + 4))
                project(st, kind, p, st.base + j, BASE_BODY + j)

            def attention(st):
                for s in range(10):
                    fills = body_fills(s, st.next)
                    if s < 8:
                        head_scores(st, s)
                    for j in fills[:-1]:
                        fill(st, j)
                    if 2 <= s <= 9:
                        head_values(st, s - 2)
                    if 1 <= s <= 8:
                        prob_transpose(st, s - 1, 0)
                        prob_transpose(st, s - 1, 1)
                    for j in fills[-1:]:
                        fill(st, j)
                    if s == 6 and st.next:
                        t_units(st, "t1", st.x_t1)
                    if 1 <= s <= 8:
                        prob_transpose(st, s - 1, 2)
                    if s in (2, 4, 6):
                        v_transpose(st, s // 2)
                    if s in (3, 5, 7):
                        v_tails(st, s // 2)
                    if s in (4, 6, 8):
                        vals_transpose(st, s // 2 - 2)
                vals_transpose(st, 3)
                o0 = 11 if st.next else 8
                for j in range(4):
                    out_projection(st, j, st.base + o0 + j, BASE_BODY + o0 + j)
                    if j == 0 and st.next:
                        v_transpose(st, 0, 1)
                    if j == 1 and st.next:
                        v_tails(st, 0, 1)
                if st.next:
                    project(st, "q", 1, st.base + 15, BASE_BODY + 15)
                if st.next:
                    t_units(st, "t2", st.x_t2)
                else:
                    pe.wait_ge(ht_loaded, 32)
                    pe.wait_ge(scores_free, HEADS * B + 1)
                    gate_slot(BASE_MLP, 0)
                    gate_slot(BASE_MLP + 1, 1)
                    pe.wait_ge(bank_free[3], bank_total(3))
                    t_units(st, "t2", st.x_t2, {0: lambda: gate_slot(BASE_MLP + 2, 2), 1: lambda: gate_slot(BASE_MLP + 3, 3)})

            def bank_total(bank):
                return PRO_N.get(bank, 0) + (B - 1) * BODY_N.get(bank, 0) + LAST_N.get(bank, 0)

            def gate_slot(n, r):
                pe.wait_ge(w_lo, n + 1)
                for k in range(DK):
                    c = slice(P * k, P * k + P)
                    last = three(ps[:, r, :], gu_h[:, r, c], gu_l[:, r, c], ht_h[:, k, :], ht_l[:, k, :],
                                 k == 0, k == DK - 1)
                last.then_inc(w_used, 1)

            with pe.Fori(0, B - 1) as b:
                attention(Stage(b, True))
            attention(Stage(B - 1, False))
            for bank in (4, 5, 6, 7):
                pe.wait_ge(bank_free[bank], bank_total(bank))
            pe.sem_inc(att_done, 1)

            def down_chunk(n, r, k_count, first, last_chunk):
                pe.wait_ge(w_lo, n + 1)
                pe.wait_ge(a_lo, k_count + 1)
                wh, wl = w_h[:, r, :], w_l[:, r, :]
                for tt in range(TT):
                    c = slice(P * tt, P * tt + P)
                    banks = (ps[:, 2 * tt, :], ps[:, 2 * tt + 1, :])
                    d = (slice(0, 512), slice(512, 1024))
                    for dh in range(2):
                        mm(banks[dh], a_h[:, r, c], wh[:, d[dh]], start=first, stop=False)
                        mm(banks[dh], a_h[:, r, c], wl[:, d[dh]], start=False, stop=False)
                    for dh in range(2):
                        last = mm(banks[dh], a_l[:, r, c], wh[:, d[dh]], start=False, stop=last_chunk)
                        if last_chunk and 2 * tt + dh < 7:
                            last.then_inc(down_full, 1)
                last.then_inc(w_used, 1)

            def mlp(blk, more):
                n0 = BASE_MLP + MLP_SLOTS * blk
                with pe.Fori(1, FT // 2) as i:
                    for s in range(2):
                        tile = FT * blk + 2 * i + s
                        pe.wait_ge(silu_ready, tile - 1)
                        gate_slot(n0 + 4 * i + 2 * s, 2 * s)
                        pe.wait_ge(act_ready, tile - 1)
                        gate_slot(n0 + 4 * i + 2 * s + 1, 2 * s + 1)
                pe.wait_ge(act_ready, FT * blk + FT)
                nd = n0 + 2 * FT
                down_chunk(nd, 0, FT * blk, True, False)
                down_chunk(nd + 1, 1, FT * blk + 1, False, False)
                with pe.Fori(1, FT // 2 - 1) as i:
                    for r in range(2):
                        down_chunk(nd + 2 * i + r, r, FT * blk + 2 * i + r, False, False)
                down_chunk(nd + FT - 2, 0, FT * blk + FT - 2, False, False)
                down_chunk(nd + FT - 1, 1, FT * blk + FT - 1, False, True)
                if more:
                    pe.wait_ge(ht_loaded, 32 * blk + 64)
                    for r in range(GATE_SLOTS):
                        pe.wait_ge(y_ready, 8 * blk + r + 1)
                        gate_slot(n0 + MLP_SLOTS + r, r)

            with pe.Fori(0, B - 1) as blk:
                mlp(blk, True)
            mlp(B - 1, False)


def kernel(**inputs):
    import numpy as np
    import concourse.bacc as bacc
    from concourse.bass_utils import run_bass_kernel_spmd as run

    g = {k: np.asarray(v) for k, v in inputs.items()}
    pad = FT * P - F
    gate, up = (np.pad(g[n], ((0, pad), (0, 0))).reshape(FT, P, DK, P).transpose(0, 3, 2, 1)
                for n in ("L0_ffn_W_gate", "L0_ffn_W_up"))
    gate_up = np.stack([gate, up], axis=1).reshape(2 * FT, P, W)
    down = np.pad(g["L0_ffn_W_down"], ((0, 0), (0, pad))).T.reshape(FT, P, D)
    arrays = {
        "x_in": g["L0_attn_x"],
        "c_in": g["L0_c"].T.reshape(DK, P, B).transpose(1, 0, 2),
        "w_mod": g["L0_wmod"].reshape(4, 2, P, MOD_CHUNKS, 512).transpose(3, 0, 2, 1, 4).reshape(4 * MOD_CHUNKS, P, W),
        "w_pairs": g["L0_attn_w_qkv"].reshape(3, PAIRS, P, DK, P).transpose(1, 0, 4, 3, 2).reshape(3 * PAIRS, P, W),
        "b_pairs": g["L0_attn_b_qkv"].reshape(3, PAIRS, P).transpose(2, 1, 0).reshape(P, 3 * PAIRS),
        "w_o": g["L0_attn_w_o"].reshape(4, 256, PAIRS, P).transpose(0, 3, 2, 1).reshape(4, P, W),
        "b_o": g["L0_attn_b_o"],
        "w_mlp": np.concatenate([gate_up, down], axis=0),
    }
    arrays = {k: np.ascontiguousarray(v) for k, v in arrays.items()}
    nc = bacc.Bacc("TRN2", target_bir_lowering=False, num_devices=1)
    args = [nc.dram_tensor(k, a.shape, F32, kind="ExternalInput").ap() for k, a in arrays.items()]
    y = nc.dram_tensor("y_out", (B, S, D), F32, kind="ExternalOutput").ap()
    mlp_block(nc, *args, y)
    r = run(nc, [arrays], core_ids=[0])
    return r.results[0]["y_out"]
```

```python
from contextlib import ExitStack

import concourse.bass as bass
from concourse import mybir

F32 = mybir.dt.float32
F32R = mybir.dt.float32r
I32 = mybir.dt.int32
U32 = mybir.dt.uint32
ALU = mybir.AluOpType
ACT = mybir.ActivationFunctionType
AX = mybir.AxisListType

P = 128
B, S, D = 4, 512, 1024
PART = 512
HEADS, HD = 8, 64
PAIRS = HEADS // 2
F = 2752
FT = -(-F // P)
DK = D // P
TT = S // P
NEG = -10000.0
EPS = 1e-5
W = 1024
RAW, SPLIT, PRO_SPLIT = 4, 2, 4
GATE_SLOTS = 4
MOD_CHUNKS = 6 * D // 512
GATES = {4: (0, 0), 5: (0, 1), 10: (1, 0), 11: (1, 1)}

PRO = ([("mod", n) for n in range(4)] + [("t1", 0), ("mod", 4), ("t1", 1), ("t1", 2), ("mod", 5), ("t1", 3), ("mod", 6),
       ("q", 0), ("mod", 7), ("k", 0), ("mod", 8), ("v", 0), ("mod", 9), ("q", 1), ("mod", 10), ("k", 1), ("mod", 11)])
MOD_T = {1: (0,), 2: (1,), 3: (2, 3), 7: (6,), 8: (7,), 9: (8,), 10: (9,)}
PRO_SLOTS = []
for kind, n in PRO:
    if kind == "mod":
        PRO_SLOTS += [("mod", 4 * n + q) for q in range(4)]
    elif kind != "t1":
        PRO_SLOTS.append((kind, n))
BODY_SLOTS = [("v", 1), ("q", 2), ("k", 2), ("v", 2), ("q", 3), ("k", 3), ("v", 3),
              ("q", 0), ("k", 0), ("v", 0), ("o", 0), ("o", 1), ("o", 2), ("o", 3), ("q", 1), ("k", 1)]
OWN = 7
NEXT = 3
LAST_SLOTS = BODY_SLOTS[:OWN] + BODY_SLOTS[OWN + NEXT:OWN + NEXT + 4]
FILLS = {0: [0], 1: [1], 2: [2, 3], 3: [4, 5], 4: [6], 7: [7], 8: [8], 9: [9]}
T1_STEPS = {5: (0, 1), 6: (2, 3)}
VT_STEPS, VS_STEPS = {1: 1, 3: 2, 5: 3}, {2: 1, 4: 2, 6: 3}
BASE_BODY = len(PRO_SLOTS)
BASE_LAST = BASE_BODY + (B - 1) * len(BODY_SLOTS)
BASE_MLP = BASE_LAST + len(LAST_SLOTS)
HALF = P // 2
GU_SLOTS = 2 * FT - 1
MLP_SLOTS = GU_SLOTS + FT
assert F == (FT - 1) * P + HALF
assert len(BODY_SLOTS) % RAW == 0 and BASE_MLP % RAW == 0 and GATE_SLOTS == RAW and FT % 2 == 0

STRIP = {3: 0, 2: 512, 0: 896, 1: 1024}
STRIPS = 1280
KEYS = {0: 0, 3: 640, 1: 768, 2: 1152}
ZERO = 512
PT = 1408
TP_UNITS = [(0, [(i, 0) for i in range(4)]), (640, [(3, 3), (1, 1), (2, 1), (3, 1)]), (1152, [(2, 2), (3, 2)])]


DOWN_ORDER = (2, 3, 0, 1)
DOWN_UNITS = [(tt, dh) for tt in DOWN_ORDER for dh in range(2)]

FILL_BANK = {("v", 1): 6, ("q", 2): 7, ("k", 2): 6, ("v", 2): 7, ("q", 3): 6, ("k", 3): 7, ("v", 3): 6,
             ("q", 0): 7, ("k", 0): 6, ("v", 0): 7, ("q", 1): 6, ("k", 1): 7}
VT_BANK = {1: 6, 2: 6, 3: 6}


def body_fills(s, has_next):
    fills = [j for j in FILLS.get(s, []) if j < OWN or has_next]
    return (fills, []) if s == 1 else (fills[:-1], fills[-1:])


def body_evacs(s, has_next):
    early, late = body_fills(s, has_next)
    return ([], early) if s == 1 else (early, late)


def step_uses(s, has_next):
    out = []
    early, late = ([(FILL_BANK[BODY_SLOTS[j]], BODY_SLOTS[j]) for j in part] for part in body_fills(s, has_next))
    if s in T1_STEPS and has_next:
        out += [(7 - kh, ("t1", T1_STEPS[s][0], kh)) for kh in range(2)]
    out += early
    if 2 <= s <= 9:
        out.append((5, ("pv", s - 2)))
    if 1 <= s <= 8:
        out += [(3, ("tp", s - 1, 0)), (4, ("tp", s - 1, 1))]
    out += late
    if s in T1_STEPS and has_next:
        out += [(7 - kh, ("t1", T1_STEPS[s][1], kh)) for kh in range(2)]
    if 1 <= s <= 8:
        free = not has_next and s >= 5
        out += [(7 if free else 5, ("tp", s - 1, 2)), (6 if free else 3, ("tail", s - 1))]
    if s in VT_STEPS:
        out.append((VT_BANK[VT_STEPS[s]], ("vt", VT_STEPS[s])))
    if s in VS_STEPS:
        out.append((4, ("vs", VS_STEPS[s])))
    return out


def stage_uses(has_next):
    out = [u for s in range(10) for u in step_uses(s, has_next)]
    for j in range(4):
        out += [(3, ("o", j, 0)), (4, ("o", j, 1))]
        if has_next and j == 0:
            out.append((6, ("vt", 0)))
        if has_next and j == 1:
            out.append((5, ("vs", 0)))
    if has_next:
        out += [(FILL_BANK[kind, 1], (kind, 1)) for kind in "qk"]
    t2_bank = 3 if has_next else 6
    out += [(t2_bank + kh, ("t2", tt, kh)) for tt in range(TT) for kh in range(2)]
    return out


def prologue_uses():
    out = []
    for kind, n in PRO:
        if kind == "mod":
            out.append((3 + n % 2, ("mod", n)))
            out += [(5, ("mt", m)) for m in MOD_T.get(n, ())]
            if n == 9:
                out.append((6, ("vt", 0)))
            if n == 10:
                out.append((7, ("vs", 0)))
        elif kind == "t1":
            out += [(6 + kh, ("t1", n, kh)) for kh in range(2)]
        else:
            out.append((FILL_BANK[kind, n], (kind, n)))
    return out


def filled_by(label):
    if label[0] in ("q", "k", "v", "mod") or (label[0] == "o" and label[2] == 1):
        return "w_used"
    return "xn_used" if label[0] in ("t1", "t2") and label[2] == 1 else "bank_full"


def number(uses):
    seen, full, at = {}, {}, {}
    for bank, label in uses:
        at[label] = (bank, seen.get(bank, 0), full.get(bank, 0))
        seen[bank] = seen.get(bank, 0) + 1
        full[bank] = full.get(bank, 0) + (filled_by(label) == "bank_full")
    return at, seen, full


PRO_AT, PRO_N, PRO_FULL = number(prologue_uses())
BODY_AT, BODY_N, BODY_FULL = number(stage_uses(True))
LAST_AT, LAST_N, LAST_FULL = number(stage_uses(False))


class Stage:

    def __init__(self, b, has_next):
        self.b, self.next = b, has_next
        self.at = BODY_AT if has_next else LAST_AT
        self.slots = BODY_SLOTS if has_next else LAST_SLOTS
        self.base = BASE_BODY + len(BODY_SLOTS) * b
        self.x_t1 = 4 + 8 * b
        self.x_t2 = self.x_t1 + (4 if has_next else 0)

    def use(self, *label):
        bank, n, _ = self.at[label]
        return bank, PRO_N.get(bank, 0) + BODY_N.get(bank, 0) * self.b + n

    def made(self, *label):
        bank, n = self.use(*label)
        return bank, n + 1

    def pair(self, p, ahead=0):
        return PAIRS * self.b + PAIRS * ahead + p

    def before(self, bank):
        return PRO_N.get(bank, 0) + BODY_N.get(bank, 0) * self.b

    def filled(self, *label):
        bank, _, n = self.at[label]
        how = filled_by(label)
        if how == "w_used":
            slot = ("o", label[1]) if label[0] == "o" else label
            return how, self.base + self.slots.index(slot) + 1
        if how == "xn_used":
            return how, (self.x_t1 if label[0] == "t1" else self.x_t2) + label[1] + 1
        return bank, PRO_FULL.get(bank, 0) + BODY_FULL.get(bank, 0) * self.b + n + 1


class Prologue:
    b, next, x_t1 = 0, True, 0

    def use(self, *label):
        return PRO_AT[label][:2]

    def made(self, *label):
        bank, n, _ = PRO_AT[label]
        return bank, n + 1

    def pair(self, p, ahead=0):
        return p

    def filled(self, *label):
        bank, _, n = PRO_AT[label]
        how = filled_by(label)
        if how == "w_used":
            slot = ("mod", 4 * label[1] + 3) if label[0] == "mod" else label
            return how, PRO_SLOTS.index(slot) + 1
        return (how, label[1] + 1) if how == "xn_used" else (bank, n + 1)


def mlp_block(nc, x, c_t, w_mod, w_pairs, b_pairs, w_out, b_out, w_mlp, out):
    ctx = ExitStack()
    with ctx:
        attention_only = ExitStack()

        def sb(name, shape, dt=F32, where=ctx):
            return where.enter_context(nc.sbuf_tensor(name, shape, dt))

        def att(name, shape, dt=F32):
            return sb(name, shape, dt, attention_only)

        def sem(name):
            return ctx.enter_context(nc.semaphore(name))

        gate_rows = nc.dram_tensor("gate_rows", (2, B, D), F32, kind="Internal").ap()
        x1_dram = nc.dram_tensor("x1_dram", (B, P, TT, D), F32, kind="Internal").ap()
        h2_dram = nc.dram_tensor("h2_dram", (B, 2, P, DK, S), F32R, kind="Internal").ap()

        raw = sb("raw", [P, RAW, W])
        w_h = sb("w_h", [P, SPLIT, W], F32R)
        w_l = sb("w_l", [P, SPLIT, W], F32R)
        ht_h = sb("ht_h", [P, DK, S], F32R)
        ht_l = sb("ht_l", [P, DK, S], F32R)

        q_st = att("q_st", [P, 2, 2, S], F32R)
        k_h = att("k_h", [P, 2, 2, S], F32R)
        k_l = att("k_l", [P, 2, 2, S], F32R)
        v_h = att("v_h", [P, 2, TT, P], F32R)
        v_l = att("v_l", [P, 2, TT, P], F32R)
        probs = att("probs", [P, 2, STRIPS])
        pt_h = att("pt_h", [P, PT], F32R)
        pt_l = att("pt_l", [P, PT], F32R)
        v_tail_h = att("v_tail_h", [2 * TT, 2, P], F32R)
        v_tail_l = att("v_tail_l", [2 * TT, 2, P], F32R)
        tail_rows = att("tail_rows", [2 * TT, S], F32R)
        v_col = att("v_col", [P, S])
        vt_h = att("vt_h", [P, PAIRS, S], F32R)
        vt_l = att("vt_l", [P, PAIRS, S], F32R)
        x_next = att("x_next", [P, TT, D])
        x_cur = att("x_cur", [P, TT, D])
        xn = att("xn", [P, 2, D])
        h_tmp = att("h_tmp", [P, 2, S])
        ga_row = att("ga_row", [P, D])
        bo_row = att("bo_row", [P, D])
        o_tmp = att("o_tmp", [P, 2, 2, 256])
        bo_ga = h_tmp.rearrange("p k t -> p (k t)")
        mod_t = att("mod_t", [P, MOD_CHUNKS * 4, B])
        mod_a = att("mod_a", [P, 2 * DK])
        mod_b = att("mod_b", [P, 2 * DK])
        bias = att("bias", [P, 3 * PAIRS])
        c_sb = att("c_sb", [P, DK, B])
        c_act = att("c_act", [P, DK, B])
        ident = att("ident", [P, P])
        behind = att("behind", [P, TT, 2 * TT], F32R)
        masked = att("masked", [P, P])
        neg_fill = att("neg_fill", [P, P])
        neg_col = att("neg_col", [P, 1])
        n_tail = att("n_tail", [P, TT])
        neg_m = att("neg_m", [P, 4, TT])
        tail_e = att("tail_e", [P, 4, TT])
        sums = att("sums", [P, 4, TT])
        den = att("den", [P, 4, TT])
        r_den = att("r_den", [P, 4, TT])
        tail_w = att("tail_w", [P, TT])
        tail_parts = att("tail_parts", [P, 2, 2 * TT * TT], F32R)
        stats = att("stats", [P, TT, 4, 6])
        mv = att("mv", [P, TT, 2])
        ve = att("ve", [P, TT])
        rs = att("rs", [P, 2, TT])
        rt = att("rt", [P, TT])
        c_st = [pt_h[:, o:o + 512].rearrange("p (k m) -> p k m", k=4) for o in (0, 640)]
        mod_lo = probs[0:B, 0, 0:1024].rearrange("p (n c) -> p n c", n=2)
        mod_row = probs[0:B, 1, 0:1024].rearrange("p (n c) -> p n c", n=2)
        gate_row = x_cur[0:B, 0, :].rearrange("p (n c) -> p n c", n=2)
        gate_row2 = x_cur[0:B, 1, :].rearrange("p (n c) -> p n c", n=2)
        gate_sgn = x_cur[0:B, 2, 0:512]
        gate_abs = x_cur[0:B, 2, 512:1024]

        attention_only.close()
        gu_h = sb("gu_h", [P, GATE_SLOTS, W], F32R)
        gu_l = sb("gu_l", [P, GATE_SLOTS, W], F32R)
        silu = sb("silu", [P, 2, S])
        act = sb("act", [P, FT, S])
        raw_down = sb("raw_down", [P, 2, W])
        a_h = sb("a_h", [P, 2, S], F32R)
        a_l = sb("a_l", [P, 2, S], F32R)
        gb_row = sb("gb_row", [P, D])
        x1_sb = sb("x1_sb", [P, TT, D])
        y_sb = sb("y_sb", [P, 4, S])

        ps = ctx.enter_context(nc.psum_tensor("ps", [P, 8, 512], F32))
        scores = ps[:, 0:3, :].rearrange("p b c -> p (b c)")

        w_loaded = [sem(f"w_loaded{i}") for i in range(RAW)]
        down_loaded = [sem(f"down_loaded{i}") for i in range(2)]
        w_hi, w_lo, w_used = sem("w_hi"), sem("w_lo"), sem("w_used")
        bias_loaded, bo_loaded = sem("bias_loaded"), sem("bo_loaded")
        c_loaded = sem("c_loaded")
        c_silu, c_ready = sem("c_silu"), sem("c_ready")
        consts = sem("consts")
        pool_consts = sem("pool_consts")
        bank_full = {k: sem(f"bank_full{k}") for k in range(3, 8)}
        bank_free = {k: sem(f"bank_free{k}") for k in range(3, 8)}
        scores_full, scores_free = sem("scores_full"), sem("scores_free")
        mod_lo_ready, mod_picked = sem("mod_lo_ready"), sem("mod_picked")
        gate_ready, gate_stored = sem("gate_ready"), sem("gate_stored")
        x0_loaded, x_loaded, xc_loaded, ga_loaded = sem("x0_loaded"), sem("x_loaded"), sem("xc_loaded"), sem("ga_loaded")
        xn_ready, xn_used = sem("xn_ready"), sem("xn_used")
        t_hi, t_lo = sem("t_hi"), sem("t_lo")
        q_hi, k_hi, v_hi = sem("q_hi"), sem("k_hi"), sem("v_hi")
        negm_ready, exp_done = sem("negm_ready"), sem("exp_done")
        probs_ready, tail_ready = sem("probs_ready"), sem("tail_ready")
        pt_hi, tail_hi, o_hi = sem("pt_hi"), sem("tail_hi"), sem("o_hi")
        x_biased = sem("x_biased")
        x1_ready, x1_stored = sem("x1_ready"), sem("x1_stored")
        h2_stored = [sem(f"h2_stored{i}") for i in range(4)]
        stage_clear = sem("stage_clear")
        ht_loaded, ht_free = sem("ht_loaded"), sem("ht_free")
        silu_ready, act_ready = sem("silu_ready"), sem("act_ready")
        a_hi, a_lo = sem("a_hi"), sem("a_lo")
        down_full = sem("down_full")
        mlp_loaded = sem("mlp_loaded")
        y_ready, y_added, out_stored = sem("y_ready"), sem("y_added"), sem("out_stored")
        att_done = sem("att_done")
        waited = {e: sem(f"waited_{e}") for e in ("pool", "dve", "pe")}

        def split_slot(static_n):
            r = static_n % (PRO_SPLIT if static_n < BASE_BODY else SPLIT)
            if r < SPLIT:
                return w_h[:, r, :], w_l[:, r, :]
            two = slice(2 * (r - SPLIT), 2 * (r - SPLIT) + 2)
            return tuple(t[:, two, :].rearrange("p a t -> p (a t)") for t in (vt_h, vt_l))

        def hold(engine, name):
            engine.sem_inc(waited[name], 1)

        def filled(engine, st, *label):
            how, value = st.filled(*label)
            engine.wait_ge({"w_used": w_used, "xn_used": xn_used}[how] if isinstance(how, str) else bank_full[how], value)
            return st.use(*label)[0]

        def made(engine, st, *label):
            bank, count = st.made(*label)
            engine.wait_ge(bank_free[bank], count)

        block = ctx.enter_context(nc.Block())

        @block.sync
        def _(sp):
            def load(n, static_n, src):
                if not isinstance(n, int) or n >= RAW:
                    sp.wait_ge(w_lo, n - RAW + 1)
                sp.dma_start(raw[:, static_n % RAW, :], src).then_inc(w_loaded[static_n % RAW], 16)

            def source(kind, i):
                return {"mod": w_mod, "o": w_out}[kind][i] if kind in ("mod", "o") else w_pairs[3 * i + "qkv".index(kind)]

            sp.dma_start(c_sb[:], c_t).then_inc(c_loaded, 16)
            sp.dma_start(bias[:], b_pairs).then_inc(bias_loaded, 16)
            for n, (kind, i) in enumerate(PRO_SLOTS):
                load(n, n, source(kind, i))
                if n == 3:
                    sp.dma_start(x_next[:], x[0].rearrange("(t p) d -> p t d", p=P)).then_inc(x0_loaded, 16)
                    sp.dma_start(bo_row[:], b_out.partition_broadcast(P)).then_inc(bo_loaded, 16)
            def store_h2(st, units):
                for u in units:
                    tt, kh = divmod(u, 2)
                    sp.wait_ge(t_lo, 2 * (st.x_t2 + tt) + kh + 1)
                    for hl, stage in ((0, vt_h), (1, vt_l)):
                        sp.dma_start(h2_dram[st.b][hl][:, 4 * kh:4 * kh + 4, P * tt:P * tt + P].bitcast(F32),
                                     stage[:, u % 4, :].rearrange("p (k t) -> p k t", k=4).bitcast(F32)
                                     ).then_inc(h2_stored[u % 4], 16)

            for j in range(RAW):
                load(BASE_BODY + j, BASE_BODY + j, source(*BODY_SLOTS[j]))
            with sp.Fori(0, B - 1) as b:
                st = Stage(b, True)
                for j in range(RAW, len(BODY_SLOTS) + RAW):
                    load(st.base + j, BASE_BODY + j, source(*BODY_SLOTS[j % len(BODY_SLOTS)]))
                store_h2(st, range(2 * TT))
            for j in range(RAW, len(LAST_SLOTS)):
                load(BASE_LAST + j, BASE_LAST + j, source(*LAST_SLOTS[j]))

            def load_gate(blk, i, r):
                sp.wait_ge(w_lo, BASE_MLP + MLP_SLOTS * blk + 4 * i + r - RAW + 1)
                sp.dma_start(raw[:, r, :], w_mlp[i * 4 + r]).then_inc(w_loaded[r], 16)

            def load_down(blk):
                with sp.Fori(0, FT // 2) as i:
                    for r in range(2):
                        n = BASE_MLP + MLP_SLOTS * blk + GU_SLOTS + 2 * i + r
                        sp.wait_ge(w_lo, n - 1)
                        sp.dma_start(raw_down[:, r, :], w_mlp[i * 2 + r + GU_SLOTS]).then_inc(down_loaded[r], 16)

            last = Stage(B - 1, False)
            for r in range(GATE_SLOTS):
                load_gate(0, 0, r)
            store_h2(last, (0, 1))
            load_gate(0, 1, 0)
            load_gate(0, 1, 1)
            store_h2(last, range(2, 2 * TT))
            load_gate(0, 1, 2)
            load_gate(0, 1, 3)

            with sp.Fori(2, FT // 2 - 1) as i:
                for r in range(GATE_SLOTS):
                    load_gate(0, i, r)
            for r in range(3):
                load_gate(0, FT // 2 - 1, r)
            sp.wait_ge(att_done, 4)
            load_down(0)
            with sp.Fori(1, B) as blk:
                with sp.Fori(0, FT // 2 - 1) as i:
                    for r in range(GATE_SLOTS):
                        load_gate(blk, i, r)
                for r in range(3):
                    load_gate(blk, FT // 2 - 1, r)
                load_down(blk)

        @block.gpsimd
        def _(pool):
            pool.sem_inc(stage_clear, 1)
            nc.gpsimd.memset(ident[:], 0.0).then_inc(pool_consts, 1)
            nc.gpsimd.memset(masked[:], 0.0).then_inc(pool_consts, 1)
            pool.wait_ge(pool_consts, 2)
            nc.gpsimd.affine_select(out=ident[:], in_=ident[:], compare_op=ALU.not_equal, fill=1.0, base=0,
                                    pattern=[[-1, P]], channel_multiplier=1).then_inc(consts, 1)
            nc.gpsimd.affine_select(out=masked[:], in_=masked[:], compare_op=ALU.is_ge, fill=1.0, base=0,
                                    pattern=[[-1, P]], channel_multiplier=1).then_inc(consts, 1)

            def t_unit_lo(u_count, dst, tmp, hi):
                pool.wait_ge(t_hi, u_count + 1)
                nc.gpsimd.tensor_tensor(dst, tmp, hi.bitcast(F32), ALU.subtract).then_inc(t_lo, 1)

            def weight_lo(n, static_n):
                pool.wait_ge(w_hi, n + 1)
                pool.wait_ge(w_lo, n)
                hi, lo = split_slot(static_n)
                nc.gpsimd.tensor_tensor(lo, raw[:, static_n % RAW, :], hi.bitcast(F32), ALU.subtract).then_inc(w_lo, 1)

            def t1_units(x0, tiles=range(TT)):
                for tt in tiles:
                    for kh in range(2):
                        sl = (slice(None), slice(4 * kh, 4 * kh + 4), slice(P * tt, P * tt + P))
                        tmp = h_tmp[:, kh, :].rearrange("p (k t) -> p k t", k=4)
                        t_unit_lo(2 * (x0 + tt) + kh, ht_l[sl], tmp, ht_h[sl])

            t1_units(0)
            for i, n in enumerate(sorted(GATES)):
                which, half = GATES[n]
                pool.wait_ge(gate_ready, i + 1)
                src = (gate_row if which == 0 else gate_row2)[:, half, :]
                pool.dma_start(gate_rows[which][:, 512 * half:512 * half + 512], src).then_inc(gate_stored, 16)
            pool.wait_ge(gate_stored, 64)

            def attention(st):
                b = st.b
                pool.wait_ge(xn_ready, 8 * b + 4)
                hold(pool, "pool")
                if st.next:
                    pool.dma_start(x_next[:], x[b + 1].rearrange("(t p) d -> p t d", p=P)).then_inc(x_loaded, 16)
                pool.dma_start(x_cur[:], x[b].rearrange("(t p) d -> p t d", p=P)).then_inc(xc_loaded, 16)
                pool.dma_start(ga_row[:], gate_rows[0][b].partition_broadcast(P)).then_inc(ga_loaded, 16)
                for s in range(10):
                    if s in T1_STEPS and st.next:
                        t1_units(st.x_t1, T1_STEPS[s][:1])
                    early, late = body_fills(s, st.next)
                    for j in early:
                        weight_lo(st.base + j + 2, BASE_BODY + j + 2)
                    if s == 1:
                        pool.wait_ge(bo_loaded, 16)
                        pool.wait_ge(ga_loaded, 16 * b + 16)
                        nc.gpsimd.tensor_tensor(bo_ga, bo_row[:], ga_row[:], ALU.mult).then_inc(x_biased, 1)
                        pool.wait_ge(xc_loaded, 16 * b + 16)
                        pool.wait_ge(x_biased, 5 * b + 1)
                        hold(pool, "pool")
                    if s in (1, 2, 3, 4):
                        nc.gpsimd.tensor_tensor(x_cur[:, s - 1, :], x_cur[:, s - 1, :], bo_ga, ALU.add).then_inc(x_biased, 1)
                    if s in T1_STEPS and st.next:
                        t1_units(st.x_t1, T1_STEPS[s][1:])
                    for j in late:
                        weight_lo(st.base + j + 2, BASE_BODY + j + 2)
                    if s == 5 and not st.next:
                        pool.wait_ge(w_used, BASE_LAST + OWN)
                        load_h2(0)
                pool.wait_ge(x1_ready, b + 1)
                hold(pool, "pool")
                pool.dma_start(x1_dram[b], x_cur[:]).then_inc(x1_stored, 16)
                for s in range(4):
                    pool.wait_ge(h2_stored[s], 64 * b + 64)
                pool.wait_ge(x1_stored, 16 * b + 16)
                hold(pool, "pool")
                nc.gpsimd.drain().then_inc(stage_clear, 1)

            def load_h2(blk):
                pool.dma_start(ht_h[:], h2_dram[blk][0]).then_inc(ht_loaded, 16)
                pool.dma_start(ht_l[:], h2_dram[blk][1]).then_inc(ht_loaded, 16)

            with pool.Fori(0, B - 1) as b:
                attention(Stage(b, True))
            attention(Stage(B - 1, False))

            pool.sem_inc(att_done, 1)
            pool.wait_ge(att_done, 4)

            def mlp(blk, more):
                n0 = BASE_MLP + MLP_SLOTS * blk
                pool.dma_start(x1_sb[:], x1_dram[blk]).then_inc(mlp_loaded, 16)
                pool.dma_start(gb_row[:], gate_rows[1][blk].partition_broadcast(P)).then_inc(mlp_loaded, 16)
                if more:
                    pool.wait_ge(w_used, n0 + GU_SLOTS)
                    hold(pool, "pool")
                    load_h2(blk + 1)
                for u in range(2 * TT):
                    tt, dh = DOWN_UNITS[u]
                    xs = x1_sb[:, tt, 512 * dh:512 * dh + 512]
                    if u == 0:
                        pool.wait_ge(mlp_loaded, 32 * blk + 32)
                    pool.wait_ge(y_ready, 8 * blk + u + 1)
                    nc.gpsimd.tensor_tensor(xs, xs, y_sb[:, u % 4, :], ALU.add).then_inc(y_added, 1)
                    pool.wait_ge(y_added, 8 * blk + u + 1)
                    hold(pool, "pool")
                    pool.dma_start(out[blk][P * tt:P * tt + P, 512 * dh:512 * dh + 512], xs).then_inc(out_stored, 16)
                pool.wait_ge(out_stored, 128 * blk + 128)
                hold(pool, "pool")

            with pool.Fori(0, B - 1) as blk:
                mlp(blk, True)
            mlp(B - 1, False)

        @block.scalar
        def _(act_e):
            A, COPY = nc.scalar.activation, nc.scalar.copy

            def weight_hi(n, static_n):
                act_e.wait_ge(w_loaded[static_n % RAW], 16 * (n // RAW + 1) if isinstance(n, int)
                              else (16 * (static_n // RAW + 1) + (n - static_n) * (16 // RAW)))
                hi, _ = split_slot(static_n)
                depth = PRO_SPLIT if static_n < BASE_BODY else SPLIT
                if not isinstance(n, int) or n >= depth:
                    act_e.wait_ge(w_used, n - depth + 1)
                COPY(hi, raw[:, static_n % RAW, :]).then_inc(w_hi, 1)

            def t_units(st, name, x0, mod, picked, tiles=range(TT)):
                act_e.wait_ge(mod_picked, picked)
                if st is not pro:
                    act_e.wait_ge(x_biased, 5 * st.b + 5)
                for tt in tiles:
                    for kh in range(2):
                        bank = filled(act_e, st, name, tt, kh)
                        count = 2 * (x0 + tt) + kh
                        if not isinstance(count, int) or count >= 2:
                            act_e.wait_ge(t_lo, count - 1)
                        for k in range(4):
                            last = A(h_tmp[:, kh, P * k:P * k + P], ps[:, bank, P * k:P * k + P], ACT.Identity,
                                     bias=mod[:, 4 * kh + k:4 * kh + k + 1],
                                     scale=mod[:, DK + 4 * kh + k:DK + 4 * kh + k + 1])
                        last.then_inc(bank_free[bank], 1)

            def q_evac(st, p):
                bank = filled(act_e, st, "q", p)
                col = bias[:, 3 * p:3 * p + 1]
                A(q_st[0:64, p % 2, 0, :], ps[0:64, bank, :], ACT.Identity, bias=col[0:64])
                A(q_st[64:128, p % 2, 1, :], ps[64:128, bank, :], ACT.Identity, bias=col[64:128]).then_inc(q_hi, 1)

            def k_evac(st, p):
                bank = filled(act_e, st, "k", p)
                col = bias[:, 3 * p + 1:3 * p + 2]
                for hd in range(2):
                    rows = slice(64 * hd, 64 * hd + 64)
                    for half in (0, 64):
                        last = A(k_h[half:half + 64, p % 2, hd, :], ps[rows, bank, :], ACT.Identity, bias=col[rows])
                last.then_inc(k_hi, 1)

            def v_evac(st, p):
                bank = filled(act_e, st, "v", p)
                A(v_col[:], ps[:, bank, :], ACT.Identity, bias=bias[:, 3 * p + 2:3 * p + 3]).then_inc(bank_free[bank], 1)

            def vt_evac(st, p):
                bank = filled(act_e, st, "vt", p)
                COPY(v_h[:, p % 2].rearrange("p t c -> p (t c)"), ps[:, bank, :]).then_inc(v_hi, 1)

            def vs_evac(st, p):
                bank = filled(act_e, st, "vs", p)
                COPY(v_tail_h[:, p % 2, :], ps[0:2 * TT, bank, 0:P]).then_inc(tail_hi, 1)

            def pv_evac(st, h):
                rows = slice(HD * (h % 2), HD * (h % 2) + HD)
                bank = filled(act_e, st, "pv", h)
                COPY(vt_h[rows, h // 2, :], ps[rows, bank, :]).then_inc(o_hi, 1)

            def tail_evac(st, h):
                bank = filled(act_e, st, "tail", h)
                COPY(tail_rows[:], ps[0:2 * TT, bank, :]).then_inc(bank_free[bank], 1)

            def tp_evac(st, h, u):
                bank = filled(act_e, st, "tp", h, u)
                o, blocks = TP_UNITS[u]
                n = P * len(blocks)
                COPY(pt_h[:, o:o + n], ps[:, bank, 0:n]).then_inc(pt_hi, 1)

            def softmax(st, h):
                g = 8 * st.b + h
                act_e.wait_ge(negm_ready, g + 1)
                par = h % 4
                for i in (3, 2, 0, 1):
                    o, n = STRIP[i], P * (i + 1)
                    last = A(probs[:, h % 2, o:o + n], scores[:, o:o + n], ACT.Exp, bias=neg_m[:, par, i:i + 1],
                             accum_out=sums[:, par, i:i + 1])
                last.then_inc(scores_free, 1)
                A(tail_e[:, par, 0:3], neg_m[:, par, 0:3], ACT.Exp, bias=neg_col[:]).then_inc(exp_done, 1)

            EVAC = {"q": q_evac, "k": k_evac, "v": v_evac}

            act_e.sem_inc(scores_free, 1)
            act_e.wait_ge(c_loaded, 16)
            A(c_act[:], c_sb[:], ACT.Silu).then_inc(c_silu, 1)
            pro = Prologue()

            def pro_evac(kind, n):
                if kind == "mod":
                    bank = filled(act_e, pro, "mod", n)
                    if n >= 2:
                        made(act_e, pro, "mod", n - 2)
                    COPY(mod_lo[:, n % 2, :], ps[32:32 + B, bank, :]).then_inc(mod_lo_ready, 1)
                    if n == 9:
                        vt_evac(pro, 0)
                    if n == 10:
                        vs_evac(pro, 0)
                elif kind == "t1":
                    t_units(pro, "t1", 0, mod_a, 1, (n,))
                else:
                    if (kind, n) == ("q", 0):
                        act_e.wait_ge(bias_loaded, 16)
                    EVAC[kind](pro, n)

            n = 0
            for idx, (kind, i) in enumerate(PRO):
                for _ in range({"mod": 4, "t1": 0}.get(kind, 1)):
                    weight_hi(n, n)
                    n += 1
                if idx:
                    pro_evac(*PRO[idx - 1])
            pro_evac(*PRO[-1])
            for n in (BASE_BODY, BASE_BODY + 1):
                weight_hi(n, n)
            act_e.wait_ge(gate_stored, 64)
            act_e.wait_ge(mod_picked, 1)

            def gate_hi(n, r, blk, i):
                per_block = FT // 2 - (r == 3)
                act_e.wait_ge(w_loaded[r], 16 * (BASE_MLP // RAW + per_block * blk + i + 1))
                COPY(gu_h[:, r, :], raw[:, r, :]).then_inc(w_hi, 1)

            def gate_hi_first(blk, used):
                act_e.wait_ge(w_used, used)
                for r in range(GATE_SLOTS):
                    gate_hi(BASE_MLP + MLP_SLOTS * blk + r, r, blk, 0)

            def attention(st):
                def fill_evac(j):
                    EVAC[BODY_SLOTS[j][0]](st, BODY_SLOTS[j][1])
                    weight_hi(st.base + j + 2, BASE_BODY + j + 2)

                for s in range(10):
                    early, late = body_evacs(s, st.next)
                    if s in T1_STEPS and st.next:
                        t_units(st, "t1", st.x_t1, mod_a, 2 * st.b + 2, T1_STEPS[s][:1])
                    if s < 8:
                        softmax(st, s)
                    for j in early:
                        fill_evac(j)
                    if 2 <= s <= 9:
                        if s == 2:
                            act_e.wait_ge(stage_clear, st.b + 1)
                        pv_evac(st, s - 2)
                    if 1 <= s <= 8:
                        tp_evac(st, s - 1, 0)
                        tp_evac(st, s - 1, 1)
                    if s in T1_STEPS and st.next:
                        t_units(st, "t1", st.x_t1, mod_a, 2 * st.b + 2, T1_STEPS[s][1:])
                    if 1 <= s <= 8:
                        tp_evac(st, s - 1, 2)
                        tail_evac(st, s - 1)
                    if s in VT_STEPS:
                        vt_evac(st, VT_STEPS[s])
                    if s in VS_STEPS:
                        vs_evac(st, VS_STEPS[s])
                    for j in late:
                        fill_evac(j)
                o0 = st.slots.index(("o", 0))
                for j in range(4):
                    if st.next or j < 2:
                        weight_hi(st.base + o0 + j + 2, BASE_BODY + o0 + j + 2)
                    if j == 1 and not st.next:
                        gate_hi_first(0, BASE_MLP - RAW + 1)
                    if j == 0 and st.next:
                        vt_evac(st, 0)
                    if j == 1 and st.next:
                        vs_evac(st, 0)
                if st.next:
                    q_evac(st, 1)
                    weight_hi(st.base + 16, BASE_BODY + 16)
                    t_units(st, "t2", st.x_t2, mod_b, 2 * st.b + 3)
                    weight_hi(st.base + 17, BASE_BODY + 17)
                    k_evac(st, 1)
                else:
                    t_units(st, "t2", st.x_t2, mod_b, 2 * st.b + 2, (0,))
                    first_tile(0)
                    t_units(st, "t2", st.x_t2, mod_b, 2 * st.b + 2, range(1, TT))

            def silu_tile(i, s, blk, first=False):
                n0 = BASE_MLP + MLP_SLOTS * blk
                act_e.wait_ge(w_used, n0 + 4 * i + 2 * s + 1)
                if not first:
                    act_e.wait_ge(act_ready, FT * blk + 2 * i + s - 1)
                A(silu[:, s, :], ps[:, 2 * s, :], ACT.Silu).then_inc(silu_ready, 1)

            def gate_tile(i, s, blk, first=False, slots=2):
                silu_tile(i, s, blk, first)
                for r in range(2 * s, 2 * s + slots):
                    n = BASE_MLP + MLP_SLOTS * blk + 4 * i + r
                    act_e.wait_ge(w_used, n + 1)
                    gate_hi(n + GATE_SLOTS, r, blk, i + 1)

            def first_tile(blk):
                gate_tile(0, 0, blk, True)

            with act_e.Fori(0, B - 1) as b:
                attention(Stage(b, True))
            attention(Stage(B - 1, False))
            act_e.sem_inc(att_done, 1)

            def down_hi(i, r, blk):
                n = BASE_MLP + MLP_SLOTS * blk + GU_SLOTS + 2 * i + r
                act_e.wait_ge(down_loaded[r], 16 * (FT // 2 * blk + i + 1))
                if not (isinstance(i, int) and i == 0):
                    act_e.wait_ge(w_used, n - 1)
                COPY(w_h[:, r, :], raw_down[:, r, :]).then_inc(w_hi, 1)

            def act_hi(i, r, blk):
                act_e.wait_ge(act_ready, FT * blk + 2 * i + r + 1)
                COPY(a_h[:, r, :], act[:, bass.ds(2 * i + r, 1), :].rearrange("p a t -> p (a t)")).then_inc(a_hi, 1)

            def mlp(blk, more):
                n0 = BASE_MLP + MLP_SLOTS * blk

                gate_tile(0, 1, blk, True)
                with act_e.Fori(1, FT // 2 - 2) as i:
                    for s in range(2):
                        gate_tile(i, s, blk)
                gate_tile(FT // 2 - 2, 0, blk)
                gate_tile(FT // 2 - 2, 1, blk, slots=1)
                for r in range(2):
                    act_e.wait_ge(att_done, 4)
                    act_hi(0, r, blk)
                for r in range(2):
                    down_hi(0, r, blk)
                silu_tile(FT // 2 - 1, 0, blk)
                act_e.wait_ge(w_used, n0 + GU_SLOTS)
                act_e.wait_ge(act_ready, FT * blk + FT - 2)
                A(silu[HALF:P, 1, :], ps[0:HALF, 2, :], ACT.Silu).then_inc(silu_ready, 1)
                with act_e.Fori(1, FT // 2 - 1) as i:
                    for r in range(2):
                        down_hi(i, r, blk)
                        act_hi(i, r, blk)
                down_hi(FT // 2 - 1, 0, blk)
                act_hi(FT // 2 - 1, 0, blk)
                down_hi(FT // 2 - 1, 1, blk)
                act_e.wait_ge(act_ready, FT * blk + FT)
                COPY(a_h[HALF:P, 1, :], act[HALF:P, FT - 1, :]).then_inc(a_hi, 1)
                if more:
                    gate_hi_first(blk + 1, n0 + GU_SLOTS)
                    first_tile(blk + 1)

            with act_e.Fori(0, B - 1) as blk:
                mlp(blk, True)
            mlp(B - 1, False)

        @block.vector
        def _(dve):
            V = nc.vector

            def weight_lo(n, static_n):
                dve.wait_ge(w_hi, n + 1)
                hi, lo = split_slot(static_n)
                V.tensor_tensor(lo, raw[:, static_n % RAW, :], hi.bitcast(F32), ALU.subtract).then_inc(w_lo, 1)

            def q_lo(st, p, ahead=0):
                bank, _ = st.use("q", p)
                dve.wait_ge(q_hi, st.pair(p, ahead) + 1)
                for hd in range(2):
                    rows, other = slice(64 * hd, 64 * hd + 64), slice(64 - 64 * hd, 128 - 64 * hd)
                    last = V.scalar_tensor_tensor(out=q_st[other, p % 2, hd, :], in0=ps[rows, bank, :],
                                                  scalar=bias[rows, 3 * p:3 * p + 1],
                                                  in1=q_st[rows, p % 2, hd, :].bitcast(F32),
                                                  op0=ALU.add, op1=ALU.subtract)
                last.then_inc(bank_free[bank], 1)

            def k_lo(st, p, ahead=0):
                bank = FILL_BANK["k", p]
                dve.wait_ge(k_hi, st.pair(p, ahead) + 1)
                for hd in range(2):
                    rows = slice(64 * hd, 64 * hd + 64)
                    for half in (0, 64):
                        last = V.scalar_tensor_tensor(out=k_l[half:half + 64, p % 2, hd, :], in0=ps[rows, bank, :],
                                                      scalar=bias[rows, 3 * p + 1:3 * p + 2],
                                                      in1=k_h[rows, p % 2, hd, :].bitcast(F32),
                                                      op0=ALU.add, op1=ALU.subtract)
                last.then_inc(bank_free[bank], 1)

            def vt_lo(st, p, ahead=0):
                bank, _ = st.use("vt", p)
                dve.wait_ge(v_hi, st.pair(p, ahead) + 1)
                V.tensor_tensor(v_l[:, p % 2].rearrange("p t c -> p (t c)"), ps[:, bank, :],
                                v_h[:, p % 2].rearrange("p t c -> p (t c)").bitcast(F32), ALU.subtract
                                ).then_inc(bank_free[bank], 1)

            def vs_lo(st, p, ahead=0):
                bank, _ = st.use("vs", p)
                dve.wait_ge(tail_hi, st.pair(p, ahead) + 1)
                V.tensor_tensor(v_tail_l[:, p % 2, :], ps[0:2 * TT, bank, 0:P], v_tail_h[:, p % 2, :].bitcast(F32),
                                ALU.subtract).then_inc(bank_free[bank], 1)

            def pv_lo(st, h):
                bank, _ = st.use("pv", h)
                rows = slice(HD * (h % 2), HD * (h % 2) + HD)
                dve.wait_ge(o_hi, 8 * st.b + h + 1)
                V.tensor_tensor(vt_l[rows, h // 2, :], ps[rows, bank, :], vt_h[rows, h // 2, :].bitcast(F32), ALU.subtract
                                ).then_inc(bank_free[bank], 1)

            def tp_lo(st, h, u):
                bank, _ = st.use("tp", h, u)
                o, blocks = TP_UNITS[u]
                n = P * len(blocks)
                dve.wait_ge(pt_hi, 3 * (8 * st.b + h) + u + 1)
                V.tensor_tensor(pt_l[:, o:o + n], ps[:, bank, 0:n], pt_h[:, o:o + n].bitcast(F32), ALU.subtract
                                ).then_inc(bank_free[bank], 1)

            def row_max(st, h):
                par, g = h % 4, 8 * st.b + h
                dve.wait_ge(scores_full, g + 1)
                hold(dve, "dve")
                for i in range(TT):
                    o = STRIP[i] + P * i
                    V.copy_predicated(scores[:, o:o + P], masked[:].bitcast(U32), neg_fill[:])
                V.drain()
                for i in range(TT):
                    o, n = STRIP[i], P * (i + 1)
                    V.tensor_reduce(neg_m[:, par, i:i + 1], scores[:, o:o + n], AX.X, ALU.max, negate=True)
                V.drain()
                V.tensor_scalar(neg_m[:, par, 0:3], neg_m[:, par, 0:3], -NEG, None, ALU.min).then_inc(negm_ready, 1)

            def denominators(st, h):
                par, g = h % 4, 8 * st.b + h
                dve.wait_ge(exp_done, g + 1)
                V.tensor_tensor(den[:, par, :], tail_e[:, par, :], n_tail[:], ALU.mult)
                V.drain()
                V.tensor_tensor(den[:, par, :], den[:, par, :], sums[:, par, :], ALU.add)
                V.drain()
                V.reciprocal(r_den[:, par, :], den[:, par, :])
                V.drain()
                for i in (3, 2, 0, 1):
                    strip = probs[:, h % 2, STRIP[i]:STRIP[i] + P * (i + 1)]
                    last = V.tensor_scalar(strip, strip, r_den[:, par, i:i + 1], None, ALU.mult)
                last.then_inc(probs_ready, 1)
                hi, lo = (tail_parts[:, h % 2, o:o + 9 * TT - 8:9] for o in (0, TT))
                V.tensor_tensor(tail_w[:], tail_e[:, par, :], r_den[:, par, :], ALU.mult)
                V.drain()
                V.tensor_copy(hi, tail_w[:])
                V.drain()
                V.tensor_tensor(lo, tail_w[:], hi.bitcast(F32), ALU.subtract).then_inc(tail_ready, 1)

            def column_stats(xt, j, width):
                for tt in range(TT):
                    V.bn_stats(stats[:, tt, j, :], xt[:, tt, width * j:width * j + width])

            def layer_stats(groups):
                V.drain()
                for tt in range(TT):
                    V.bn_aggr(mv[:, tt, :], stats[:, tt, 0:groups, :])
                V.drain()
                V.tensor_scalar(ve[:], mv[:, :, 1], EPS, None, ALU.add)
                V.drain()
                V.tensor_scalar(rs[:, 0, :].bitcast(I32), ve[:].bitcast(I32), -0.5, 1597463007.0, ALU.mult, ALU.add)
                V.drain()
                for it in range(3):
                    y, y2 = rs[:, it % 2, :], rs[:, (it + 1) % 2, :]
                    V.tensor_tensor(rt[:], y, y, ALU.mult)
                    V.drain()
                    V.scalar_tensor_tensor(out=rt[:], in0=rt[:], scalar=-0.5, in1=ve[:], op0=ALU.mult, op1=ALU.mult)
                    V.drain()
                    V.scalar_tensor_tensor(out=y2, in0=rt[:], scalar=1.5, in1=y, op0=ALU.add, op1=ALU.mult)
                    V.drain()

            def normalise(xt, tt, count):
                if not isinstance(count, int) or count >= 2:
                    dve.wait_ge(xn_used, count - 1)
                V.tensor_scalar(xn[:, tt % 2, :], xt[:, tt, :], mv[:, tt, 0:1], rs[:, 1, tt:tt + 1],
                                ALU.subtract, ALU.mult).then_inc(xn_ready, 1)

            def pick(dst, first, b):
                src = mod_t[:, first:first + 2 * DK, b:b + 1] if isinstance(b, int) else \
                    mod_t[:, first:first + 2 * DK, bass.ds(b, 1)]
                V.tensor_copy(dst[:].unsqueeze(2), src).then_inc(mod_picked, 1)

            def t_units(st, name, xt, x0, tiles=range(TT)):
                staged, b = name == "t2", st.b
                for tt in tiles:
                    if 2 <= tt + 1 < TT:
                        normalise(xt, tt + 1, x0 + tt + 1)
                    for kh in range(2):
                        u = 2 * tt + kh
                        made(dve, st, name, tt, kh)
                        if staged:
                            if u >= 4:
                                dve.wait_ge(h2_stored[u % 4], 64 * b + 32)
                            dst, src = vt_h[:, u % 4, :], h_tmp[:, kh, :]
                        else:
                            dst = ht_h[:, 4 * kh:4 * kh + 4, P * tt:P * tt + P]
                            src = h_tmp[:, kh, :].rearrange("p (k t) -> p k t", k=4)
                        V.tensor_copy(dst, src).then_inc(t_hi, 1)
                        if staged:
                            V.drain()
                            V.tensor_tensor(vt_l[:, u % 4, :], src, dst.bitcast(F32), ALU.subtract).then_inc(t_lo, 1)

            LO = {"q": q_lo, "k": k_lo}

            V.memset(behind[:].bitcast(F32), 0.0)
            V.memset(tail_parts[:].bitcast(F32), 0.0)
            V.memset(tail_e[:, :, 3:4], 0.0)
            V.memset(neg_fill[:], NEG)
            V.memset(neg_col[:], NEG)
            for i in range(TT):
                V.memset(n_tail[:, i:i + 1], float(P * (TT - 1 - i)))
            V.memset(pt_h[:].bitcast(F32), 0.0)
            V.memset(pt_l[:, ZERO:ZERO + P].bitcast(F32), 0.0)
            V.drain()
            for j in range(1, TT):
                for o in (0, TT):
                    V.memset(behind[:, j, o:o + j].bitcast(F32), 1.0)
            V.drain().then_inc(consts, 1)
            dve.wait_ge(c_silu, 1)
            for half in range(2):
                V.tensor_copy(c_st[half][:, :, 0:B], c_act[:, 4 * half:4 * half + 4, :])
            V.drain()
            for half in range(2):
                V.tensor_tensor(c_st[half][:, :, 32:32 + B], c_act[:, 4 * half:4 * half + 4, :],
                                c_st[half][:, :, 0:B].bitcast(F32), ALU.subtract).then_inc(c_ready, 1)
            pro = Prologue()

            def mod_row_evac(n):
                bank, _ = pro.use("mod", n)
                dve.wait_ge(mod_lo_ready, n + 1)
                V.tensor_tensor(mod_row[:, n % 2, :], ps[0:B, bank, :], mod_lo[:, n % 2, :], ALU.add
                                ).then_inc(bank_free[bank], 1)
                if n in GATES:
                    V.drain()
                    which, half = GATES[n]
                    row = mod_row[:, n % 2, :]
                    V.tensor_scalar(gate_sgn, row, 0.0, 2.0, ALU.is_ge, ALU.mult)
                    V.tensor_scalar(gate_abs, row, -1.0, None, ALU.mult)
                    V.drain()
                    V.tensor_tensor(gate_abs, gate_abs, row, ALU.max)
                    V.drain()
                    V.tensor_scalar(gate_abs, gate_abs, 0.25, None, ALU.max)
                    V.drain()
                    V.scalar_tensor_tensor(out=(gate_row if which == 0 else gate_row2)[:, half, :], in0=gate_sgn,
                                           scalar=-1.0, in1=gate_abs, op0=ALU.add, op1=ALU.mult).then_inc(gate_ready, 1)
                    V.drain()

            def mod_t_evac(n):
                bank = filled(dve, pro, "mt", n)
                V.tensor_scalar(mod_t[:, 4 * n:4 * n + 4, :], ps[:, bank, 0:4 * B].rearrange("p (t b) -> p t b", t=4),
                                1.0 if n // 2 in (1, 4) else 0.0, None, ALU.add).then_inc(bank_free[bank], 1)

            def pro_evac(kind, n):
                if kind == "mod":
                    mod_row_evac(n)
                    for m in MOD_T.get(n, ()):
                        mod_t_evac(m)
                    if n == 0:
                        dve.wait_ge(x0_loaded, 16)
                    if n < 2:
                        column_stats(x_next, n, 512)
                    if n == 2:
                        layer_stats(2)
                        normalise(x_next, 0, 0)
                        normalise(x_next, 1, 1)
                    if n == 3:
                        V.drain()
                        pick(mod_a, 0, 0)
                    if n == 9:
                        vt_lo(pro, 0)
                    if n == 10:
                        vs_lo(pro, 0)
                elif kind == "t1":
                    t_units(pro, "t1", x_next, 0, (n,))
                elif kind in LO and (kind, n) != ("k", 1):
                    LO[kind](pro, n)

            n = 0
            for idx, (kind, i) in enumerate(PRO):
                for _ in range({"mod": 4, "t1": 0}.get(kind, 1)):
                    weight_lo(n, n)
                    n += 1
                if idx:
                    pro_evac(*PRO[idx - 1])
            pro_evac(*PRO[-1])
            weight_lo(BASE_BODY, BASE_BODY)

            def gate_lo(n, r):
                dve.wait_ge(w_hi, n + 1)
                V.tensor_tensor(gu_l[:, r, :], raw[:, r, :], gu_h[:, r, :].bitcast(F32), ALU.subtract).then_inc(w_lo, 1)

            def attention(st):
                b = st.b

                def fill_lo(j):
                    kind, p = BODY_SLOTS[j]
                    if kind in LO:
                        LO[kind](st, p, 1 if j >= OWN else 0)

                for s in range(10):
                    early, late = body_evacs(s, st.next)
                    if s in T1_STEPS and st.next:
                        t_units(st, "t1", x_next, st.x_t1, T1_STEPS[s][:1])
                    if s < 8:
                        row_max(st, s)
                    if s == 0:
                        weight_lo(st.base + 1, BASE_BODY + 1)
                        k_lo(st, 1)
                    for j in (body_evacs(s - 1, st.next)[1] if s else ()):
                        fill_lo(j)
                    if s in (1, 2) and st.next:
                        if s == 1:
                            dve.wait_ge(x_loaded, 16 * b + 16)
                        column_stats(x_next, s - 1, 512)
                    if s == 3 and st.next:
                        layer_stats(2)
                    for j in early:
                        fill_lo(j)
                    if 2 <= s <= 9:
                        pv_lo(st, s - 2)
                    if 1 <= s <= 8:
                        tp_lo(st, s - 1, 0)
                        tp_lo(st, s - 1, 1)
                    if s < 8:
                        denominators(st, s)
                    if s in T1_STEPS and st.next:
                        t_units(st, "t1", x_next, st.x_t1, T1_STEPS[s][1:])
                    if 1 <= s <= 8:
                        tp_lo(st, s - 1, 2)
                    if s in VT_STEPS:
                        vt_lo(st, VT_STEPS[s])
                    if s in VS_STEPS:
                        vs_lo(st, VS_STEPS[s])
                    if s == 9:
                        for j in late:
                            fill_lo(j)
                    if s == 4 and st.next:
                        normalise(x_next, 0, st.x_t1)
                        normalise(x_next, 1, st.x_t1 + 1)
                        pick(mod_a, 0, b + 1)
                o0 = st.slots.index(("o", 0))
                dve.wait_ge(x_biased, 5 * b + 5)
                for j in range(4):
                    cols = slice(256 * j, 256 * j + 256)
                    ga = ga_row[:, cols].unsqueeze(1).to_broadcast([P, 2, 256])
                    for half in range(2):
                        bank = filled(dve, st, "o", j, half)
                        V.tensor_tensor(o_tmp[:, half], ps[:, bank, :].rearrange("p (t c) -> p t c", t=2), ga, ALU.mult
                                        ).then_inc(bank_free[bank], 1)
                        V.drain()
                        V.tensor_tensor(x_cur[:, 2 * half:2 * half + 2, cols], x_cur[:, 2 * half:2 * half + 2, cols],
                                        o_tmp[:, half], ALU.add)
                    if j == 0:
                        dve.wait_ge(w_lo, st.base + o0 + 2)
                    if st.next or j < 2:
                        weight_lo(st.base + o0 + j + 2, BASE_BODY + o0 + j + 2)
                    else:
                        gate_lo(BASE_MLP + j - 2, j - 2)
                    V.drain()
                    column_stats(x_cur, j, 256)
                    if j == 0 and st.next:
                        vt_lo(st, 0, 1)
                    if j == 1 and st.next:
                        vs_lo(st, 0, 1)
                V.drain().then_inc(x1_ready, 1)
                layer_stats(4)
                normalise(x_cur, 0, st.x_t2)
                normalise(x_cur, 1, st.x_t2 + 1)
                pick(mod_b, 6 * DK // 2, b)
                if st.next:
                    q_lo(st, 1, 1)
                    t_units(st, "t2", x_cur, st.x_t2)
                    weight_lo(st.base + 16, BASE_BODY + 16)
                else:
                    gate_lo(BASE_MLP + 2, 2)
                    gate_lo(BASE_MLP + 3, 3)
                    t_units(st, "t2", x_cur, st.x_t2, (0,))
                    gate_tile(0, 0, 0)
                    t_units(st, "t2", x_cur, st.x_t2, range(1, TT))

            def act_tile(i, s, blk):
                n0 = BASE_MLP + MLP_SLOTS * blk
                dve.wait_ge(silu_ready, FT * blk + 2 * i + s + 1)
                dve.wait_ge(w_used, n0 + 4 * i + 2 * s + 2)
                tile = act[:, 2 * i + s, :] if isinstance(i, int) else \
                    act[:, bass.ds(2 * i + s, 1), :].rearrange("p a t -> p (a t)")
                V.tensor_tensor(tile, ps[:, 2 * s + 1, :], silu[:, s, :], ALU.mult).then_inc(act_ready, 1)

            def gate_tile(i, s, blk, slots=2):
                n = BASE_MLP + MLP_SLOTS * blk + 4 * i + GATE_SLOTS + 2 * s
                gate_lo(n, 2 * s)
                act_tile(i, s, blk)
                if slots == 2:
                    gate_lo(n + 1, 2 * s + 1)

            with dve.Fori(0, B - 1) as b:
                attention(Stage(b, True))
            attention(Stage(B - 1, False))
            V.drain().then_inc(att_done, 1)

            def down_lo(i, r, blk):
                dve.wait_ge(w_hi, BASE_MLP + MLP_SLOTS * blk + GU_SLOTS + 2 * i + r + 1)
                V.tensor_tensor(w_l[:, r, :], raw_down[:, r, :], w_h[:, r, :].bitcast(F32), ALU.subtract).then_inc(w_lo, 1)

            def act_lo(i, r, blk):
                dve.wait_ge(a_hi, FT * blk + 2 * i + r + 1)
                tile = act[:, 2 * i + r, :] if isinstance(i, int) else \
                    act[:, bass.ds(2 * i + r, 1), :].rearrange("p a t -> p (a t)")
                V.tensor_tensor(a_l[:, r, :], tile, a_h[:, r, :].bitcast(F32), ALU.subtract).then_inc(a_lo, 1)

            def mlp(blk, more):
                n0 = BASE_MLP + MLP_SLOTS * blk

                gate_tile(0, 1, blk)
                dve.wait_ge(att_done, 4)
                with dve.Fori(1, FT // 2 - 2) as i:
                    for s in range(2):
                        gate_tile(i, s, blk)
                gate_tile(FT // 2 - 2, 0, blk)
                gate_tile(FT // 2 - 2, 1, blk, slots=1)
                for r in range(2):
                    act_lo(0, r, blk)
                for r in range(2):
                    down_lo(0, r, blk)
                act_tile(FT // 2 - 1, 0, blk)
                dve.wait_ge(silu_ready, FT * blk + FT)
                V.tensor_tensor(act[HALF:P, FT - 1, :], ps[HALF:P, 2, :], silu[HALF:P, 1, :], ALU.mult).then_inc(act_ready, 1)
                with dve.Fori(1, FT // 2 - 1) as i:
                    for r in range(2):
                        down_lo(i, r, blk)
                        act_lo(i, r, blk)
                down_lo(FT // 2 - 1, 0, blk)
                act_lo(FT // 2 - 1, 0, blk)
                down_lo(FT // 2 - 1, 1, blk)
                dve.wait_ge(a_hi, FT * blk + FT)
                V.tensor_tensor(a_h[0:HALF, 1, :], act[HALF:P, FT - 1, :], a_h[HALF:P, 1, :].bitcast(F32), ALU.subtract
                                ).then_inc(a_lo, 1)
                if more:
                    for r in range(3):
                        gate_lo(n0 + MLP_SLOTS + r, r)
                dve.wait_ge(mlp_loaded, 32 * blk + 32)
                for u in range(2 * TT):
                    tt, dh = DOWN_UNITS[u]
                    if u < 7:
                        dve.wait_ge(down_full, 7 * blk + u + 1)
                    else:
                        dve.wait_ge(w_used, n0 + MLP_SLOTS)
                    if u >= 4:
                        dve.wait_ge(y_added, 8 * blk + u - 3)
                    V.tensor_tensor(y_sb[:, u % 4, :], ps[:, 2 * tt + dh, :], gb_row[:, 512 * dh:512 * dh + 512], ALU.mult
                                    ).then_inc(y_ready, 1)
                if more:
                    gate_lo(n0 + MLP_SLOTS + 3, 3)
                    gate_tile(0, 0, blk + 1)

            with dve.Fori(0, B - 1) as blk:
                mlp(blk, True)
            mlp(B - 1, False)

        @block.tensor
        def _(pe):
            mm = nc.tensor.matmul

            def claim(st, *label):
                bank, n = st.use(*label)
                if not isinstance(n, int) or n > 0:
                    pe.wait_ge(bank_free[bank], n)
                return bank

            def three(out, a_h_, a_l_, b_h_, b_l_, first, last):
                mm(out, a_h_, b_h_, start=first, stop=False)
                mm(out, a_h_, b_l_, start=False, stop=False)
                return mm(out, a_l_, b_h_, start=False, stop=last)

            def slot(n, static_n):
                pe.wait_ge(w_lo, n + 1)
                return split_slot(static_n)

            def project(st, kind, p, n, static_n):
                bank = claim(st, kind, p)
                wh, wl = slot(n, static_n)
                for k in range(DK):
                    c = slice(P * k, P * k + P)
                    last = three(ps[:, bank, :], wh[:, c], wl[:, c], ht_h[:, k, :], ht_l[:, k, :], k == 0, k == DK - 1)
                last.then_inc(w_used, 1)

            def modulation(n, n0):
                bank = claim(pro, "mod", n)
                for q in range(4):
                    wh, wl = slot(n0 + q, n0 + q)
                    for kk in range(2):
                        k = 2 * q + kk
                        c = slice(512 * kk, 512 * kk + 512)
                        mm(ps[:, bank, :], c_st[k // 4][:, k % 4, :], wh[:, c], start=(k == 0), stop=False)
                        last = mm(ps[:, bank, :], c_st[k // 4][:, k % 4, :], wl[:, c], start=False, stop=(k == DK - 1))
                    last.then_inc(w_used, 1)

            def mod_transpose(n):
                bank = claim(pro, "mt", n)
                made(pe, pro, "mod", n)
                for t in range(4):
                    last = nc.tensor.transpose(ps[:, bank, B * t:B * t + B], mod_row[:, n % 2, P * t:P * t + P],
                                               ident[0:B, 0:B])
                last.then_inc(bank_full[bank], 1)

            def t_units(st, name, x0, tiles=range(TT)):
                for tt in tiles:
                    pe.wait_ge(xn_ready, x0 + tt + 1)
                    for kh in range(2):
                        bank = claim(st, name, tt, kh)
                        for k in range(4):
                            c = P * (4 * kh + k)
                            last = nc.tensor.transpose(ps[:, bank, P * k:P * k + P], xn[:, tt % 2, c:c + P], ident[:])
                        last.then_inc(xn_used if kh else bank_full[bank], 1)

            def v_transpose(st, p, ahead=0):
                bank = claim(st, "vt", p)
                made(pe, st, "v", p)
                for t in range(TT):
                    last = nc.tensor.transpose(ps[:, bank, P * t:P * t + P], v_col[:, P * t:P * t + P], ident[:])
                last.then_inc(bank_full[bank], 1)

            def v_tails(st, p, ahead=0):
                bank = claim(st, "vs", p)
                made(pe, st, "vt", p)
                for j in range(1, TT):
                    for part in (v_h, v_l):
                        last = mm(ps[0:2 * TT, bank, 0:P], behind[:, j, :], part[:, p % 2, j, :],
                                  start=(j == 1 and part is v_h), stop=(j == TT - 1 and part is v_l))
                last.then_inc(bank_full[bank], 1)

            def head_scores(st, h):
                p, hd = divmod(h, 2)
                g = 8 * st.b + h
                if h == 0:
                    for k in (6, 7):
                        pe.wait_ge(bank_free[k], st.before(k) - 1)
                if h == 2:
                    for k in (6, 7):
                        pe.wait_ge(bank_free[k], st.before(k))
                if hd == 0 and p >= 2:
                    made(pe, st, "q", p)
                if hd == 0 and p >= 2:
                    made(pe, st, "k", p)
                if not isinstance(g, int) or g > 0:
                    pe.wait_ge(scores_free, g + 1)
                for i in (3, 2, 0, 1):
                    o, n = STRIP[i], P * (i + 1)
                    mm(scores[:, o:o + n], q_st[:, p % 2, hd, P * i:P * i + P], k_h[:, p % 2, hd, 0:n], start=True, stop=False)
                    last = mm(scores[:, o:o + n], q_st[:, p % 2, hd, P * i:P * i + P], k_l[:, p % 2, hd, 0:n],
                              start=False, stop=True)
                last.then_inc(scores_full, 1)

            def prob_transpose(st, h, u):
                bank = claim(st, "tp", h, u)
                pe.wait_ge(probs_ready, 8 * st.b + h + 1)
                for n, (i, j) in enumerate(TP_UNITS[u][1]):
                    o = STRIP[i] + P * j
                    last = nc.tensor.transpose(ps[:, bank, P * n:P * n + P], probs[:, h % 2, o:o + P], ident[:])
                last.then_inc(bank_full[bank], 1)

            def head_values(st, h):
                p, hd = divmod(h, 2)
                bank = claim(st, "pv", h)
                made(pe, st, "tp", h, 1)
                if hd == 0 and p:
                    made(pe, st, "vt", p)
                    made(pe, st, "vs", p)
                for j, o, t in ((0, KEYS[0], 0), (1, KEYS[1], P), (3, ZERO, 2 * P), (2, KEYS[2], 2 * P)):
                    if j == 2:
                        made(pe, st, "tp", h, 2)
                    c = slice(o, o + S - t)
                    three(ps[:, bank, t:S], v_h[:, p % 2, j, :], v_l[:, p % 2, j, :], pt_h[:, c], pt_l[:, c], j == 0, False)
                made(pe, st, "tail", h)
                mm(ps[:, bank, :], v_tail_h[:, p % 2, :], tail_rows[:], start=False, stop=False)
                mm(ps[:, bank, :], v_tail_l[:, p % 2, :], tail_rows[:], start=False, stop=True).then_inc(bank_full[bank], 1)

            def tail_transpose(st, h):
                bank = claim(st, "tail", h)
                pe.wait_ge(tail_ready, 8 * st.b + h + 1)
                for i in range(TT):
                    last = nc.tensor.transpose(ps[0:2 * TT, bank, P * i:P * i + P],
                                               tail_parts[:, h % 2, 2 * TT * i:2 * TT * i + 2 * TT].bitcast(F32), ident[:])
                last.then_inc(bank_full[bank], 1)

            def out_projection(st, j, n, static_n):
                wh, wl = slot(n, static_n)
                if j == 0:
                    made(pe, st, "pv", HEADS - 1)
                for half in range(2):
                    bank = claim(st, "o", j, half)
                    for t in range(2):
                        tt = 2 * half + t
                        for p in range(PAIRS):
                            c = slice(256 * p, 256 * p + 256)
                            last = three(ps[:, bank, 256 * t:256 * t + 256], vt_h[:, p, P * tt:P * tt + P],
                                         vt_l[:, p, P * tt:P * tt + P], wh[:, c], wl[:, c], p == 0, p == PAIRS - 1)
                    last.then_inc(w_used if half else bank_full[bank], 1)

            pe.wait_ge(c_ready, 2)
            pe.wait_ge(consts, 3)
            pro = Prologue()
            n = 0
            for kind, i in PRO:
                if kind == "mod":
                    modulation(i, n)
                    n += 4
                    for m in MOD_T.get(i, ()):
                        mod_transpose(m)
                    if i == 9:
                        v_transpose(pro, 0)
                    if i == 10:
                        v_tails(pro, 0)
                elif kind == "t1":
                    t_units(pro, "t1", 0, (i,))
                else:
                    if (kind, i) == ("q", 0):
                        pe.wait_ge(t_lo, 8)
                    project(pro, kind, i, n, n)
                    n += 1

            def fill(st, j):
                kind, p = BODY_SLOTS[j]
                if j == OWN:
                    pe.wait_ge(t_lo, 2 * (st.x_t1 + 4))
                project(st, kind, p, st.base + j, BASE_BODY + j)

            def attention(st):
                for s in range(10):
                    early, late = body_fills(s, st.next)
                    if s in T1_STEPS and st.next:
                        t_units(st, "t1", st.x_t1, T1_STEPS[s][:1])
                    if s < 8:
                        head_scores(st, s)
                    for j in early:
                        fill(st, j)
                    if 2 <= s <= 9:
                        head_values(st, s - 2)
                    if 1 <= s <= 8:
                        prob_transpose(st, s - 1, 0)
                        prob_transpose(st, s - 1, 1)
                    for j in late:
                        fill(st, j)
                    if s in T1_STEPS and st.next:
                        t_units(st, "t1", st.x_t1, T1_STEPS[s][1:])
                    if 1 <= s <= 8:
                        prob_transpose(st, s - 1, 2)
                        tail_transpose(st, s - 1)
                    if s in VT_STEPS:
                        v_transpose(st, VT_STEPS[s])
                    if s in VS_STEPS:
                        v_tails(st, VS_STEPS[s])
                o0 = st.slots.index(("o", 0))
                for j in range(4):
                    out_projection(st, j, st.base + o0 + j, BASE_BODY + o0 + j)
                    if j == 0 and st.next:
                        v_transpose(st, 0, 1)
                    if j == 1 and st.next:
                        v_tails(st, 0, 1)
                if st.next:
                    project(st, "q", 1, st.base + 14, BASE_BODY + 14)
                    project(st, "k", 1, st.base + 15, BASE_BODY + 15)
                if st.next:
                    t_units(st, "t2", st.x_t2)
                else:
                    pe.wait_ge(ht_loaded, 32)
                    pe.wait_ge(scores_free, HEADS * B + 1)
                    gate_slot(BASE_MLP, 0)
                    gate_slot(BASE_MLP + 1, 1)
                    pe.wait_ge(bank_free[3], bank_total(3))
                    t_units(st, "t2", st.x_t2, (0,))
                    gate_slot(BASE_MLP + 2, 2)
                    t_units(st, "t2", st.x_t2, (1,))
                    gate_slot(BASE_MLP + 3, 3)
                    t_units(st, "t2", st.x_t2, (2, 3))

            def bank_total(bank):
                return PRO_N.get(bank, 0) + (B - 1) * BODY_N.get(bank, 0) + LAST_N.get(bank, 0)

            def gate_slot(n, r):
                pe.wait_ge(w_lo, n + 1)
                for k in range(DK):
                    c = slice(P * k, P * k + P)
                    last = three(ps[:, r, :], gu_h[:, r, c], gu_l[:, r, c], ht_h[:, k, :], ht_l[:, k, :],
                                 k == 0, k == DK - 1)
                last.then_inc(w_used, 1)

            with pe.Fori(0, B - 1) as b:
                attention(Stage(b, True))
            attention(Stage(B - 1, False))
            for bank in (4, 5, 6, 7):
                pe.wait_ge(bank_free[bank], bank_total(bank))
            pe.sem_inc(att_done, 1)

            def down_half_chunk(n, r, k_count):
                pe.wait_ge(w_lo, n + 1)
                pe.wait_ge(a_lo, k_count + 1)
                for tt, dh in DOWN_UNITS:
                    out, c, d = ps[:, 2 * tt + dh, :], slice(P * tt, P * tt + P), slice(512 * dh, 512 * dh + 512)
                    mm(out, a_h[:, r, c], w_h[:, r, d], start=False, stop=False)
                    last = mm(out, a_h[:, r, c], w_l[:, r, d], start=False, stop=True)
                    last.then_inc(w_used if (tt, dh) == DOWN_UNITS[-1] else down_full, 1)

            def down_chunk(n, r, k_count, first):
                pe.wait_ge(w_lo, n + 1)
                pe.wait_ge(a_lo, k_count + 1)
                wh, wl = w_h[:, r, :], w_l[:, r, :]
                for tt in DOWN_ORDER:
                    if first and tt < 2:
                        pe.wait_ge(act_ready, k_count + FT - 1 + tt)
                    c = slice(P * tt, P * tt + P)
                    banks = (ps[:, 2 * tt, :], ps[:, 2 * tt + 1, :])
                    d = (slice(0, 512), slice(512, 1024))
                    for dh in range(2):
                        mm(banks[dh], a_h[:, r, c], wh[:, d[dh]], start=first, stop=False)
                        mm(banks[dh], a_h[:, r, c], wl[:, d[dh]], start=False, stop=False)
                    for dh in range(2):
                        last = mm(banks[dh], a_l[:, r, c], wh[:, d[dh]], start=False, stop=False)
                last.then_inc(w_used, 1)

            def mlp(blk, more):
                n0 = BASE_MLP + MLP_SLOTS * blk
                with pe.Fori(1, FT // 2 - 1) as i:
                    for s in range(2):
                        tile = FT * blk + 2 * i + s
                        pe.wait_ge(silu_ready, tile - 1)
                        gate_slot(n0 + 4 * i + 2 * s, 2 * s)
                        pe.wait_ge(act_ready, tile - 1)
                        gate_slot(n0 + 4 * i + 2 * s + 1, 2 * s + 1)
                nd = n0 + GU_SLOTS
                pe.wait_ge(silu_ready, FT * blk + FT - 3)
                gate_slot(n0 + 2 * FT - 4, 0)
                pe.wait_ge(act_ready, FT * blk + FT - 3)
                gate_slot(n0 + 2 * FT - 3, 1)
                pe.wait_ge(silu_ready, FT * blk + FT - 2)
                gate_slot(n0 + 2 * FT - 2, 2)
                down_chunk(nd, 0, FT * blk, True)
                down_chunk(nd + 1, 1, FT * blk + 1, False)
                with pe.Fori(1, FT // 2 - 1) as i:
                    for r in range(2):
                        down_chunk(nd + 2 * i + r, r, FT * blk + 2 * i + r, False)
                down_chunk(nd + FT - 2, 0, FT * blk + FT - 2, False)
                down_half_chunk(nd + FT - 1, 1, FT * blk + FT - 1)
                if more:
                    pe.wait_ge(ht_loaded, 32 * blk + 64)
                    for r in range(GATE_SLOTS):
                        pe.wait_ge(y_ready, 8 * blk + DOWN_UNITS.index(divmod(r, 2)) + 1)
                        gate_slot(n0 + MLP_SLOTS + r, r)

            with pe.Fori(0, B - 1) as blk:
                mlp(blk, True)
            mlp(B - 1, False)


def kernel(**inputs):
    import numpy as np
    import concourse.bacc as bacc
    from concourse.bass_utils import run_bass_kernel_spmd as run

    g = {k: np.asarray(v) for k, v in inputs.items()}
    full = F // P * P
    gate, up = g["L0_ffn_W_gate"], g["L0_ffn_W_up"]
    tiles = np.stack([w[:full].reshape(FT - 1, P, D) for w in (gate, up)], axis=1).reshape(2 * FT - 2, P, D)
    half = np.concatenate([gate[full:], up[full:]])[None]
    gate_up = np.concatenate([tiles, half]).reshape(GU_SLOTS, P, DK, P).transpose(0, 3, 2, 1).reshape(GU_SLOTS, P, W)
    down_t = g["L0_ffn_W_down"].T
    down = np.concatenate([down_t, down_t[full:]]).reshape(FT, P, D)
    arrays = {
        "x_in": g["L0_attn_x"],
        "c_in": g["L0_c"].T.reshape(DK, P, B).transpose(1, 0, 2),
        "w_mod": g["L0_wmod"].reshape(4, 2, P, MOD_CHUNKS, 512).transpose(3, 0, 2, 1, 4).reshape(4 * MOD_CHUNKS, P, W),
        "w_pairs": g["L0_attn_w_qkv"].reshape(3, PAIRS, P, DK, P).transpose(1, 0, 4, 3, 2).reshape(3 * PAIRS, P, W),
        "b_pairs": g["L0_attn_b_qkv"].reshape(3, PAIRS, P).transpose(2, 1, 0).reshape(P, 3 * PAIRS),
        "w_o": g["L0_attn_w_o"].reshape(4, 256, PAIRS, P).transpose(0, 3, 2, 1).reshape(4, P, W),
        "b_o": g["L0_attn_b_o"],
        "w_mlp": np.concatenate([gate_up, down], axis=0),
    }
    arrays = {k: np.ascontiguousarray(v) for k, v in arrays.items()}
    nc = bacc.Bacc("TRN2", target_bir_lowering=False, num_devices=1)
    args = [nc.dram_tensor(k, a.shape, F32, kind="ExternalInput").ap() for k, a in arrays.items()]
    y = nc.dram_tensor("y_out", (B, S, D), F32, kind="ExternalOutput").ap()
    mlp_block(nc, *args, y)
    r = run(nc, [arrays], core_ids=[0])
    return r.results[0]["y_out"]
```
